# Optimizing a Trainium2 kernel written in Bass

```python
import numpy as np
import jax
import jax.numpy as jnp

def _softmax(x, axis=-1):
    return jax.nn.softmax(x, axis=axis)

def _gelu(x):
    return jax.nn.gelu(x, approximate=True)

def _silu(x):
    return jax.nn.silu(x)

def _sigmoid(x):
    return jax.nn.sigmoid(x)

def _layernorm(x, axis=-1, eps=1e-05):
    m = jnp.mean(x, axis=axis, keepdims=True)
    v = jnp.var(x, axis=axis, keepdims=True)
    return (x - m) / jnp.sqrt(v + eps)

def _scatter_add(tgt, idx, src, axis=0):
    return tgt.at[idx].add(src)

def _segment_sum(src, seg, n):
    return jax.ops.segment_sum(src, seg, n)
kernel_name = 'mk_metaformer_d4_conv_nhwc256_r4_f9f41d'

def setup_inputs(seed: int=0):
    np.random.seed(seed)
    _w = jnp.asarray

    def _rec_inputs():
        import jax
        import jax.numpy as jnp
        _gk = jax.random.key(seed)
        x = -0.0005207 + 1.001 * jax.random.normal(jax.random.fold_in(_gk, 1), (2, 16, 16, 64), jnp.float32)
        return x
    x = _rec_inputs()

    def _L0_conv_setup():
        import jax, jax.numpy as jnp
        import numpy as np
        B, H, W = (2, 16, 16)
        D_MODEL, D_STATE, DT_RANK = (64, 16, 16)
        D_INNER = 2 * D_MODEL

        def _selective_scan(u, delta, A, Bm, Cm, Dv):

            def step(h, inp):
                dt, bt, ct, ut = inp
                h = jnp.exp(dt[..., None] * A) * h + (dt * ut)[..., None] * bt[:, None, :]
                return (h, jnp.einsum('bdn,bn->bd', h, ct))
            h0 = jnp.zeros(u.shape[:2] + (A.shape[1],), u.dtype)
            xs = (jnp.moveaxis(delta, 2, 0), jnp.moveaxis(Bm, 2, 0), jnp.moveaxis(Cm, 2, 0), jnp.moveaxis(u, 2, 0))
            _, ys = jax.lax.scan(step, h0, xs)
            return jnp.moveaxis(ys, 0, 2) + Dv[None, :, None] * u

        def _forward(x, in_proj_w, conv_w, conv_b, xproj_w, dt_w, dt_b, A_logs, Ds, out_proj_w):
            b, h, w, _ = x.shape
            n, r = (D_STATE, DT_RANK)
            l = h * w
            xz = x @ in_proj_w
            xi, z = jnp.split(xz, 2, axis=-1)
            xc = jnp.transpose(xi, (0, 3, 1, 2))
            xc = jax.lax.conv_general_dilated(xc, conv_w, (1, 1), ((1, 1), (1, 1)), dimension_numbers=('NCHW', 'OIHW', 'NCHW'))
            xc = jax.nn.silu(xc + conv_b[None, :, None, None])
            x_dbl = jnp.einsum('bchw,oc->bohw', xc, xproj_w)
            half = x_dbl.shape[1] // 2
            hw_flat = x_dbl[:, :half].reshape(b, half, l)
            wh_flat = jnp.transpose(x_dbl[:, half:], (0, 1, 3, 2)).reshape(b, half, l)

            def split_params(flat):
                dts, bc = (flat[:, :2 * r], flat[:, 2 * r:])
                return ((dts[:, :r], dts[:, r:]), (bc[:, :n], bc[:, n:2 * n]), (bc[:, 2 * n:3 * n], bc[:, 3 * n:]))
            (hd1, hd2), (hb1, hb2), (hc1, hc2) = split_params(hw_flat)
            (wd1, wd2), (wb1, wb2), (wc1, wc2) = split_params(wh_flat)
            hw_x = xc.reshape(b, -1, l)
            wh_x = jnp.transpose(xc, (0, 1, 3, 2)).reshape(b, -1, l)
            xs = jnp.stack([hw_x, hw_x[:, ::-1], wh_x, wh_x[:, ::-1]])
            dt_stack = jnp.stack([hd1, hd2, wd1, wd2])
            Bst = jnp.stack([hb1, hb2, wb1, wb2])
            Cst = jnp.stack([hc1, hc2, wc1, wc2])
            dts = jnp.einsum('kbrl,kdr->kbdl', dt_stack, dt_w)
            delta = jax.nn.softplus(dts + dt_b[:, None, :, None])
            A = -jnp.exp(A_logs)
            ys = jax.vmap(_selective_scan)(xs, delta, A, Bst, Cst, Ds)
            y = ys.sum(0)
            y = jnp.transpose(y, (0, 2, 1)).reshape(b, h, w, -1)
            y = y * jax.nn.silu(z)
            return y @ out_proj_w
        key = jax.random.key(seed)
        ks = jax.random.split(key, 8)
        f = lambda k, shape, s=0.02: jax.random.normal(k, shape, dtype=jnp.float32) * s
        x = jax.random.normal(ks[0], (B, H, W, D_MODEL), dtype=jnp.float32)
        in_proj_w = f(ks[1], (D_MODEL, 2 * D_INNER))
        conv_w = f(ks[2], (D_INNER, D_INNER, 3, 3))
        conv_b = jnp.zeros((D_INNER,), jnp.float32)
        xproj_w = f(ks[3], (4 * (DT_RANK + 2 * D_STATE), D_INNER))
        std = DT_RANK ** (-0.5)
        dt_w = jax.random.uniform(ks[4], (4, D_INNER, DT_RANK), jnp.float32, -std, std)
        dt = jnp.exp(jax.random.uniform(ks[5], (4, D_INNER), jnp.float32) * (np.log(0.1) - np.log(0.001)) + np.log(0.001)).clip(0.0001)
        dt_b = dt + jnp.log(-jnp.expm1(-dt))
        A_logs = jnp.log(jnp.tile(jnp.arange(1, D_STATE + 1, dtype=jnp.float32)[None, None, :], (4, D_INNER, 1)))
        Ds = jnp.ones((4, D_INNER), jnp.float32)
        out_proj_w = f(ks[6], (D_INNER, D_MODEL))
        return dict(x=x, in_proj_w=in_proj_w, conv_w=conv_w, conv_b=conv_b, xproj_w=xproj_w, dt_w=dt_w, dt_b=dt_b, A_logs=A_logs, Ds=Ds, out_proj_w=out_proj_w)
    _L0_conv_all = _L0_conv_setup()
    _L0_conv_in = {k: v for k, v in _L0_conv_all.items() if k in ('in_proj_w', 'conv_w', 'conv_b', 'xproj_w', 'dt_w', 'dt_b', 'A_logs', 'Ds', 'out_proj_w')}
    del _L0_conv_all

    def _L0_ffn_setup():
        import jax, jax.numpy as jnp
        import numpy as np
        TOP_K = 2
        LN_EPS = 1e-05
        key = jax.random.key(seed)
        ks = jax.random.split(key, 8)
        B, S, D, E, H = (16, 256, 64, 8, 256)
        x = jax.random.normal(ks[0], (B, S, D), dtype=jnp.float32)
        Wr = jax.random.normal(ks[1], (D, E), dtype=jnp.float32) * 0.1
        br = jnp.zeros((E,), dtype=jnp.float32)
        ln_g = jnp.ones((E, D), dtype=jnp.float32)
        ln_b = jnp.zeros((E, D), dtype=jnp.float32)
        W1 = jax.random.normal(ks[2], (E, D, H), dtype=jnp.float32) * (1.0 / np.sqrt(D))
        b1 = jnp.zeros((E, H), dtype=jnp.float32)
        W2 = jax.random.normal(ks[3], (E, H, D), dtype=jnp.float32) * (1.0 / np.sqrt(H))
        b2 = jnp.zeros((E, D), dtype=jnp.float32)
        return {'x': x, 'Wr': Wr, 'br': br, 'ln_g': ln_g, 'ln_b': ln_b, 'W1': W1, 'b1': b1, 'W2': W2, 'b2': b2}
    _L0_ffn_all = _L0_ffn_setup()
    _L0_ffn_in = {k: v for k, v in _L0_ffn_all.items() if k in ('Wr', 'br', 'ln_g', 'ln_b', 'W1', 'b1', 'W2', 'b2')}
    del _L0_ffn_all

    def _L1_conv_setup():
        import jax, jax.numpy as jnp
        import numpy as np
        B, H, W, C = (1, 16, 16, 64)
        NH = 8
        K = 7

        def _neighbor_idx(n, k):
            start = jnp.clip(jnp.arange(n) - k // 2, 0, n - k)
            return start[:, None] + jnp.arange(k)[None, :]
        key = jax.random.key(seed)
        ks = jax.random.split(key, 6)
        x = jax.random.normal(ks[0], (B, H, W, C), dtype=jnp.float32)
        qkv_w = jax.random.normal(ks[1], (3 * C, C), dtype=jnp.float32) * 0.02
        qkv_b = jnp.zeros((3 * C,), dtype=jnp.float32)
        proj_w = jax.random.normal(ks[2], (C, C), dtype=jnp.float32) * 0.02
        proj_b = jnp.zeros((C,), dtype=jnp.float32)
        rpb = jax.random.normal(ks[3], (NH, 2 * K - 1, 2 * K - 1), dtype=jnp.float32) * 0.02
        return {'x': x, 'qkv_w': qkv_w, 'qkv_b': qkv_b, 'proj_w': proj_w, 'proj_b': proj_b, 'rpb': rpb}
    _L1_conv_all = _L1_conv_setup()
    _L1_conv_in = {k: v for k, v in _L1_conv_all.items() if k in ('qkv_w', 'qkv_b', 'proj_w', 'proj_b', 'rpb')}
    del _L1_conv_all

    def _L1_ffn_setup():
        import jax, jax.numpy as jnp
        import numpy as np
        TOP_K = 2
        key = jax.random.key(seed)
        ks = jax.random.split(key, 4)
        B, L, D, H, E = (8, 1024, 64, 256, 8)
        s = 0.02
        return {'x': jax.random.normal(ks[0], (B, L, D), jnp.float32), 'Wg': jax.random.normal(ks[1], (D, E), jnp.float32) * s, 'bg': jnp.zeros((E,), jnp.float32), 'W1': jax.random.normal(ks[2], (E, D, H), jnp.float32) * s, 'b1': jnp.zeros((E, H), jnp.float32), 'W2': jax.random.normal(ks[3], (E, H, D), jnp.float32) * s, 'b2': jnp.zeros((E, D), jnp.float32)}
    _L1_ffn_all = _L1_ffn_setup()
    _L1_ffn_in = {k: v for k, v in _L1_ffn_all.items() if k in ('Wg', 'bg', 'W1', 'b1', 'W2', 'b2')}
    del _L1_ffn_all

    def _L2_conv_setup():
        import jax, jax.numpy as jnp
        import numpy as np
        K = 3
        FILTERS = 64
        GC = 16
        G = FILTERS // GC
        key = jax.random.key(seed)
        ks = jax.random.split(key, 5)
        B, H, W, C = (8, 16, 16, FILTERS)
        red = FILTERS // 4
        x = jax.random.normal(ks[0], (B, H, W, C), dtype=jnp.float32)
        W1 = jax.random.normal(ks[1], (C, red), dtype=jnp.float32) * 0.05
        b1 = jnp.zeros((red,), dtype=jnp.float32)
        W2 = jax.random.normal(ks[2], (red, K * K * G), dtype=jnp.float32) * 0.05
        b2 = jnp.zeros((K * K * G,), dtype=jnp.float32)
        return {'x': x, 'W1': W1, 'b1': b1, 'W2': W2, 'b2': b2}
    _L2_conv_all = _L2_conv_setup()
    _L2_conv_in = {k: v for k, v in _L2_conv_all.items() if k in ('W1', 'b1', 'W2', 'b2')}
    del _L2_conv_all

    def _L2_ffn_setup():
        import math
        import jax, jax.numpy as jnp
        import numpy as np
        CAPACITY_FACTOR = 1.25
        key = jax.random.key(seed)
        ks = jax.random.split(key, 5)
        B, L, D, F, E = (8, 2048, 64, 256, 8)
        h = jax.random.normal(ks[0], (B, L, D), dtype=jnp.float32)
        gate_w = jax.random.normal(ks[1], (D, E), dtype=jnp.float32) * 0.02
        gate_b = jnp.zeros((E,), dtype=jnp.float32)
        w1 = jax.random.normal(ks[2], (E, D, F), dtype=jnp.float32) * (1.0 / math.sqrt(D))
        b1 = jnp.zeros((E, F), dtype=jnp.float32)
        w2 = jax.random.normal(ks[3], (E, F, D), dtype=jnp.float32) * (1.0 / math.sqrt(F))
        b2 = jnp.zeros((E, D), dtype=jnp.float32)
        return {'h': h, 'gate_w': gate_w, 'gate_b': gate_b, 'w1': w1, 'b1': b1, 'w2': w2, 'b2': b2}
    _L2_ffn_all = _L2_ffn_setup()
    _L2_ffn_in = {k: v for k, v in _L2_ffn_all.items() if k in ('gate_w', 'gate_b', 'w1', 'b1', 'w2', 'b2')}
    del _L2_ffn_all

    def _L3_conv_setup():
        import jax, jax.numpy as jnp
        import numpy as np
        key = jax.random.key(seed)
        k1, k2 = jax.random.split(key)
        x = jax.random.normal(k1, (8, 56, 56, 64), dtype=jnp.float32)
        W = jax.random.normal(k2, (64, 64), dtype=jnp.float32) * (1.0 / np.sqrt(256.0))
        return {'x': x, 'W': W}
    _L3_conv_all = _L3_conv_setup()
    _L3_conv_in = {k: v for k, v in _L3_conv_all.items() if k in ('W',)}
    del _L3_conv_all

    def _L3_ffn_setup():
        import jax, jax.numpy as jnp
        import numpy as np
        D_MODEL = 64
        N_EXPERTS = 16
        HIDDEN = 128
        SCALE = 0.02
        key = jax.random.key(seed)
        ks = jax.random.split(key, 5)
        x = jax.random.normal(ks[0], (4, 2048, D_MODEL), dtype=jnp.float32)
        gate_w = jax.random.normal(ks[1], (D_MODEL, N_EXPERTS), dtype=jnp.float32) * SCALE
        gate_b = jnp.zeros((N_EXPERTS,), dtype=jnp.float32)
        w1 = jax.random.normal(ks[2], (N_EXPERTS, D_MODEL, HIDDEN), dtype=jnp.float32) * SCALE
        w2 = jax.random.normal(ks[3], (N_EXPERTS, D_MODEL, HIDDEN), dtype=jnp.float32) * SCALE
        w3 = jax.random.normal(ks[4], (N_EXPERTS, HIDDEN, D_MODEL), dtype=jnp.float32) * SCALE
        return {'x': x, 'gate_w': gate_w, 'gate_b': gate_b, 'w1': w1, 'w2': w2, 'w3': w3}
    _L3_ffn_all = _L3_ffn_setup()
    _L3_ffn_in = {k: v for k, v in _L3_ffn_all.items() if k in ('gate_w', 'gate_b', 'w1', 'w2', 'w3')}
    del _L3_ffn_all
    return {'x': x, 'L0_conv_in_proj_w': _L0_conv_in['in_proj_w'], 'L0_conv_conv_w': _L0_conv_in['conv_w'], 'L0_conv_conv_b': _L0_conv_in['conv_b'], 'L0_conv_xproj_w': _L0_conv_in['xproj_w'], 'L0_conv_dt_w': _L0_conv_in['dt_w'], 'L0_conv_dt_b': _L0_conv_in['dt_b'], 'L0_conv_A_logs': _L0_conv_in['A_logs'], 'L0_conv_Ds': _L0_conv_in['Ds'], 'L0_conv_out_proj_w': _L0_conv_in['out_proj_w'], 'L0_ffn_Wr': _L0_ffn_in['Wr'], 'L0_ffn_br': _L0_ffn_in['br'], 'L0_ffn_ln_g': _L0_ffn_in['ln_g'], 'L0_ffn_ln_b': _L0_ffn_in['ln_b'], 'L0_ffn_W1': _L0_ffn_in['W1'], 'L0_ffn_b1': _L0_ffn_in['b1'], 'L0_ffn_W2': _L0_ffn_in['W2'], 'L0_ffn_b2': _L0_ffn_in['b2'], 'L1_conv_qkv_w': _L1_conv_in['qkv_w'], 'L1_conv_qkv_b': _L1_conv_in['qkv_b'], 'L1_conv_proj_w': _L1_conv_in['proj_w'], 'L1_conv_proj_b': _L1_conv_in['proj_b'], 'L1_conv_rpb': _L1_conv_in['rpb'], 'L1_ffn_Wg': _L1_ffn_in['Wg'], 'L1_ffn_bg': _L1_ffn_in['bg'], 'L1_ffn_W1': _L1_ffn_in['W1'], 'L1_ffn_b1': _L1_ffn_in['b1'], 'L1_ffn_W2': _L1_ffn_in['W2'], 'L1_ffn_b2': _L1_ffn_in['b2'], 'L2_conv_W1': _L2_conv_in['W1'], 'L2_conv_b1': _L2_conv_in['b1'], 'L2_conv_W2': _L2_conv_in['W2'], 'L2_conv_b2': _L2_conv_in['b2'], 'L2_ffn_gate_w': _L2_ffn_in['gate_w'], 'L2_ffn_gate_b': _L2_ffn_in['gate_b'], 'L2_ffn_w1': _L2_ffn_in['w1'], 'L2_ffn_b1': _L2_ffn_in['b1'], 'L2_ffn_w2': _L2_ffn_in['w2'], 'L2_ffn_b2': _L2_ffn_in['b2'], 'L3_conv_W': _L3_conv_in['W'], 'L3_ffn_gate_w': _L3_ffn_in['gate_w'], 'L3_ffn_gate_b': _L3_ffn_in['gate_b'], 'L3_ffn_w1': _L3_ffn_in['w1'], 'L3_ffn_w2': _L3_ffn_in['w2'], 'L3_ffn_w3': _L3_ffn_in['w3']}

def reference(x, L0_conv_in_proj_w, L0_conv_conv_w, L0_conv_conv_b, L0_conv_xproj_w, L0_conv_dt_w, L0_conv_dt_b, L0_conv_A_logs, L0_conv_Ds, L0_conv_out_proj_w, L0_ffn_Wr, L0_ffn_br, L0_ffn_ln_g, L0_ffn_ln_b, L0_ffn_W1, L0_ffn_b1, L0_ffn_W2, L0_ffn_b2, L1_conv_qkv_w, L1_conv_qkv_b, L1_conv_proj_w, L1_conv_proj_b, L1_conv_rpb, L1_ffn_Wg, L1_ffn_bg, L1_ffn_W1, L1_ffn_b1, L1_ffn_W2, L1_ffn_b2, L2_conv_W1, L2_conv_b1, L2_conv_W2, L2_conv_b2, L2_ffn_gate_w, L2_ffn_gate_b, L2_ffn_w1, L2_ffn_b1, L2_ffn_w2, L2_ffn_b2, L3_conv_W, L3_ffn_gate_w, L3_ffn_gate_b, L3_ffn_w1, L3_ffn_w2, L3_ffn_w3):
    import jax
    import jax.numpy as jnp

    def _L0_conv_ref(x, in_proj_w, conv_w, conv_b, xproj_w, dt_w, dt_b, A_logs, Ds, out_proj_w):
        import jax, jax.numpy as jnp
        import numpy as np
        B, H, W = (2, 16, 16)
        D_MODEL, D_STATE, DT_RANK = (64, 16, 16)
        D_INNER = 2 * D_MODEL

        def _selective_scan(u, delta, A, Bm, Cm, Dv):

            def step(h, inp):
                dt, bt, ct, ut = inp
                h = jnp.exp(dt[..., None] * A) * h + (dt * ut)[..., None] * bt[:, None, :]
                return (h, jnp.einsum('bdn,bn->bd', h, ct))
            h0 = jnp.zeros(u.shape[:2] + (A.shape[1],), u.dtype)
            xs = (jnp.moveaxis(delta, 2, 0), jnp.moveaxis(Bm, 2, 0), jnp.moveaxis(Cm, 2, 0), jnp.moveaxis(u, 2, 0))
            _, ys = jax.lax.scan(step, h0, xs)
            return jnp.moveaxis(ys, 0, 2) + Dv[None, :, None] * u

        def _forward(x, in_proj_w, conv_w, conv_b, xproj_w, dt_w, dt_b, A_logs, Ds, out_proj_w):
            b, h, w, _ = x.shape
            n, r = (D_STATE, DT_RANK)
            l = h * w
            xz = x @ in_proj_w
            xi, z = jnp.split(xz, 2, axis=-1)
            xc = jnp.transpose(xi, (0, 3, 1, 2))
            xc = jax.lax.conv_general_dilated(xc, conv_w, (1, 1), ((1, 1), (1, 1)), dimension_numbers=('NCHW', 'OIHW', 'NCHW'))
            xc = jax.nn.silu(xc + conv_b[None, :, None, None])
            x_dbl = jnp.einsum('bchw,oc->bohw', xc, xproj_w)
            half = x_dbl.shape[1] // 2
            hw_flat = x_dbl[:, :half].reshape(b, half, l)
            wh_flat = jnp.transpose(x_dbl[:, half:], (0, 1, 3, 2)).reshape(b, half, l)

            def split_params(flat):
                dts, bc = (flat[:, :2 * r], flat[:, 2 * r:])
                return ((dts[:, :r], dts[:, r:]), (bc[:, :n], bc[:, n:2 * n]), (bc[:, 2 * n:3 * n], bc[:, 3 * n:]))
            (hd1, hd2), (hb1, hb2), (hc1, hc2) = split_params(hw_flat)
            (wd1, wd2), (wb1, wb2), (wc1, wc2) = split_params(wh_flat)
            hw_x = xc.reshape(b, -1, l)
            wh_x = jnp.transpose(xc, (0, 1, 3, 2)).reshape(b, -1, l)
            xs = jnp.stack([hw_x, hw_x[:, ::-1], wh_x, wh_x[:, ::-1]])
            dt_stack = jnp.stack([hd1, hd2, wd1, wd2])
            Bst = jnp.stack([hb1, hb2, wb1, wb2])
            Cst = jnp.stack([hc1, hc2, wc1, wc2])
            dts = jnp.einsum('kbrl,kdr->kbdl', dt_stack, dt_w)
            delta = jax.nn.softplus(dts + dt_b[:, None, :, None])
            A = -jnp.exp(A_logs)
            ys = jax.vmap(_selective_scan)(xs, delta, A, Bst, Cst, Ds)
            y = ys.sum(0)
            y = jnp.transpose(y, (0, 2, 1)).reshape(b, h, w, -1)
            y = y * jax.nn.silu(z)
            return y @ out_proj_w
        return _forward(x, in_proj_w, conv_w, conv_b, xproj_w, dt_w, dt_b, A_logs, Ds, out_proj_w)

    def _L0_ffn_ref(x, Wr, br, ln_g, ln_b, W1, b1, W2, b2):
        import jax, jax.numpy as jnp
        import numpy as np
        TOP_K = 2
        LN_EPS = 1e-05
        B, S, D = x.shape
        N = B * S
        xt = x.reshape(N, D)
        logits = xt @ Wr + br
        probs = jax.nn.softmax(logits, axis=-1)
        top_p, top_idx = jax.lax.top_k(probs, TOP_K)
        weights = top_p / top_p.sum(axis=-1, keepdims=True)
        mu = xt.mean(axis=-1, keepdims=True)
        var = ((xt - mu) ** 2).mean(axis=-1, keepdims=True)
        xn = (xt - mu) * jax.lax.rsqrt(var + LN_EPS)
        xe = xn[None, :, :] * ln_g[:, None, :] + ln_b[:, None, :]
        h = jax.nn.gelu(jnp.einsum('end,edh->enh', xe, W1) + b1[:, None, :], approximate=False)
        y = jnp.einsum('enh,ehd->end', h, W2) + b2[:, None, :]
        y_tok = jnp.transpose(y, (1, 0, 2))
        sel = jnp.take_along_axis(y_tok, top_idx[:, :, None], axis=1)
        out = (weights[:, :, None] * sel).sum(axis=1)
        return out.reshape(B, S, D)

    def _L1_conv_ref(x, qkv_w, qkv_b, proj_w, proj_b, rpb):
        import jax, jax.numpy as jnp
        import numpy as np
        B, H, W, C = (1, 16, 16, 64)
        NH = 8
        K = 7

        def _neighbor_idx(n, k):
            start = jnp.clip(jnp.arange(n) - k // 2, 0, n - k)
            return start[:, None] + jnp.arange(k)[None, :]
        b, h, w, c = x.shape
        nh = rpb.shape[0]
        k = (rpb.shape[1] + 1) // 2
        hd = c // nh
        scale = hd ** (-0.5)
        qkv = x @ qkv_w.T + qkv_b
        qkv = qkv.reshape(b, h, w, 3, nh, hd)
        qkv = jnp.transpose(qkv, (3, 0, 4, 1, 2, 5))
        q, kk, v = (qkv[0], qkv[1], qkv[2])
        ni = _neighbor_idx(h, k)
        nj = _neighbor_idx(w, k)
        k_nb = kk[:, :, ni][:, :, :, :, nj]
        v_nb = v[:, :, ni][:, :, :, :, nj]
        attn = jnp.einsum('bnijd,bniajcd->bnijac', q * scale, k_nb)
        bi = ni - jnp.arange(h)[:, None] + (k - 1)
        bj = nj - jnp.arange(w)[:, None] + (k - 1)
        bias = rpb[:, bi][:, :, :, bj]
        attn = attn + jnp.transpose(bias, (0, 1, 3, 2, 4))[None]
        attn = jax.nn.softmax(attn.reshape(b, nh, h, w, k * k), axis=-1)
        attn = attn.reshape(b, nh, h, w, k, k)
        out = jnp.einsum('bnijac,bniajcd->bnijd', attn, v_nb)
        out = jnp.transpose(out, (0, 2, 3, 1, 4)).reshape(b, h, w, c)
        out = out @ proj_w.T + proj_b
        return out

    def _L1_ffn_ref(x, Wg, bg, W1, b1, W2, b2):
        import jax, jax.numpy as jnp
        import numpy as np
        TOP_K = 2
        B, L, D = x.shape
        E = W1.shape[0]
        xf = x.reshape(-1, D)
        gate_logits = xf @ Wg + bg
        top_w, top_i = jax.lax.top_k(gate_logits, TOP_K)
        top_w = jax.nn.softmax(top_w, axis=-1)
        w_dense = jnp.sum(jax.nn.one_hot(top_i, E, dtype=xf.dtype) * top_w[..., None], axis=1)
        out = jnp.zeros_like(xf)
        for e in range(E):
            h = jax.nn.gelu(xf @ W1[e] + b1[e], approximate=False)
            out = out + w_dense[:, e:e + 1] * (h @ W2[e] + b2[e])
        return out.reshape(B, L, D)

    def _L2_conv_ref(x, W1, b1, W2, b2):
        import jax, jax.numpy as jnp
        import numpy as np
        K = 3
        FILTERS = 64
        GC = 16
        G = FILTERS // GC
        b, h, w, c = x.shape
        kk = K * K
        wgt = jnp.einsum('bhwc,cd->bhwd', x, W1) + b1
        wgt = jnp.einsum('bhwd,de->bhwe', wgt, W2) + b2
        wgt = wgt.transpose(0, 3, 1, 2).reshape(b, G, 1, kk, h, w)
        pad = (K - 1) // 2
        xp = jnp.pad(x, ((0, 0), (pad, K - 1 - pad), (pad, K - 1 - pad), (0, 0)))
        patches = jnp.stack([xp[:, i:i + h, j:j + w, :] for i in range(K) for j in range(K)], axis=3)
        out = patches.reshape(b, h, w, kk * c).transpose(0, 3, 1, 2).reshape(b, G, GC, kk, h, w)
        out = jnp.einsum('bgokhw,bgckhw->bgchw', wgt, out)
        out = out.reshape(b, FILTERS, h, w).transpose(0, 2, 3, 1)
        return out

    def _L2_ffn_ref(h, gate_w, gate_b, w1, b1, w2, b2):
        import math
        import jax, jax.numpy as jnp
        import numpy as np
        CAPACITY_FACTOR = 1.25
        B, L, D = h.shape
        E = gate_w.shape[1]
        T = B * L
        C = max(1, math.ceil(CAPACITY_FACTOR * T / E))
        x = h.reshape(T, D)
        logits = x @ gate_w + gate_b
        probs = jax.nn.softmax(logits, axis=-1)
        idx = jnp.argmax(probs, axis=-1)
        prb = jnp.take_along_axis(probs, idx[:, None], axis=1)[:, 0]
        one_hot = jax.nn.one_hot(idx, E, dtype=jnp.float32)
        pos = (jnp.cumsum(one_hot, axis=0) * one_hot).sum(-1).astype(jnp.int32) - 1
        kept = pos < C
        pos_safe = jnp.where(kept, pos, C)
        buf = jnp.zeros((E, C, D), dtype=h.dtype).at[idx, pos_safe].set(x, mode='drop')
        hmid = jax.nn.relu(jnp.einsum('ecd,edf->ecf', buf, w1) + b1[:, None, :])
        ybuf = jnp.einsum('ecf,efd->ecd', hmid, w2) + b2[:, None, :]
        pos_g = jnp.minimum(pos, C - 1)
        y_tok = ybuf[idx, pos_g] * (prb * kept)[:, None]
        y = y_tok.reshape(B, L, D)
        y = jnp.nan_to_num(y, nan=0.0, posinf=10000.0, neginf=-10000.0)
        return y

    def _L3_conv_ref(x, W):
        import jax, jax.numpy as jnp
        import numpy as np
        return jnp.einsum('bhwc,co->bhwo', x, W)

    def _L3_ffn_ref(x, gate_w, gate_b, w1, w2, w3):
        import jax, jax.numpy as jnp
        import numpy as np
        D_MODEL = 64
        N_EXPERTS = 16
        HIDDEN = 128
        SCALE = 0.02
        n_experts = w1.shape[0]
        logits = jnp.einsum('bsd,de->bse', x, gate_w) + gate_b
        probs = jax.nn.softmax(logits, axis=-1)
        top_probs, top_idx = jax.lax.top_k(probs, 2)
        top_probs = top_probs / jnp.sum(top_probs, axis=-1, keepdims=True)
        dispatch = jnp.sum(jax.nn.one_hot(top_idx, n_experts, dtype=x.dtype) * top_probs[..., None], axis=-2)
        h1 = jnp.einsum('bsd,edh->bseh', x, w1)
        h2 = jnp.einsum('bsd,edh->bseh', x, w2)
        hidden = jax.nn.silu(h1) * h2
        expert_out = jnp.einsum('bseh,eho->bseo', hidden, w3)
        return jnp.einsum('bseo,bse->bso', expert_out, dispatch)

    def _gn(v, G=32, eps=1e-05):
        B_, H_, W_, C_ = v.shape
        g = v.reshape(B_, H_, W_, G, C_ // G)
        m = jnp.mean(g, axis=(1, 2, 4), keepdims=True)
        s = jnp.var(g, axis=(1, 2, 4), keepdims=True)
        return ((g - m) / jnp.sqrt(s + eps)).reshape(v.shape)

    def _ln_c(v, eps=1e-06):
        m = jnp.mean(v, axis=-1, keepdims=True)
        s = jnp.var(v, axis=-1, keepdims=True)
        return (v - m) / jnp.sqrt(s + eps)

    def _ln_t(v, eps=1e-05):
        m = jnp.mean(v, axis=-1, keepdims=True)
        s = jnp.var(v, axis=-1, keepdims=True)
        return (v - m) / jnp.sqrt(s + eps)

    def _to_tokens(v):
        B_, H_, W_, C_ = v.shape
        return v.reshape(B_, H_ * W_, C_)

    def _from_tokens(t, like):
        return t.reshape(like.shape)
    x = x + _L0_conv_ref(_ln_c(x), L0_conv_in_proj_w, L0_conv_conv_w, L0_conv_conv_b, L0_conv_xproj_w, L0_conv_dt_w, L0_conv_dt_b, L0_conv_A_logs, L0_conv_Ds, L0_conv_out_proj_w)
    t = _to_tokens(x)
    t = t + _L0_ffn_ref(_ln_t(t), L0_ffn_Wr, L0_ffn_br, L0_ffn_ln_g, L0_ffn_ln_b, L0_ffn_W1, L0_ffn_b1, L0_ffn_W2, L0_ffn_b2)
    x = _from_tokens(t, x)
    x = x + _L1_conv_ref(_ln_c(x), L1_conv_qkv_w, L1_conv_qkv_b, L1_conv_proj_w, L1_conv_proj_b, L1_conv_rpb)
    t = _to_tokens(x)
    t = t + _L1_ffn_ref(_ln_t(t), L1_ffn_Wg, L1_ffn_bg, L1_ffn_W1, L1_ffn_b1, L1_ffn_W2, L1_ffn_b2)
    x = _from_tokens(t, x)
    x = x + _L2_conv_ref(_ln_c(x), L2_conv_W1, L2_conv_b1, L2_conv_W2, L2_conv_b2)
    t = _to_tokens(x)
    t = t + _L2_ffn_ref(_ln_t(t), L2_ffn_gate_w, L2_ffn_gate_b, L2_ffn_w1, L2_ffn_b1, L2_ffn_w2, L2_ffn_b2)
    x = _from_tokens(t, x)
    x = x + _L3_conv_ref(_ln_c(x), L3_conv_W)
    t = _to_tokens(x)
    t = t + _L3_ffn_ref(_ln_t(t), L3_ffn_gate_w, L3_ffn_gate_b, L3_ffn_w1, L3_ffn_w2, L3_ffn_w3)
    x = _from_tokens(t, x)
    return x

_drawn_inputs = setup_inputs


def setup_inputs(seed=0):
    import zlib

    import numpy as np

    out = dict(_drawn_inputs(seed))
    spreads = {'L0_conv_conv_b': (0.0, 0.358),
     'L0_conv_Ds': (1.0, 0.6),
     'L0_ffn_br': (0.0, 0.1),
     'L0_ffn_ln_g': (1.0, 0.2),
     'L0_ffn_ln_b': (0.0, 0.1),
     'L0_ffn_b1': (0.0, 0.1),
     'L0_ffn_b2': (0.0, 0.1),
     'L1_conv_qkv_b': (0.0, 0.414),
     'L1_conv_proj_b': (0.0, 0.1),
     'L1_ffn_bg': (0.0, 0.1),
     'L1_ffn_b1': (0.0, 0.444),
     'L1_ffn_b2': (0.0, 0.1),
     'L2_conv_b1': (0.0, 0.1),
     'L2_conv_b2': (0.0, 0.1),
     'L2_ffn_gate_b': (0.0, 0.1),
     'L2_ffn_b1': (0.0, 0.8),
     'L2_ffn_b2': (0.0, 0.758),
     'L3_ffn_gate_b': (0.0, 0.8)}
    factors = {'L0_conv_in_proj_w': 2.697,
     'L0_conv_conv_w': 4.434,
     'L0_conv_xproj_w': 8.0,
     'L0_conv_dt_w': 8.0,
     'L0_conv_dt_b': 8.0,
     'L0_conv_A_logs': 8.0,
     'L0_conv_out_proj_w': 3.097,
     'L1_conv_qkv_w': 5.423,
     'L1_conv_proj_w': 3.089,
     'L1_conv_rpb': 8.0,
     'L1_ffn_W1': 2.876,
     'L3_ffn_gate_w': 8.0,
     'L3_ffn_w1': 8.0,
     'L3_ffn_w2': 8.0,
     'L3_ffn_w3': 8.0}
    for name, (base, spread) in spreads.items():
        noise = np.random.default_rng([zlib.crc32(name.encode()), seed]).standard_normal(out[name].shape)
        drawn = base * np.exp(spread * noise) if base else spread * noise
        out[name] = jnp.asarray(drawn.astype(out[name].dtype))
    for name, factor in factors.items():
        out[name] = (out[name] * factor).astype(out[name].dtype)
    return out
```

```python
from contextlib import ExitStack

import concourse.bass as bass
from concourse import mybir
import numpy as np

ALU = mybir.AluOpType
ACT = mybir.ActivationFunctionType
F32 = mybir.dt.float32
BF16 = mybir.dt.bfloat16
X_AXIS = mybir.AxisListType.X

P = 128
BATCH, SIDE, CH = 2, 16, 64
TOKENS = BATCH * SIDE * SIDE
TB = TOKENS // P
HALVES = P // CH
BANK = 512
BIG = 1.0e30
FLT_MAX = 3.4028234663852886e38

INNER, STATE, RANK, DIRS = 128, 16, 16, 4
TILE_CH = P // STATE
GROUPS = 4
PER_GROUP = 32 // TILE_CH
SEQ = SIDE * SIDE
PARTS = 3
PAIRS_PER_DIR = GROUPS * PER_GROUP // 2
PAIRS = DIRS * PAIRS_PER_DIR
HC_SLOTS = 6
PAD = SIDE + 2

HEADS, HEAD_CH, WIN = 8, 8, 7
KEY_ROWS = 11
KEYS = KEY_ROWS * SIDE
KEY_HALF = KEYS // 2
KEY_ROW0 = [0, 5]
BIAS_ROWS, BIAS_COLS = 21, 31
UNITS = TB * HEADS

TAPS, INV_GROUPS, INV_HID = 9, 4, 16
TAP_BLOCKS = [(0, 1), (4, 5), (6, 7), (3, 2), (8,)]
CAPACITY = 80

E_OF = [8, 8, 8, 16]
HID_BLOCKS = [16, 16, 16, 16]
LN_OF_FFN = [1, 3, 5, 7]
EPS = [1e-6, 1e-5, 1e-6, 1e-5, 1e-6, 1e-5, 1e-6, 1e-5]
RING = 8

LOG_FROM = 2.0 ** -6
LOG_C2, LOG_C1, LOG_C0 = 0.32755528, -1.5263569653, 3.0529197377


def build(nc, d, out):
    ctx = ExitStack()
    with ctx:
        def sb(name, shape, dt=F32):
            return ctx.enter_context(nc.sbuf_tensor(name, shape, dt))

        def sem(name):
            return ctx.enter_context(nc.semaphore(name))

        ps = ctx.enter_context(nc.psum_tensor("ps", [P, 8, BANK], F32))

        def bank(i):
            return ps[:, i, :]

        c32 = sb("c32", [P, C32_COLS])
        c16 = sb("c16", [P, C16_COLS], BF16)

        def k32(name):
            o, n = C32_AT[name]
            return c32[:, o:o + n]

        def k16(name):
            o, n = C16_AT[name]
            return c16[:, o:o + n]

        ident, anti, stack_i = k32("ident"), k32("anti"), k32("stack_i")
        state_sum = k32("state_sum").rearrange("p (m c) -> p m c", c=32)
        tap_sum = k32("tap_sum").rearrange("p (r c) -> p r c", c=CH)
        window = k32("window").rearrange("p (q k) -> p q k", k=KEYS)
        ident16, tri16, ones16 = k16("ident"), k16("tri"), k16("ones")
        spread = k16("spread").rearrange("p (m c) -> p m c", c=P)
        spread_w = {8: k16("spread_w8").rearrange("p (m c) -> p m c", c=P),
                    16: k16("spread_w16").rearrange("p (m c) -> p m c", c=P)}
        rank_of = {8: k32("rank8"), 16: k32("rank16")}

        cols = sb("cols", [P, COLS_N])
        rows = sb("rows", [P, ROWS_N])

        def col(name, i=0):
            o = COLS_AT[name][0] + i
            return cols[:, o:o + 1]

        def colv(name):
            o, n = COLS_AT[name]
            return cols[:, o:o + n]

        def row(name):
            o, n = ROWS_AT[name]
            return rows[:, o:o + n]

        x = sb("x", [P, 9, TB, CH])
        xn = sb("xn", [P, TB, HALVES * CH])
        xt = sb("xt", [P, TOKENS])
        stats = sb("stats", [P, TB, 6])
        mv = sb("mv", [P, TB, 2])
        ve = sb("ve", [P, 2, TB])
        rstd = sb("rstd", [P, 2, TB])
        sq = sb("sq", [P, TB])
        mhalf = sb("mhalf", [P, TB])

        w_bc = sb("w_bc", [P, DIRS, 2, P])
        aexp = sb("aexp", [P, 64])
        aneg = sb("aneg", [P, 64])
        w_out = sb("w_out", [P, CH])
        log_from, log_at = sb("log_from", [P, 1]), sb("log_at", [P, 1])

        wr = [sb(f"wr_{f}", [P, E_OF[f]]) for f in range(4)]
        b1f = sb("b1f", [P, 16])

        w_qk = sb("w_qk", [P, 4, P])
        w_v = sb("w_v", [P, CH])
        w_pr = sb("w_pr", [CH, CH])
        bias_g = sb("bias_g", [SIDE, HEADS, BIAS_ROWS, SIDE])
        bias = sb("bias", [P, 2, HEADS, KEYS])
        w_i1 = sb("w_i1", [P, INV_HID])
        w_i2 = sb("w_i2", [INV_HID + 1, 5, P])
        w_pt = sb("w_pt", [P, CH])

        arena = sb("arena", [P, ARENA])

        def view(at, n):
            return arena[:, at:at + n]

        u = view(0, 2048).rearrange("p (k l) -> p k l", k=DIRS)
        zs = view(2048, 512)
        dd = view(2560, 4096).rearrange("p (k v l) -> p k v l", k=DIRS, v=2)
        res = view(6656, 4096).rearrange("p (b r v l) -> p b r v l", b=2, r=2, v=2)
        stk = view(10752, 8192).rearrange("p (b g v l) -> p b g v l", b=2, g=GROUPS, v=2)
        bc = view(18944, 4096).rearrange("p (k v l) -> p k v l", k=DIRS, v=2)
        xp = view(18944 + 2048, 2 * PAD * PAD).rearrange("p (b h w) -> p b h w", b=2, h=PAD)
        da = view(23040, 2048).rearrange("p (b s l) -> p b s l", b=2, s=2)
        hs = view(25088, 2048).rearrange("p (b s l) -> p b s l", b=2, s=2)
        w_in = view(27136, 2 * INNER)
        w_conv = view(27392, TAPS * INNER).rearrange("p (s c) -> p s c", s=TAPS)
        w_xdt = view(28544, DIRS * P)[0:RANK].rearrange("p (k c) -> p k c", k=DIRS)
        w_dt = view(29056, DIRS * P)[0:RANK].rearrange("p (k c) -> p k c", k=DIRS)
        w_fdt = view(29568, DIRS * P).rearrange("p (k c) -> p k c", k=DIRS)
        diag = view(30080, DIRS * P).rearrange("p (k c) -> p k c", k=DIRS)
        alog = view(30592, P)[0:64]
        hc = view(27136, HC_SLOTS * 1024).rearrange("p (b s l) -> p b s l", b=HC_SLOTS, s=2)
        z_ = view(25088, 2048).rearrange("p (k l) -> p k l", k=DIRS)
        z1 = view(30720, 2048).rearrange("p (k l) -> p k l", k=DIRS)
        zmax = view(14848, 2048).rearrange("p (k l) -> p k l", k=DIRS)
        zmin = view(16896, 2048).rearrange("p (k l) -> p k l", k=DIRS)
        gated = view(2560, 512)
        hid = view(0, RING * 512).rearrange("p (r l) -> p r l", r=RING)
        wb = view(4096, 4096).rearrange("p (q l) -> p q l", q=8)
        acc = view(8192, 512)
        tmp = view(8704, 1024).rearrange("p (r l) -> p r l", r=2)
        gate = view(9728, 1024).rearrange("p (r l) -> p r l", r=2)
        w1 = [sb("w1_0", [P, 16 * P])[:]] + [view(11264 + 2048 * f, 2048) for f in range(2)] + [view(15360, 4096)]
        w2 = [sb("w2_0", [P, 16, CH])[:]] + [view(19456 + 1024 * f, 1024).rearrange("p (b c) -> p b c", c=CH) for f in range(3)]
        qf = view(0, 1024).rearrange("p (a l) -> p a l", a=2)
        kf = view(1024, 1024).rearrange("p (a l) -> p a l", a=2)
        vf = view(2048, 512)[0:KEY_HALF].rearrange("p (u c) -> p u c", u=8)
        sm = view(2560, 16 * KEYS).rearrange("p (r k) -> p r k", r=16)
        pr = view(5376, 16 * KEYS).rearrange("p (r k) -> p r k", r=16)
        pt = view(8192, 4 * 512)[0:KEY_HALF].rearrange("p (r l) -> p r l", r=4)
        ao = view(10240, 256).rearrange("p (t c) -> p t c", t=TB)
        at = view(10496, 512)[0:CH]
        xpp = view(22528, 2 * PAD * PAD).rearrange("p (b h w) -> p b h w", b=2, h=PAD)
        ih = view(23176, 512)[0:INV_HID + 1]
        prod = view(23688, 5 * 512).rearrange("p (r l) -> p r l", r=5)

        lg = sb("lg", [P, 64]); dl = sb("dl", [P, 64]); c1 = sb("c1", [P, 64]); oh1 = sb("oh1", [P, 64])
        d2 = sb("d2", [P, 64]); g2 = sb("g2", [P, 64]); c2 = sb("c2", [P, 64]); oh2 = sb("oh2", [P, 64])
        ex = sb("ex", [P, 64]); ww = sb("ww", [P, 64]); wr1 = sb("wr1", [P, 64]); wr2 = sb("wr2", [P, 64])
        m1 = sb("m1", [P, TB]); i1 = sb("i1", [P, TB]); m2 = sb("m2", [P, TB]); i2 = sb("i2", [P, TB])
        th = sb("th", [P, TB]); wa = sb("wa", [P, TB]); wc = sb("wc", [P, TB])
        oh16 = sb("oh16", [P, 32], BF16)
        wp = sb("wp", [P, TB, 48], BF16)
        wt = sb("wt", [48, TOKENS], BF16)
        nan_a, nan_b = sb("nan_a", [P, 256]), sb("nan_b", [P, 256])
        finite = sb("finite", [P, 256], mybir.dt.uint32)
        mx = sb("mx", [P, UNITS]); nmx = sb("nmx", [P, UNITS]); rsum = sb("rsum", [P, UNITS]); rrec = sb("rrec", [P, UNITS])

        load = {n: sem("l_" + n) for n in LOADS}
        dve_step, pool_step = sem("dve_step"), sem("pool_step")
        var_ready, rstd_ready, ln_ready = sem("var_ready"), sem("rstd_ready"), sem("ln_ready")
        xt_ps, xt_sb, resid = sem("xt_ps"), sem("xt_sb"), sem("resid")
        zeroed = sem("zeroed")
        zmax_ready, log_at_ready = sem("zmax_ready"), sem("log_at_ready")
        prep_ps, fdt_ps, aexp_ready, aneg_ready = sem("prep_ps"), sem("fdt_ps"), sem("aexp_ready"), sem("aneg_ready")
        fdt_sb, bias_seen, w1_scaled = sem("fdt_sb"), sem("bias_seen"), sem("w1_scaled")
        xi_ps, z_ps, xp_ready, conv_ps, u0_ready = sem("xi_ps"), sem("z_ps"), sem("xp_ready"), sem("conv_ps"), sem("u0_ready")
        zs_ready = sem("zs_ready")
        rev_ps, u_ready, dts_ps, delta_ready = sem("rev_ps"), sem("u_ready"), sem("dts_ps"), sem("delta_ready")
        parts_ready = sem("parts_ready")
        abs_ready, z_ready, log_ready, z1_ready = sem("abs_ready"), sem("z_ready"), sem("log_ready"), sem("z1_ready")
        lost_ready, log1p_ready, relu_ready = [sem("lost_dve"), sem("lost_pool")], [sem("log1p_dve"), sem("log1p_pool")], sem("relu_ready")
        stacked = [sem("stacked0"), sem("stacked1")]
        bc_ps, bc_sb, diag_ready = sem("bc_ps"), sem("bc_sb"), sem("diag_ready")
        dspread, uspread, exp_done = sem("dspread"), sem("uspread"), sem("exp_done")
        mul_done, scan_done, hc_done, sum_done = sem("mul_done"), sem("scan_done"), sem("hc_done"), sem("sum_done")
        gated_ready, proj_ps = sem("gated_ready"), sem("proj_ps")
        logits, gap, gap_act, w_ready, wt_ps, wt_sb = (sem(n) for n in ("logits", "gap", "gap_act", "w_ready", "wt_ps", "wt_sb"))
        hid_ps, hid_ready, y_ready, wb_ps, wb_sb, comb = (sem(n) for n in ("hid_ps", "hid_ready", "y_ready", "wb_ps", "wb_sb", "comb"))
        acc_ready, out_ps, gate_ready = sem("acc_ready"), sem("out_ps"), sem("gate_ready")
        oh_ready, count_ps = sem("oh_ready"), sem("count_ps")
        bias_built, bias_ready = sem("bias_built"), sem("bias_ready")
        qk_ps, v_ps, q_sb, k_sb, v_sb = (sem(n) for n in ("qk_ps", "v_ps", "q_sb", "k_sb", "v_sb"))
        score, masked, negmax, prob, pt_ps, pt_sb, pv = (sem(n) for n in ("score", "masked", "negmax", "prob", "pt_ps", "pt_sb", "pv"))
        ao_ready, ao_ps, at_sb, apr_ps = (sem(n) for n in ("ao_ready", "ao_ps", "at_sb", "apr_ps"))
        ih_ps, ih_sb, pad_ready, wq_ps, prod_ready, inv_ps = (sem(n) for n in ("ih_ps", "ih_sb", "pad_ready", "wq_ps", "prod_ready", "inv_ps"))
        stored = sem("stored")

        block = ctx.enter_context(nc.Block())

        def var_count(n):
            return n + 1 + (n > 1)

        def high(v2d):
            return v2d.bitcast(BF16).rearrange("p (l two) -> p l two", two=2)[:, :, 1]

        def tiles(v, n=TB):
            return v.rearrange("p (t e) -> p t e", t=n)

        def spread_last(v, n):
            return v.unsqueeze(2).to_broadcast([v.shape[0], v.shape[1], n])

        def probs_copy(eng, g):
            eng.wait_ge(pt_ps, g + 1)
            if g >= 4:
                eng.wait_ge(pv, 2 * (g - 4) + 2)
            src, dst = bank(5 + g % 2)[0:KEY_HALF], pt[:, g % 4]
            if g % 2 == 0:
                eng.activation(dst, src, ACT.Copy).then_inc(pt_sb[0], 1)
            else:
                eng.tensor_copy(dst, src).then_inc(pt_sb[1], 1)

        pt_sb = [sem("pt_sb_act"), sem("pt_sb_dve")]

        def log1p(eng, k):
            on, count = int(k > 0), max(k, 1)
            eng.wait_ge(z1_ready, k + 1)
            eng.tensor_tensor(z1[:, k], zmax[:, k], z1[:, k], ALU.subtract).then_inc(lost_ready[on], 1)
            eng.wait_ge(lost_ready[on], count)
            eng.wait_ge(log_ready, k + 1)
            eng.tensor_tensor(z1[:, k], z1[:, k], dd[:, k, 1], ALU.add).then_inc(log1p_ready[on], 1)

        pair_tiles = [[(2 * (i % 2) + s, (i % PAIRS_PER_DIR) // 2) for s in range(2)] for i in range(PAIRS)]

        @block.sync
        def _(sp):
            def get(name, dst, src):
                sp.dma_start(dst, src).then_inc(load[name], 16)

            get("x", x[:, 0], d["x"].rearrange("(t p) c -> p t c", p=P))
            get("c32", c32[:], d["c32"])
            get("cols", cols[:], d["cols"])
            get("w_in", w_in, d["w_in"])
            get("alog", alog, d["alog"])
            get("w_xdt", w_xdt, d["w_xdt"])
            get("w_dt", w_dt, d["w_dt"])
            get("w_conv", w_conv, d["w_conv"])
            get("w_bc", w_bc[:], d["w_bc"])
            get("c16", c16[:], d["c16"])
            get("rows", rows[:], d["rows"].partition_broadcast(P))
            get("w1_0", w1[0][CH:P, :], d["w1_0"])
            for j in range(SIDE):
                sp.dma_start(bias_g[j:j + 1], d["rpb"][:, :, SIDE - 1 - j:2 * SIDE - 1 - j].unsqueeze(0)).then_inc(load["rpb"], 16)

            def stack(k):
                if k >= 2:
                    sp.wait_ge(dspread, 2 * PAIRS_PER_DIR * (k - 1))
                    sp.wait_ge(uspread, PAIRS_PER_DIR * (k - 1))
                for part in range(PARTS):
                    sp.wait_ge(parts_ready, PARTS * k + part + 1)
                    for g in range(GROUPS):
                        src = dd[32 * g:32 * g + 32, k] if part == 0 else res[32 * g:32 * g + 32, k % 2, part - 1]
                        sp.dma_start(stk[32 * part:32 * part + 32, k % 2, g], src).then_inc(stacked[k % 2], 16)

            get("w_out", w_out[:], d["w_out"])
            for f in range(4):
                get(f"wr_{f}", wr[f][:], d[f"wr_{f}"])
            stack(0)
            get("w2_0", w2[0], d["w2_0"])
            for i in range(SIDE // 2):
                for q in range(2):
                    first = KEY_ROW0[q] - (8 * q + i) + 6 + 4
                    if i == 0 and q == 0:
                        sp.wait_ge(load["rpb"], 16 * SIDE)
                    sp.dma_start(bias[16 * i:16 * i + 16, q].rearrange("p h k -> p h k"),
                                 bias_g[:, :, first:first + KEY_ROWS, :].rearrange("p h a c -> p h (a c)"))\
                      .then_inc(bias_built, 16)
            stack(1)
            get("w_qk", w_qk[:], d["w_qk"])
            get("w_v", w_v[:], d["w_v"])
            get("w_pr", w_pr[:], d["w_pr"])
            stack(2)
            get("w_i1", w_i1[:], d["w_i1"])
            get("w_i2", w_i2[:], d["w_i2"])
            get("w_pt", w_pt[:], d["w_pt"])
            stack(3)
            sp.wait_ge(sum_done, PAIRS // 2)
            for f in (1, 2, 3):
                get(f"w1_{f}", w1[f][0:CH, :], d[f"w1_{f}"])
                get(f"w2_{f}", w2[f], d[f"w2_{f}"])
            sp.wait_ge(resid, 8)
            sp.dma_start(out.rearrange("(t p) c -> p t c", p=P), x[:, 8]).then_inc(stored, 16)
            sp.wait_ge(stored, 16)

        @block.gpsimd
        def _(pool):
            def rsqrt(which, count):
                pool.wait_ge(var_ready, count)
                pool.tensor_tensor(rstd[:, which], ve[:, which], mhalf[:], ALU.pow).then_inc(rstd_ready, 1)

            pool.memset(mhalf[:], -0.5).then_inc(pool_step, 1)
            pool.memset(xp, 0.0).then_inc(zeroed, 1)
            pool.memset(da.rearrange("p b s (i l) -> p (b s i) l", l=SEQ)[:, :, 0:1], 0.0).then_inc(zeroed, 1)
            pool.memset(log_from[:], LOG_FROM).then_inc(zeroed, 1)
            pool.wait_ge(pool_step, 1)
            rsqrt(0, var_count(0))
            pool.memset(w1[0][0:CH, :], 0.0).then_inc(zeroed, 1)
            for k in range(1, DIRS):
                log1p(pool, k)
            for i in range(PAIRS):
                k = i // PAIRS_PER_DIR
                if i == 0:
                    pool.wait_ge(bc_sb, 2)
                elif i % PAIRS_PER_DIR == 0:
                    pool.wait_ge(bc_sb, 2 * k + 2)
                if i >= HC_SLOTS:
                    pool.wait_ge(sum_done, (i - HC_SLOTS) // 2 + 1)
                pool.wait_ge(scan_done, i + 1)
                c_all = bc[:, k, 1].unsqueeze(1).to_broadcast([P, 2, 2 * SEQ])
                pool.tensor_tensor(hc[:, i % HC_SLOTS], hs[:, i % 2], c_all, ALU.mult).then_inc(hc_done, 1)
            pool.wait_ge(bias_built, 16 * SIDE)
            pool.wait_ge(load["c32"], 16)
            pool.wait_ge(sum_done, PAIRS // 2)
            for q in range(2):
                outside = window[:, q].unsqueeze(1).to_broadcast([P, HEADS, KEYS])
                pool.tensor_tensor(bias[:, q], bias[:, q], outside, ALU.add).then_inc(bias_ready, 1)
            rsqrt(0, 2)
            rsqrt(1, 3)
            pool.wait_ge(rstd_ready, 3)
            for f in (1, 2, 3):
                pool.memset(w1[f][CH:P, :], 0.0).then_inc(zeroed, 1)
            pool.wait_ge(zeroed, 7)
            pool.memset(view(22528, 2 * PAD * PAD), 0.0).then_inc(zeroed, 1)
            pool.memset(ih, 1.0).then_inc(zeroed, 1)
            pool.wait_ge(zeroed, 9)
            for n in range(2, 8):
                rsqrt(0, var_count(n))

        @block.scalar
        def _(act):
            def turned(n):
                act.wait_ge(xt_ps, n + 1)
                act.activation(xt[:], bank(0), ACT.Copy).then_inc(xt_sb, 1)

            act.preload_act_table(ACT.Silu)
            turned(0)
            act.wait_ge(z_ps, 1)
            act.activation(zs, bank(2), ACT.Silu).then_inc(zs_ready, 1)
            act.wait_ge(load["cols"], 16)
            act.wait_ge(conv_ps, 1)
            act.activation(u[:, 0], bank(3), ACT.Silu, bias=col("conv_b")).then_inc(u0_ready, 1)
            act.preload_act_table_set("natural_log_exp_and_others")
            act.wait_ge(zeroed, 3)
            act.activation(log_at[:], log_from[:], ACT.Ln, bias=1.0).then_inc(log_at_ready, 1)
            for k in range(DIRS):
                act.wait_ge(dts_ps, k + 1)
                act.activation(dd[:, k, 1], bank(k), ACT.Abs, bias=col("dt_b", k)).then_inc(abs_ready, 1)
                act.wait_ge(abs_ready, k + 1)
                act.activation(z_[:, k], dd[:, k, 1], ACT.Exp, scale=-1.0).then_inc(z_ready, 1)
                act.activation(dd[:, k, 0], bank(k), ACT.Relu, bias=col("dt_b", k)).then_inc(relu_ready, 1)
                act.wait_ge(z_ready, k + 1)
                act.wait_ge(zmax_ready, k + 1)
                act.activation(dd[:, k, 1], zmax[:, k], ACT.Ln, bias=1.0).then_inc(log_ready, 1)
            act.wait_ge(prep_ps, 1)
            act.activation(aexp[:], bank(4)[:, 0:64], ACT.Exp).then_inc(aexp_ready, 1)

            def bc_copy(q):
                act.wait_ge(bc_ps, q + 1)
                if q == 4:
                    act.wait_ge(conv_ps, 1)
                act.activation(bc[:, q // 2, q % 2], bank(7), ACT.Copy).then_inc(bc_sb, 1)

            bc_copy(0)
            bc_copy(1)
            for i in range(PAIRS):
                k, ii = divmod(i, PAIRS_PER_DIR)
                if i == 0:
                    act.wait_ge(aneg_ready, 1)
                    act.wait_ge(zeroed, 2)
                if i >= 2:
                    act.wait_ge(scan_done, i - 1)
                for s, (g, m) in enumerate(pair_tiles[i]):
                    act.wait_ge(dspread, 2 * i + s + 1)
                    q = 16 * k + PER_GROUP * g + m
                    act.activation(da[:, i % 2, s].rearrange("p (b l) -> p b l", b=2)[:, :, 1:SEQ],
                                   bank(s).rearrange("p (b l) -> p b l", b=2)[:, :, 1:SEQ],
                                   ACT.Exp, scale=aneg[:, q:q + 1]).then_inc(exp_done, 1)
                if k < DIRS - 1 and ii in (3, 5):
                    bc_copy(2 * (k + 1) + (ii == 5))

            def experts(f, func):
                base, base_w = 16 * f, 4 * f
                if f == 2:
                    act.wait_ge(gap, f + 1)
                    act.activation(ex[:, 0:32], dl[:, 0:32], ACT.Exp).then_inc(gap_act, 1)
                for j in range(16):
                    act.wait_ge(hid_ps, base + j + 1)
                    if j >= RING:
                        act.wait_ge(y_ready, base_w + (j - RING) // 4 + 1)
                    p, q = divmod(j, 4)
                    blk = 4 * p + 2 * (q % 2) + q // 2
                    b1 = b1f[:, blk:blk + 1] if f == 0 else col(f"b1_{f}", blk)
                    act.activation(hid[:, j % RING], bank(1 + j % 4), func, bias=b1).then_inc(hid_ready, 1)
                    if j == 2 and f < 2:
                        act.wait_ge(gap, f + 1)
                        act.activation(th[:], m2[:], ACT.Tanh, scale=-0.5).then_inc(gap_act, 1)
                    if j % 4 == 3 and j > 3:
                        weight_copy(base_w, p - 1)
                weight_copy(base_w, 3)

            def weight_copy(base_w, p):
                act.wait_ge(wb_ps, base_w + p + 1)
                act.activation(wb[:, p], bank(7), ACT.Copy).then_inc(wb_sb, 1)

            act.preload_act_table(ACT.Gelu)
            turned(1)
            act.wait_ge(w1_scaled, 2)
            experts(0, ACT.Gelu)

            act.preload_act_table(ACT.Exp)
            turned(2)
            act.wait_ge(qk_ps, 2)
            for a in range(2):
                act.activation(kf[:, a], bank(3 + a), ACT.Identity, bias=col("k_b", a)).then_inc(k_sb, 1)
            for t in range(TB):
                act.wait_ge(negmax, t + 1)
                for h in range(HEADS):
                    unit = t * HEADS + h
                    if unit >= 16:
                        act.wait_ge(pt_ps, (unit - 16) // 2 + 1)
                    act.activation(pr[:, unit % 16], sm[:, unit % 16], ACT.Exp, bias=nmx[:, unit:unit + 1],
                                   accum_out=rsum[:, unit:unit + 1]).then_inc(prob, 1)
                    if unit >= 4 and unit % 4 == 0:
                        probs_copy(act, unit // 2 - 2)
            probs_copy(act, 14)
            act.wait_ge(ao_ps, 1)
            act.activation(at, bank(0)[0:CH], ACT.Copy).then_inc(at_sb, 1)
            act.preload_act_table(ACT.Gelu)
            turned(3)
            experts(1, ACT.Gelu)

            act.preload_act_table(ACT.Exp)
            turned(4)
            act.wait_ge(zeroed, 9)
            act.wait_ge(xt_sb, 5)
            act.activation(xpp[0:CH, :, 1:SIDE + 1, 1:SIDE + 1],
                           xt[0:CH].rearrange("p (b h w) -> p b h w", b=2, h=SIDE), ACT.Copy).then_inc(pad_ready, 1)
            act.wait_ge(ih_ps, 1)
            act.activation(ih[0:INV_HID], bank(1)[0:INV_HID], ACT.Identity,
                           bias=col("b_i1")[0:INV_HID]).then_inc(ih_sb, 1)
            turned(5)
            experts(2, ACT.Relu)

            act.preload_act_table(ACT.Silu)
            turned(6)
            turned(7)
            for j in range(16):
                act.wait_ge(hid_ps, 48 + j + 1)
                if j >= 2:
                    act.wait_ge(hid_ready, 48 + j - 1)
                act.activation(gate[:, j % 2], bank(1 + 2 * (j % 2)), ACT.Silu).then_inc(gate_ready, 1)
                if j == 3:
                    act.wait_ge(gap, 4)
                    act.activation(th[:], m2[:], ACT.Tanh, scale=-0.5).then_inc(gap_act, 1)
                if j % 2 == 1 and j >= 5:
                    weight_copy(12, (j - 5) // 2)
            weight_copy(12, 6)
            weight_copy(12, 7)

        @block.tensor
        def _(pe):
            def turn(n):
                pe.wait_ge(ln_ready, n + 1)
                if n:
                    pe.wait_ge(xt_sb, n)
                for t in range(TB):
                    last = pe.transpose(bank(0)[:, t * P:(t + 1) * P], xn[:, t], ident)
                last.then_inc(xt_ps, 1)

            def got(*names):
                for n in names:
                    pe.wait_ge(load[n], 16)

            got("c32", "alog", "w_xdt", "w_dt")
            pe.transpose(bank(4)[:, 0:64], alog, ident[0:64, 0:64]).then_inc(prep_ps, 1)
            for k in range(DIRS):
                last = pe.matmul(bank(5)[:, k * P:(k + 1) * P], w_xdt[:, k], w_dt[:, k], start=True, stop=True)
            last.then_inc(fdt_ps, 1)
            turn(0)
            got("w_in")
            pe.wait_ge(xt_sb, 1)
            pe.matmul(bank(1), w_in[:, 0:INNER], xt[:], start=True, stop=True).then_inc(xi_ps, 1)
            pe.matmul(bank(2), w_in[:, INNER:], xt[:], start=True, stop=True).then_inc(z_ps, 1)
            got("w_conv")
            pe.wait_ge(xp_ready, 1)
            for s in range(TAPS):
                dy, dx = divmod(s, 3)
                last = pe.matmul(bank(3), w_conv[:, s], xp[:, :, dy:dy + SIDE, dx:dx + SIDE],
                                 start=(s == 0), stop=(s == TAPS - 1))
            last.then_inc(conv_ps, 1)
            pe.wait_ge(u0_ready, 1)
            pe.wait_ge(fdt_sb, 1)

            def dts(k):
                pe.matmul(bank(k), w_fdt[:, k], u[:, 0 if k < 2 else 2], start=True, stop=True).then_inc(dts_ps, 1)

            def bc_mm(q):
                if q:
                    pe.wait_ge(bc_sb, q)
                pe.matmul(bank(7), w_bc[:, q // 2, q % 2], u[:, 0 if q < 4 else 2], start=True, stop=True).then_inc(bc_ps, 1)

            dts(0)
            pe.matmul(bank(6), anti, u[:, 0], start=True, stop=True).then_inc(rev_ps, 1)
            got("w_bc")
            bc_mm(0)
            dts(1)
            pe.wait_ge(u_ready, 1)
            pe.wait_ge(zs_ready, 1)
            dts(2)
            dts(3)
            bc_mm(1)
            pe.wait_ge(diag_ready, 1)
            pe.wait_ge(u_ready, 3)
            for k in range(DIRS):
                pe.matmul(bank(6), diag[:, k], u[:, k], start=(k == 0), stop=False, skip_group_check=True)
            got("w1_0", "cols")
            pe.wait_ge(zeroed, 4)
            pe.wait_ge(bc_sb, 2)
            for blk in range(16):
                last = pe.matmul(bank(7)[:, blk:blk + 1], w1[0][:, blk * P:(blk + 1) * P], col("ln_b", blk // 2),
                                 start=True, stop=True)
            last.then_inc(bias_seen, 1)

            def spread_pair(i):
                k = i // PAIRS_PER_DIR
                if i % PAIRS_PER_DIR == 0:
                    pe.wait_ge(stacked[k % 2], 16 * PARTS * GROUPS * (k // 2 + 1))
                for s, (g, m) in enumerate(pair_tiles[i]):
                    if i:
                        pe.wait_ge(exp_done, 2 * (i - 1) + s + 1)
                    pe.matmul(bank(s), spread[0:96, m], high(stk[0:96, k % 2, g, 0]),
                              start=True, stop=True).then_inc(dspread, 1)
                if i >= 2:
                    pe.wait_ge(scan_done, i - 1)
                for s, (g, m) in enumerate(pair_tiles[i]):
                    last = pe.matmul(bank(2 + 2 * (i % 2) + s), spread[0:96, m], high(stk[0:96, k % 2, g, 1]),
                                     start=True, stop=True)
                last.then_inc(uspread, 1)

            def sum_states(q):
                pe.wait_ge(hc_done, 2 * q + 2)
                for i in (2 * q, 2 * q + 1):
                    for s, (g, m) in enumerate(pair_tiles[i]):
                        last = pe.matmul(ps[32 * g:32 * g + 32, 6, :], state_sum[:, m], hc[:, i % HC_SLOTS, s],
                                         start=False, stop=(q == PAIRS // 2 - 1), skip_group_check=True)
                last.then_inc(sum_done, 1)

            got("c16")
            pe.wait_ge(delta_ready, DIRS)
            pe.wait_ge(abs_ready, DIRS)
            pe.wait_ge(aexp_ready, 1)
            spread_pair(0)
            spread_pair(1)
            for i in range(PAIRS):
                k, ii = divmod(i, PAIRS_PER_DIR)
                if i + 2 < PAIRS:
                    spread_pair(i + 2)
                if i >= 3 and i % 2:
                    sum_states((i - 3) // 2)
                if k < DIRS - 1 and ii in (2, 4):
                    if k == 0 and ii == 2:
                        pe.wait_ge(w1_scaled, 1)
                    bc_mm(2 * (k + 1) + (ii == 4))
            sum_states(PAIRS // 2 - 1)
            pe.wait_ge(gated_ready, 1)
            got("w_out")
            for t in range(TB):
                last = pe.matmul(bank(1)[:, t * CH:(t + 1) * CH], gated[:, t * P:(t + 1) * P], w_out[:], start=True, stop=True)
            last.then_inc(proj_ps, 1)

            def experts(f):
                n, e_n = LN_OF_FFN[f], E_OF[f]
                pairs = e_n // 2
                base, base_w = 16 * f, 4 * f
                got(f"wr_{f}", f"w1_{f}", f"w2_{f}")
                turn(n)
                pe.wait_ge(xt_sb, n + 1)
                if f == 1:
                    pe.wait_ge(zeroed, 9)
                for t in range(TB):
                    last = pe.matmul(bank(7)[:, t * e_n:(t + 1) * e_n], xt[:, t * P:(t + 1) * P], wr[f][:], start=True, stop=True)
                last.then_inc(logits, 1)
                if f == 0:
                    pe.wait_ge(w1_scaled, 2)
                per = 16 // pairs

                def hidden(p):
                    for q in range(per):
                        j = per * p + q
                        if f < 3:
                            if j >= 4:
                                pe.wait_ge(hid_ready, base + j - 3)
                            blk = 4 * p + 2 * (q % 2) + q // 2
                            pe.matmul(bank(1 + j % 4), w1[f][:, blk * P:(blk + 1) * P], xt[:], start=True, stop=True)\
                              .then_inc(hid_ps, 1)
                        else:
                            if j >= 2:
                                pe.wait_ge(hid_ready, base + j - 1)
                            pe.matmul(bank(1 + 2 * (j % 2)), w1[3][:, j * P:(j + 1) * P], xt[:], start=True, stop=True)
                            pe.matmul(bank(2 + 2 * (j % 2)), w1[3][:, (16 + j) * P:(17 + j) * P], xt[:], start=True, stop=True)\
                              .then_inc(hid_ps, 1)

                def down(p):
                    if p >= 2:
                        pe.wait_ge(comb, base_w + p - 1)
                    for q in range(per):
                        j = per * p + q
                        blk = 4 * p + 2 * (q % 2) + q // 2 if f < 3 else j
                        pe.wait_ge(hid_ready, base + j + 1)
                        o = CH * (q % 2)
                        last = pe.matmul(ps[o:o + CH, 5 + p % 2, :], w2[f][:, blk], hid[:, j % RING],
                                         start=(q < 2), stop=(q >= per - 2), skip_group_check=True)
                    last.then_inc(y_ready, 1)

                def weights(p):
                    if p == 0:
                        pe.wait_ge(w_ready, f + 1)
                        for t in range(TB):
                            last = pe.transpose(bank(7).bitcast(BF16)[0:PARTS * e_n, t * P:(t + 1) * P],
                                                wp[:, t, 0:PARTS * e_n], ident16)
                        last.then_inc(wt_ps, 1)
                        pe.wait_ge(wt_sb, f + 1)
                    elif p:
                        pe.wait_ge(wb_sb, base_w + p)
                    pe.matmul(bank(7), spread_w[e_n][0:PARTS * e_n, p], wt[0:PARTS * e_n, :], start=True, stop=True).then_inc(wb_ps, 1)

                hidden(0)
                if f == 2:
                    pe.wait_ge(oh_ready, 1)
                    for t in range(TB):
                        for t2 in range(t + 1):
                            last = pe.matmul(bank(0)[:, t * 8:t * 8 + 8], tri16 if t2 == t else ones16,
                                             oh16[:, t2 * 8:t2 * 8 + 8], start=(t2 == 0), stop=(t2 == t))
                    last.then_inc(count_ps, 1)
                lag = 0 if f < 3 else 1
                for p in range(1, pairs):
                    hidden(p)
                    if p - 1 - lag >= 0:
                        weights(p - 1 - lag)
                        down(p - 1 - lag)
                for p in range(pairs - 1 - lag, pairs):
                    weights(p)
                    down(p)
                pe.wait_ge(acc_ready, f + 1)
                for t in range(TB):
                    last = pe.matmul(bank(0)[:, t * CH:(t + 1) * CH], acc[:, t * P:(t + 1) * P], stack_i, start=True, stop=True)
                last.then_inc(out_ps, 1)

            experts(0)

            got("w_qk", "w_v", "w_pr")
            turn(2)
            pe.wait_ge(xt_sb, 3)
            for a in range(4):
                last = pe.matmul(bank(1 + a), w_qk[:, a], xt[:], start=True, stop=True)
                if a % 2:
                    last.then_inc(qk_ps, 1)
            for t in range(TB):
                for kb in range(2):
                    k0 = (t // 2) * SEQ + KEY_ROW0[t % 2] * SIDE + kb * KEY_HALF
                    last = pe.matmul(bank(5)[0:KEY_HALF, (2 * t + kb) * CH:(2 * t + kb + 1) * CH],
                                     xt[:, k0:k0 + KEY_HALF], w_v[:], start=True, stop=True)
            last.then_inc(v_ps, 1)

            def scores(unit):
                t, h = divmod(unit, HEADS)
                a, hh = divmod(h, 2)
                k0 = (t // 2) * SEQ + KEY_ROW0[t % 2] * SIDE
                if unit >= 8 and unit % 2 == 0:
                    pe.wait_ge(masked, unit - 6)
                o = 256 * (unit % 2)
                last = pe.matmul(bank(1 + (unit // 2) % 4)[:, o:o + KEYS],
                                 qf[32 * a:32 * a + HEAD_CH, hh, t * P:(t + 1) * P],
                                 kf[32 * a:32 * a + HEAD_CH, hh, k0:k0 + KEYS], start=True, stop=True)
                if unit % 2:
                    last.then_inc(score, 1)

            def probs_turn(g):
                pe.wait_ge(prob, 2 * g + 2)
                if g >= 2:
                    pe.wait_ge(pt_sb[g % 2], (g - 2) // 2 + 1)
                for w in range(2):
                    for kb in range(2):
                        o = (2 * w + kb) * P
                        last = pe.transpose(bank(5 + g % 2)[0:KEY_HALF, o:o + P],
                                            pr[:, (2 * g + w) % 16, kb * KEY_HALF:(kb + 1) * KEY_HALF], ident)
                last.then_inc(pt_ps, 1)

            def values(g):
                pe.wait_ge(pt_sb[g % 2], g // 2 + 1)
                for w in range(2):
                    unit = 2 * g + w
                    t, h = divmod(unit, HEADS)
                    for kb in range(2):
                        last = pe.matmul(bank(7)[:, unit * HEAD_CH:(unit + 1) * HEAD_CH],
                                         pt[:, g % 4, (2 * w + kb) * P:(2 * w + kb + 1) * P],
                                         vf[:, 2 * t + kb, h * HEAD_CH:(h + 1) * HEAD_CH],
                                         start=(kb == 0), stop=(kb == 1))
                    last.then_inc(pv, 1)

            pe.wait_ge(q_sb, 2)
            pe.wait_ge(k_sb, 2)
            for unit in range(8):
                scores(unit)
            pe.wait_ge(v_sb, 1)
            for g in range(16):
                if g < 12:
                    scores(8 + 2 * g)
                    scores(9 + 2 * g)
                probs_turn(g)
                if g >= 2:
                    values(g - 2)
            values(14)
            values(15)
            pe.wait_ge(ao_ready, 1)
            for t in range(TB):
                last = pe.transpose(bank(0)[0:CH, t * P:(t + 1) * P], ao[:, t], ident)
            last.then_inc(ao_ps, 1)
            pe.wait_ge(at_sb, 1)
            for t in range(TB):
                last = pe.matmul(bank(1)[:, t * CH:(t + 1) * CH], at[:, t * P:(t + 1) * P], w_pr[:], start=True, stop=True)
            last.then_inc(apr_ps, 1)

            experts(1)

            got("w_i1", "w_i2")
            turn(4)
            pe.wait_ge(xt_sb, 5)
            pe.matmul(bank(1)[0:INV_HID], w_i1[:], xt[:], start=True, stop=True).then_inc(ih_ps, 1)
            pe.wait_ge(ih_sb, 1)
            for r in range(5):
                m = P if r < 4 else CH
                pe.matmul(bank(2 + r)[0:m], w_i2[:, r, 0:m], ih, start=True, stop=True).then_inc(wq_ps, 1)
            pe.wait_ge(prod_ready, 5)
            for t in range(TB):
                for r in range(5):
                    m = P if r < 4 else CH
                    last = pe.matmul(bank(7)[:, t * CH:(t + 1) * CH], prod[0:m, r, t * P:(t + 1) * P], tap_sum[0:m, r],
                                     start=(r == 0), stop=(r == 4))
            last.then_inc(inv_ps, 1)

            experts(2)

            got("w_pt")
            turn(6)
            pe.wait_ge(xt_sb, 7)
            for t in range(TB):
                last = pe.matmul(bank(1)[:, t * CH:(t + 1) * CH], xt[:, t * P:(t + 1) * P], w_pt[:], start=True, stop=True)
            last.then_inc(proj_ps, 1)
            experts(3)

        @block.vector
        def _(dve):
            steps = [0]

            def mark(ins):
                steps[0] += 1
                ins.then_inc(dve_step, 1)

            def settle():
                dve.wait_ge(dve_step, steps[0])

            def link(ins):
                mark(ins)
                settle()

            def norm(n):
                src = x[:, n]
                if n == 0:
                    dve.wait_ge(load["x"], 16)
                else:
                    dve.wait_ge(resid, n)
                for t in range(TB):
                    mark(dve.bn_stats(stats[:, t], src[:, t]))
                settle()
                for t in range(TB):
                    mark(dve.bn_aggr(mv[:, t], stats[:, t]))
                settle()
                dve.tensor_scalar(ve[:, 0], mv[:, :, 1], EPS[n], None, ALU.add).then_inc(var_ready, 1)
                dve.wait_ge(rstd_ready, var_count(n) if n != 1 else 2)
                for t in range(TB):
                    half = CH if n == 1 else HALVES * CH
                    o = xn[:, t, 0:half].rearrange("p (w c) -> p w c", c=CH)
                    i = src[:, t].unsqueeze(1).to_broadcast([P, half // CH, CH])
                    last = dve.tensor_scalar(o, i, mv[:, t, 0:1], rstd[:, 0, t:t + 1], ALU.subtract, ALU.mult)
                    if n == 1:
                        mark(last)
                if n == 1:
                    link(dve.tensor_tensor(sq[:], rstd[:, 0], rstd[:, 0], ALU.mult))
                    link(dve.tensor_tensor(sq[:], sq[:], mv[:, :, 1], ALU.mult))
                    dve.tensor_scalar(ve[:, 1], sq[:], EPS[1], None, ALU.add).then_inc(var_ready, 1)
                    dve.wait_ge(rstd_ready, 3)
                    for t in range(TB):
                        last = dve.tensor_scalar(xn[:, t, CH:P], xn[:, t, 0:CH], rstd[:, 1, t:t + 1], None, ALU.mult)
                last.then_inc(ln_ready, 1)

            norm(0)
            dve.wait_ge(zeroed, 1)
            dve.wait_ge(xi_ps, 1)
            dve.tensor_copy(xp[:, :, 1:SIDE + 1, 1:SIDE + 1],
                            bank(1).rearrange("p (b h w) -> p b h w", b=2, h=SIDE)).then_inc(xp_ready, 1)
            dve.wait_ge(fdt_ps, 1)
            dve.tensor_copy(w_fdt.rearrange("p k c -> p (k c)"), bank(5)).then_inc(fdt_sb, 1)
            dve.wait_ge(load["cols"], 16)
            dve.wait_ge(load["c32"], 16)
            for k in range(DIRS):
                last = dve.tensor_scalar(diag[:, k], ident, col("ds", k), None, ALU.mult)
            last.then_inc(diag_ready, 1)
            dve.wait_ge(u0_ready, 1)

            def columns_first(v):
                return v.rearrange("p (b h w) -> p b w h", b=2, h=SIDE)

            def grid(v):
                return v.rearrange("p (b h w) -> p b h w", b=2, h=SIDE)

            dve.tensor_copy(grid(u[:, 2]), columns_first(u[:, 0])).then_inc(u_ready, 1)
            def delta_u(k):
                if k == 1:
                    dve.wait_ge(u_ready, 2)
                if k == 2:
                    dve.wait_ge(u_ready, 3)
                dve.wait_ge(delta_ready, k + 1)
                dve.tensor_tensor(dd[:, k, 1], dd[:, k, 0], u[:, k], ALU.mult).then_inc(parts_ready, 1)

            def part(k, r):
                src = dd[:, k] if r == 0 else res[:, k % 2, 0]
                src = src.rearrange("p v l -> p (v l)")
                if k >= 2 and r == 0:
                    dve.wait_ge(stacked[k % 2], 16 * PARTS * GROUPS)
                dve.wait_ge(parts_ready, PARTS * k + r + 1)
                dve.tensor_tensor(res[:, k % 2, r].rearrange("p v l -> p (v l)"), src, high(src), ALU.subtract)\
                   .then_inc(parts_ready, 1)

            def bounded(k):
                dve.wait_ge(z_ready, k + 1)
                dve.tensor_scalar(zmax[:, k], z_[:, k], LOG_FROM, None, ALU.max).then_inc(zmax_ready, 1)
                mark(dve.tensor_scalar(zmin[:, k], z_[:, k], LOG_FROM, None, ALU.min))
                dve.wait_ge(zmax_ready, k + 1)
                dve.tensor_scalar(z1[:, k], zmax[:, k], 1.0, -1.0, ALU.add, ALU.add).then_inc(z1_ready, 1)

            def small_log(k):
                settle()
                link(dve.scalar_tensor_tensor(out=z_[:, k], in0=zmin[:, k], scalar=LOG_C1, in1=zmin[:, k],
                                              op0=ALU.add, op1=ALU.mult))
                mark(dve.scalar_tensor_tensor(out=z_[:, k], in0=z_[:, k], scalar=LOG_C0, in1=zmin[:, k],
                                              op0=ALU.add, op1=ALU.mult))

            def delta(k):
                dve.wait_ge(log1p_ready[k > 0], max(k, 1))
                dve.wait_ge(relu_ready, k + 1)
                dve.wait_ge(log_at_ready, 1)
                link(dve.scalar_tensor_tensor(out=z1[:, k], in0=z1[:, k], scalar=log_at[:], in1=dd[:, k, 0],
                                              op0=ALU.subtract, op1=ALU.add))
                dve.scalar_tensor_tensor(out=dd[:, k, 0], in0=z_[:, k], scalar=LOG_C2, in1=z1[:, k],
                                         op0=ALU.mult, op1=ALU.add).then_inc(delta_ready, 1)

            bounded(0)
            small_log(0)
            log1p(dve, 0)
            delta(0)
            delta_u(0)
            part(0, 0)
            part(0, 1)
            for k in range(1, DIRS):
                bounded(k)
                small_log(k)
                delta(k)
            dve.wait_ge(rev_ps, 1)
            dve.tensor_copy(u[:, 1], bank(6)).then_inc(u_ready, 1)
            dve.tensor_copy(grid(u[:, 3]), columns_first(bank(6))).then_inc(u_ready, 1)
            dve.wait_ge(aexp_ready, 1)
            dve.tensor_scalar(aneg[:], aexp[:], -1.0, None, ALU.mult).then_inc(aneg_ready, 1)
            dve.wait_ge(bias_seen, 1)
            dve.tensor_tensor(b1f[:], bank(7)[:, 0:16], colv("b1_0"), ALU.add).then_inc(w1_scaled, 1)
            for e in range(8):
                o = w1[0][CH:P, 2 * e * P:(2 * e + 2) * P]
                last = dve.tensor_scalar(o, o, col("ln_g", e)[CH:P], None, ALU.mult)
            last.then_inc(w1_scaled, 1)

            def times_b(i):
                dve.wait_ge(uspread, i + 1)
                if i % PAIRS_PER_DIR == 0:
                    dve.wait_ge(bc_sb, 2 * (i // PAIRS_PER_DIR) + 1)
                b_all = bc[:, i // PAIRS_PER_DIR, 0].unsqueeze(1).to_broadcast([P, 2, 2 * SEQ])
                v = ps[:, 2 + 2 * (i % 2):4 + 2 * (i % 2), :]
                dve.tensor_tensor(v, v, b_all, ALU.mult).then_inc(mul_done, 1)

            times_b(0)
            for i in range(PAIRS):
                k, ii = divmod(i, PAIRS_PER_DIR)
                if i + 1 < PAIRS:
                    times_b(i + 1)
                dve.wait_ge(mul_done, i + 1)
                dve.wait_ge(exp_done, 2 * i + 2)
                if i >= 2:
                    dve.wait_ge(hc_done, i - 1)
                dve.tensor_tensor_scan(hs[:, i % 2].rearrange("p s l -> p (s l)"),
                                       da[:, i % 2].rearrange("p s l -> p (s l)"),
                                       ps[:, 2 + 2 * (i % 2):4 + 2 * (i % 2), :].rearrange("p s l -> p (s l)"),
                                       0.0, ALU.mult, ALU.add).then_inc(scan_done, 1)
                if k < DIRS - 1:
                    if ii == 1:
                        delta_u(k + 1)
                    if ii == 2:
                        part(k + 1, 0)
                    if ii == 3:
                        part(k + 1, 1)
            dve.wait_ge(sum_done, PAIRS // 2)
            dve.wait_ge(zs_ready, 1)
            dve.tensor_tensor(gated, bank(6), zs, ALU.mult).then_inc(gated_ready, 1)

            def add(n, src, sem_, count):
                dve.wait_ge(sem_, count)
                dve.tensor_tensor(x[:, n + 1], x[:, n], src.rearrange("p (t c) -> p t c", t=TB), ALU.add)\
                   .then_inc(resid, 1)

            add(0, bank(1)[:, 0:TB * CH], proj_ps, 1)

            def router(f):
                e_n = E_OF[f]
                n = TB * e_n
                dve.wait_ge(load["rows"], 16)
                dve.wait_ge(logits, f + 1)
                link(dve.tensor_tensor(lg[:, 0:n], bank(7)[:, 0:n], row(f"br_{f}"), ALU.add))
                link(dve.tensor_reduce(m1[:], tiles(lg[:, 0:n]), X_AXIS, ALU.max))
                link(dve.tensor_tensor(tiles(dl[:, 0:n]), tiles(lg[:, 0:n]), spread_last(m1[:], e_n), ALU.subtract))
                link(dve.scalar_tensor_tensor(out=c1[:, 0:n], in0=dl[:, 0:n], scalar=0.0, in1=rank_of[e_n],
                                              op0=ALU.is_ge, op1=ALU.mult))
                link(dve.tensor_reduce(i1[:], tiles(c1[:, 0:n]), X_AXIS, ALU.max))
                if f == 2:
                    dve.tensor_tensor(tiles(oh16[:]), tiles(c1[:, 0:n]), spread_last(i1[:], e_n), ALU.is_equal)\
                       .then_inc(oh_ready, 1)
                link(dve.tensor_tensor(tiles(oh1[:, 0:n]), tiles(c1[:, 0:n]), spread_last(i1[:], e_n), ALU.is_equal))
                if f == 2:
                    dve.sem_inc(gap, 1)
                    dve.wait_ge(gap_act, 3)
                    link(dve.tensor_reduce(m2[:], tiles(ex[:, 0:n]), X_AXIS, ALU.add))
                    link(dve.reciprocal(i2[:], m2[:]))
                    dve.wait_ge(count_ps, 1)
                    link(dve.scalar_tensor_tensor(out=c2[:, 0:n], in0=bank(0)[:, 0:n], scalar=float(CAPACITY), in1=oh1[:, 0:n],
                                                  op0=ALU.is_le, op1=ALU.mult))
                    link(dve.tensor_tensor(tiles(ww[:, 0:n]), tiles(c2[:, 0:n]), spread_last(i2[:], e_n), ALU.mult))
                else:
                    link(dve.scalar_tensor_tensor(out=d2[:, 0:n], in0=oh1[:, 0:n], scalar=-BIG, in1=dl[:, 0:n],
                                                  op0=ALU.mult, op1=ALU.add))
                    dve.tensor_reduce(m2[:], tiles(d2[:, 0:n]), X_AXIS, ALU.max).then_inc(gap, 1)
                    dve.wait_ge(gap, f + 1)
                    link(dve.tensor_tensor(tiles(g2[:, 0:n]), tiles(d2[:, 0:n]), spread_last(m2[:], e_n), ALU.is_ge))
                    link(dve.tensor_tensor(c2[:, 0:n], g2[:, 0:n], rank_of[e_n], ALU.mult))
                    link(dve.tensor_reduce(i2[:], tiles(c2[:, 0:n]), X_AXIS, ALU.max))
                    link(dve.tensor_tensor(tiles(oh2[:, 0:n]), tiles(c2[:, 0:n]), spread_last(i2[:], e_n), ALU.is_equal))
                    dve.wait_ge(gap_act, f + 1)
                    mark(dve.tensor_scalar(wa[:], th[:], 0.5, 0.5, ALU.mult, ALU.add))
                    link(dve.tensor_scalar(wc[:], th[:], -0.5, 0.5, ALU.mult, ALU.add))
                    mark(dve.tensor_tensor(tiles(wr1[:, 0:n]), tiles(oh1[:, 0:n]), spread_last(wa[:], e_n), ALU.mult))
                    link(dve.tensor_tensor(tiles(wr2[:, 0:n]), tiles(oh2[:, 0:n]), spread_last(wc[:], e_n), ALU.mult))
                    link(dve.tensor_tensor(ww[:, 0:n], wr1[:, 0:n], wr2[:, 0:n], ALU.add))
                w3 = tiles(ww[:, 0:n])
                r3 = tiles(wr1[:, 0:n])
                link(dve.tensor_copy(wp[:, :, 0:e_n], w3))
                link(dve.tensor_tensor(r3, w3, wp[:, :, 0:e_n], ALU.subtract))
                link(dve.tensor_copy(wp[:, :, e_n:2 * e_n], r3))
                dve.tensor_tensor(wp[:, :, 2 * e_n:3 * e_n], r3, wp[:, :, e_n:2 * e_n], ALU.subtract).then_inc(w_ready, 1)
                dve.wait_ge(wt_ps, f + 1)
                dve.tensor_copy(wt[0:PARTS * e_n, :], bank(7).bitcast(BF16)[0:PARTS * e_n, 0:TOKENS]).then_inc(wt_sb, 1)

            def combine(f, p):
                base_w, pairs = 4 * f, E_OF[f] // 2
                dve.wait_ge(wb_sb, base_w + p + 1)
                dve.wait_ge(y_ready, base_w + p + 1)
                o = acc if p == 0 else tmp[:, p % 2]
                b2 = col(f"b2_{f}", p) if f < 3 else 0.0
                dve.scalar_tensor_tensor(out=o, in0=bank(5 + p % 2), scalar=b2, in1=wb[:, p],
                                         op0=ALU.add, op1=ALU.mult).then_inc(comb, 1)
                if p:
                    dve.wait_ge(comb, base_w + p + 1)
                    last = dve.tensor_tensor(acc, acc, tmp[:, p % 2], ALU.add)
                    if p == pairs - 1:
                        last.then_inc(acc_ready, 1)
                    else:
                        link(last)

            def finish(f):
                n = LN_OF_FFN[f]
                if f < 2 or f == 3:
                    add(n, bank(0)[:, 0:TB * CH], out_ps, f + 1)
                    return
                dve.wait_ge(out_ps, f + 1)
                y = bank(0)[:, 0:TB * CH]
                mark(dve.tensor_scalar(nan_a[:], y, FLT_MAX, 1.0e4, ALU.is_gt, ALU.mult))
                mark(dve.tensor_scalar(nan_b[:], y, -FLT_MAX, -1.0e4, ALU.is_lt, ALU.mult))
                link(dve.tensor_scalar(finite[:], y, 0.0, 0.0, ALU.mult, ALU.is_equal))
                link(dve.tensor_tensor(nan_a[:], nan_a[:], nan_b[:], ALU.add))
                link(dve.copy_predicated(nan_a[:], finite[:], y))
                dve.tensor_tensor(x[:, n + 1], x[:, n], nan_a[:].rearrange("p (t c) -> p t c", t=TB), ALU.add).then_inc(resid, 1)

            norm(1)
            router(0)
            for p in range(4):
                combine(0, p)
            finish(0)

            norm(2)
            dve.wait_ge(qk_ps, 1)
            for a in range(2):
                dve.tensor_scalar(qf[:, a], bank(1 + a), col("q_b", a), float(HEAD_CH) ** -0.5, ALU.add, ALU.mult)\
                   .then_inc(q_sb, 1)
            dve.wait_ge(v_ps, 1)
            v_b = row("v_b")[0:KEY_HALF].unsqueeze(1).to_broadcast([KEY_HALF, 8, CH])
            dve.tensor_tensor(vf, bank(5)[0:KEY_HALF].rearrange("p (u c) -> p u c", u=8), v_b, ALU.add).then_inc(v_sb, 1)
            pr_b = row("pr_b").unsqueeze(1).to_broadcast([P, TB, CH])
            xb = nan_a[:].rearrange("p (t c) -> p t c", t=TB)
            mark(dve.tensor_tensor(xb, x[:, 2], pr_b, ALU.add))
            dve.wait_ge(bias_ready, 2)
            for t in range(TB):
                for h in range(HEADS):
                    unit = t * HEADS + h
                    dve.wait_ge(score, unit // 2 + 1)
                    if unit >= 16:
                        dve.wait_ge(prob, unit - 15)
                    o = 256 * (unit % 2)
                    dve.tensor_tensor_reduce(sm[:, unit % 16], bank(1 + (unit // 2) % 4)[:, o:o + KEYS], bias[:, t % 2, h],
                                             1.0, -3.0e38, ALU.add, ALU.max, mx[:, unit:unit + 1]).then_inc(masked, 1)
                    if t and h % 4 == 3:
                        probs_copy(dve, 4 * t - 4 + 1 + 2 * (h // 4))
                dve.wait_ge(masked, t * HEADS + HEADS)
                dve.tensor_scalar(nmx[:, t * HEADS:(t + 1) * HEADS], mx[:, t * HEADS:(t + 1) * HEADS], -1.0, None, ALU.mult)\
                   .then_inc(negmax, 1)
            probs_copy(dve, 13)
            probs_copy(dve, 15)
            dve.wait_ge(prob, UNITS)
            link(dve.reciprocal(rrec[:], rsum[:]))
            dve.wait_ge(pv, UNITS)
            dve.tensor_tensor(ao.rearrange("p t (h c) -> p (t h) c", c=HEAD_CH),
                              bank(7)[:, 0:256].rearrange("p (u c) -> p u c", c=HEAD_CH),
                              spread_last(rrec[:], HEAD_CH), ALU.mult).then_inc(ao_ready, 1)
            dve.wait_ge(apr_ps, 1)
            settle()
            dve.tensor_tensor(x[:, 3], xb, bank(1)[:, 0:256].rearrange("p (t c) -> p t c", t=TB), ALU.add).then_inc(resid, 1)

            norm(3)
            router(1)
            for p in range(4):
                combine(1, p)
            finish(1)

            norm(4)
            dve.wait_ge(xt_sb, 5)
            dve.wait_ge(zeroed, 9)
            dve.tensor_copy(xpp[CH:P, :, 1:SIDE + 1, 0:SIDE],
                            xt[CH:P].rearrange("p (b h w) -> p b h w", b=2, h=SIDE)).then_inc(pad_ready, 1)
            dve.wait_ge(pad_ready, 2)
            for r, taps in enumerate(TAP_BLOCKS):
                dve.wait_ge(wq_ps, r + 1)
                whole = len(taps) == 2 and taps[1] == taps[0] + 1
                for half, tap in enumerate(taps[:1] if whole else taps):
                    dy, dx = divmod(tap, 3)
                    rows_ = slice(0, P) if whole else slice(CH * half, CH * half + CH)
                    dx -= half
                    last = dve.tensor_tensor(grid(prod[rows_, r]), grid(bank(2 + r)[rows_]),
                                             xpp[rows_, :, dy:dy + SIDE, dx:dx + SIDE], ALU.mult)
                last.then_inc(prod_ready, 1)
            add(4, bank(7)[:, 0:256], inv_ps, 1)

            norm(5)
            router(2)
            for p in range(4):
                combine(2, p)
            finish(2)

            norm(6)
            add(6, bank(1)[:, 0:256], proj_ps, 2)
            norm(7)

            def gate_mul(j):
                dve.wait_ge(gate_ready, j + 1)
                if j >= RING:
                    dve.wait_ge(y_ready, 12 + (j - RING) // 2 + 1)
                dve.tensor_tensor(hid[:, j % RING], gate[:, j % 2], bank(2 + 2 * (j % 2)), ALU.mult).then_inc(hid_ready, 1)

            for j in range(4):
                gate_mul(j)
            router(3)
            for p in range(8):
                if p < 6:
                    gate_mul(2 * p + 4)
                    gate_mul(2 * p + 5)
                combine(3, p)
            finish(3)


def _places(sizes):
    at, o = {}, 0
    for n, s in sizes:
        at[n] = (o, s)
        o += s
    return at, o


C32_AT, C32_COLS = _places([("ident", P), ("anti", P), ("stack_i", CH), ("state_sum", PER_GROUP * 32),
                            ("tap_sum", 5 * CH), ("window", 2 * KEYS), ("rank8", TB * 8), ("rank16", TB * 16)])
C16_AT, C16_COLS = _places([("ident", P), ("tri", P), ("ones", P), ("spread", PER_GROUP * P),
                            ("spread_w8", 4 * P), ("spread_w16", 8 * P)])
COLS_AT, COLS_N = _places([("conv_b", 1), ("dt_b", 4), ("ds", 4), ("b1_0", 16), ("b1_1", 16), ("b1_2", 16),
                           ("b2_0", 4), ("b2_1", 4), ("b2_2", 4), ("q_b", 2), ("k_b", 2), ("b_i1", 1),
                           ("ln_g", 8), ("ln_b", 8)])
ROWS_AT, ROWS_N = _places([("br_0", 32), ("br_1", 32), ("br_2", 32), ("br_3", 64), ("v_b", CH), ("pr_b", CH)])
LOADS = ["x", "c32", "c16", "cols", "rows", "w_in", "alog", "w_xdt", "w_dt", "w_conv", "w_bc", "w_out", "rpb",
         "w_qk", "w_v", "w_pr", "w_i1", "w_i2", "w_pt"] + [f"{a}_{f}" for a in ("w1", "w2", "wr") for f in range(4)]
ARENA = 27136 + HC_SLOTS * 1024


def tap_rows():
    rows = np.full((5, P), -1)
    for r, taps in enumerate(TAP_BLOCKS):
        for half, tap in enumerate(taps):
            rows[r, CH * half:CH * half + CH] = tap * CH + np.arange(CH)
    return rows


def constants():
    c = {n: np.zeros((P, s), np.float32) for n, (_, s) in C32_AT.items()}
    i = np.arange(P)
    c["ident"][:] = np.eye(P)
    c["anti"][:] = np.eye(P)[::-1]
    c["stack_i"][:] = np.tile(np.eye(CH), (2, 1))
    for m in range(PER_GROUP):
        c["state_sum"][i, m * 32 + m * TILE_CH + i // STATE] = 1
    rows = tap_rows()
    for r in range(5):
        ok = rows[r] >= 0
        c["tap_sum"][i[ok], r * CH + rows[r][ok] // TAPS] = 1
    start = np.clip(np.arange(SIDE) - WIN // 2, 0, SIDE - WIN)
    for q in range(2):
        qi, qj = 8 * q + i // SIDE, i % SIDE
        key = np.arange(KEYS)
        ki, kj = KEY_ROW0[q] + key // SIDE, key % SIDE
        inside = ((ki[None] >= start[qi][:, None]) & (ki[None] < start[qi][:, None] + WIN)
                  & (kj[None] >= start[qj][:, None]) & (kj[None] < start[qj][:, None] + WIN))
        c["window"][:, q * KEYS:(q + 1) * KEYS] = np.where(inside, 0.0, -BIG)
    c["rank8"][:] = np.tile(8 - np.arange(8), TB)
    c["rank16"][:] = np.tile(16 - np.arange(16), TB)
    h = {n: np.zeros((P, s), np.float32) for n, (_, s) in C16_AT.items()}
    h["ident"][:] = np.eye(P)
    h["tri"][:] = np.triu(np.ones((P, P)))
    h["ones"][:] = 1
    for m in range(PER_GROUP):
        for part in range(PARTS):
            for ch in range(TILE_CH):
                o = m * P + ch * STATE
                h["spread"][32 * part + TILE_CH * m + ch, o:o + STATE] = 1
    for e_n in (8, 16):
        for p in range(e_n // 2):
            for part in range(PARTS):
                for half in range(2):
                    o = p * P + CH * half
                    h[f"spread_w{e_n}"][part * e_n + 2 * p + half, o:o + CH] = 1
    return np.concatenate(list(c.values()), 1), np.concatenate(list(h.values()), 1).astype(mybir.dt.np(BF16))


def lay_out(a):
    def rows_to(w, n=P):
        return np.concatenate([w, np.zeros((n - w.shape[0], *w.shape[1:]), w.dtype)], 0)

    o = {}
    o["c32"], o["c16"] = constants()
    o["x"] = a["x"].reshape(TOKENS, CH)
    o["w_in"] = rows_to(a["L0_conv_in_proj_w"])
    o["w_conv"] = a["L0_conv_conv_w"].transpose(1, 2, 3, 0).reshape(INNER, TAPS, INNER)
    xproj = a["L0_conv_xproj_w"]
    half = xproj.shape[0] // 2
    o["w_xdt"] = np.stack([xproj[half * (k // 2) + RANK * (k % 2):][:RANK] for k in range(DIRS)], 1)
    o["w_dt"] = a["L0_conv_dt_w"].transpose(2, 0, 1)
    o["w_bc"] = np.stack([np.stack([np.tile(xproj[half * (k // 2) + 2 * RANK + 2 * STATE * v + STATE * (k % 2):][:STATE].T, (1, TILE_CH))
                                    for v in range(2)], 1) for k in range(DIRS)], 1)
    o["alog"] = a["L0_conv_A_logs"].reshape(64, P)
    o["w_out"] = a["L0_conv_out_proj_w"]
    for f, n in enumerate(("L0_ffn_W1", "L1_ffn_W1", "L2_ffn_w1")):
        o[f"w1_{f}"] = a[n].transpose(1, 0, 2).reshape(CH, -1)
        w = a[n[:-2] + ("W2" if f < 2 else "w2")]
        o[f"w2_{f}"] = w.reshape(16, P, CH).transpose(1, 0, 2)
    o["w1_3"] = np.concatenate([a["L3_ffn_" + n].transpose(1, 0, 2).reshape(CH, -1) for n in ("w1", "w2")], 1)
    o["w2_3"] = a["L3_ffn_w3"].transpose(1, 0, 2)
    for f, n in enumerate(("L0_ffn_Wr", "L1_ffn_Wg", "L2_ffn_gate_w", "L3_ffn_gate_w")):
        o[f"wr_{f}"] = rows_to(a[n])
    o["rpb"] = np.zeros((HEADS, BIAS_ROWS, BIAS_COLS), np.float32)
    o["rpb"][:, 4:17, 9:22] = a["L1_conv_rpb"]
    qkv, qkv_b = a["L1_conv_qkv_w"], a["L1_conv_qkv_b"]
    o["w_qk"] = np.zeros((P, 4, P), np.float32)
    qk_b = np.zeros((P, 4), np.float32)
    for which in range(2):
        for h in range(HEADS):
            src = CH * which + HEAD_CH * h + np.arange(HEAD_CH)
            dst = 32 * (h // 2) + np.arange(HEAD_CH)
            o["w_qk"][:CH, 2 * which + h % 2, dst] = qkv[src].T
            qk_b[dst, 2 * which + h % 2] = qkv_b[src]
    o["w_v"] = rows_to(qkv[2 * CH:].T)
    o["w_pr"] = a["L1_conv_proj_w"].T
    o["w_i1"] = rows_to(a["L2_conv_W1"])
    w_i2 = np.concatenate([a["L2_conv_W2"], a["L2_conv_b2"][None]], 0)
    rows = tap_rows()
    of = np.where(rows < 0, 0, rows // (TAPS * CH // INV_GROUPS) * TAPS + rows % TAPS)
    o["w_i2"] = w_i2[:, of]
    o["w_pt"] = rows_to(a["L3_conv_W"])
    c = {n: np.zeros((P, s), np.float32) for n, (_, s) in COLS_AT.items()}
    c["conv_b"][:, 0] = a["L0_conv_conv_b"]
    c["dt_b"][:] = a["L0_conv_dt_b"].T
    c["ds"][:] = a["L0_conv_Ds"].T
    for f, n in enumerate(("L0_ffn_b1", "L1_ffn_b1", "L2_ffn_b1")):
        c[f"b1_{f}"][:] = a[n].reshape(16, P).T
        c[f"b2_{f}"][:] = a[n[:-1] + "2"].reshape(4, P).T
    c["q_b"][:], c["k_b"][:] = qk_b[:, 0:2], qk_b[:, 2:4]
    c["b_i1"][:INV_HID, 0] = a["L2_conv_b1"]
    c["ln_g"][CH:] = a["L0_ffn_ln_g"].T
    c["ln_b"][CH:] = a["L0_ffn_ln_b"].T
    o["cols"] = np.concatenate(list(c.values()), 1)
    r = [np.tile(a[n], TB) for n in ("L0_ffn_br", "L1_ffn_bg", "L2_ffn_gate_b", "L3_ffn_gate_b")]
    o["rows"] = np.concatenate([*r, qkv_b[2 * CH:], a["L1_conv_proj_b"]])
    return {n: np.ascontiguousarray(v) for n, v in o.items()}


def kernel(**inputs):
    import concourse.bacc as bacc
    from concourse.bass_utils import run_bass_kernel_spmd

    arrays = lay_out({n: np.asarray(v) for n, v in inputs.items()})
    nc = bacc.Bacc("TRN2", target_bir_lowering=False, num_devices=1)
    d = {n: nc.dram_tensor("in_" + n, v.shape, mybir.dt.from_np(v.dtype), kind="ExternalInput").ap()
         for n, v in arrays.items()}
    out = nc.dram_tensor("out", (TOKENS, CH), F32, kind="ExternalOutput").ap()
    build(nc, d, out)
    r = run_bass_kernel_spmd(nc, [{"in_" + n: v for n, v in arrays.items()}], core_ids=[0])
    return r.results[0]["out"].reshape(BATCH, SIDE, SIDE, CH)
```

```python
from contextlib import ExitStack

import concourse.bass as bass
from concourse import mybir
import numpy as np

ALU = mybir.AluOpType
ACT = mybir.ActivationFunctionType
F32 = mybir.dt.float32
BF16 = mybir.dt.bfloat16
X_AXIS = mybir.AxisListType.X

P = 128
BATCH, SIDE, CH = 2, 16, 64
TOKENS = BATCH * SIDE * SIDE
TB = TOKENS // P
HALVES = P // CH
BANK = 512
BIG = 1.0e30
FLT_MAX = 3.4028234663852886e38

INNER, STATE, RANK, DIRS = 128, 16, 16, 4
TILE_CH = P // STATE
GROUPS = 4
PER_GROUP = 32 // TILE_CH
SEQ = SIDE * SIDE
PARTS = 3
PAIRS_PER_DIR = GROUPS * PER_GROUP // 2
PAIRS = DIRS * PAIRS_PER_DIR
HC_SLOTS = 4
PAD = SIDE + 2

HEADS, HEAD_CH, WIN = 8, 8, 7
KEY_ROWS = 11
KEYS = KEY_ROWS * SIDE
KEY_HALF = KEYS // 2
KEY_ROW0 = [0, 5]
UNITS = TB * HEADS

TAPS, INV_GROUPS, INV_HID = 9, 4, 16
TAP_BLOCKS = [(0, 1), (4, 5), (6, 7), (3, 2), (8,)]
CAPACITY = 80

E_OF = [8, 8, 8, 16]
HID_BLOCKS = [16, 16, 16, 16]
LN_OF_FFN = [1, 3, 5, 7]
EPS = [1e-6, 1e-5, 1e-6, 1e-5, 1e-6, 1e-5, 1e-6, 1e-5]
RING = 8
WARM_NORM = 16

LOG_FROM = 2.0 ** -6
LOG_C2, LOG_C1, LOG_C0 = 0.32755528, -1.5263569653, 3.0529197377


def build(nc, d, out):
    ctx = ExitStack()
    with ctx:
        def sb(name, shape, dt=F32):
            return ctx.enter_context(nc.sbuf_tensor(name, shape, dt))

        def sem(name):
            return ctx.enter_context(nc.semaphore(name))

        ps = ctx.enter_context(nc.psum_tensor("ps", [P, 8, BANK], F32))

        def bank(i):
            return ps[:, i, :]

        c32 = sb("c32", [P, C32_COLS])
        c16 = sb("c16", [P, C16_COLS], BF16)

        def k32(name):
            o, n = C32_AT[name]
            return c32[:, o:o + n]

        def k16(name):
            o, n = C16_AT[name]
            return c16[:, o:o + n]

        ident, anti, stack_i = k32("ident"), k32("anti"), k32("stack_i")
        to_scan, anti_to_scan = k32("to_scan"), k32("anti_to_scan")
        state_sum = k32("state_sum").rearrange("p (m c) -> p m c", c=32)
        tap_sum = k32("tap_sum").rearrange("p (r c) -> p r c", c=CH)
        window = k32("window").rearrange("p (q k) -> p q k", k=KEYS)
        ident16, tri16, ones16 = k16("ident"), k16("tri"), k16("ones")
        spread = k16("spread").rearrange("p (m c) -> p m c", c=P)
        spread_w = {8: k16("spread_w8").rearrange("p (m c) -> p m c", c=P),
                    16: k16("spread_w16").rearrange("p (m c) -> p m c", c=P)}
        head_mask = k32("head_mask")
        rank_of = {8: k32("rank8"), 16: k32("rank16")}

        cols = sb("cols", [P, COLS_N])
        rows = sb("rows", [P, ROWS_N])

        def col(name, i=0):
            o = COLS_AT[name][0] + i
            return cols[:, o:o + 1]

        def colv(name):
            o, n = COLS_AT[name]
            return cols[:, o:o + n]

        def row(name):
            o, n = ROWS_AT[name]
            return rows[:, o:o + n]

        x = sb("x", [P, 9, TB, CH])
        xn = sb("xn", [P, TB, HALVES * CH])
        xt = sb("xt", [P, TOKENS])
        stats = sb("stats", [P, TB, 6])
        mv = sb("mv", [P, TB, 2])
        ve = sb("ve", [P, 2, TB])
        rstd = sb("rstd", [P, 2, TB])
        sq = sb("sq", [P, TB])
        mhalf = sb("mhalf", [P, 2, TB])

        w_bc = sb("w_bc", [P, DIRS, 2, P])
        aexp = sb("aexp", [P, 64])
        aneg = sb("aneg", [P, 64])
        w_out = sb("w_out", [P, CH])
        idle = sb("idle", [P, 512], BF16)
        log_from, log_at = sb("log_from", [P, 1]), sb("log_at", [P, 1])

        wr = [sb(f"wr_{f}", [P, E_OF[f]]) for f in range(4)]
        b1f = sb("b1f", [P, 16])

        w_qk = sb("w_qk", [P, 2, P])
        w_v = sb("w_v", [P, CH])
        w_pr = sb("w_pr", [P, 2, CH])
        bias = sb("bias", [P, 2, HEADS, KEYS])
        w_i1 = sb("w_i1", [P, INV_HID])
        w_i2 = sb("w_i2", [INV_HID + 1, 5, P])
        w_pt = sb("w_pt", [P, CH])

        arena = sb("arena", [P, ARENA])

        def view(at, n):
            return arena[:, at:at + n]

        u = view(0, 2048).rearrange("p (k l) -> p k l", k=DIRS)
        zs = view(2048, 512)
        dd = view(2560, 4096).rearrange("p (k v l) -> p k v l", k=DIRS, v=2)
        res = view(6656, 4096).rearrange("p (b r v l) -> p b r v l", b=2, r=2, v=2)
        stk = view(10752, 8192).rearrange("p (b g v l) -> p b g v l", b=2, g=GROUPS, v=2)
        bc = view(18944, 4096).rearrange("p (k v l) -> p k v l", k=DIRS, v=2)
        xp = view(18944 + 2048, 2 * PAD * PAD).rearrange("p (b h w) -> p b h w", b=2, h=PAD)
        da = view(23040, 2048).rearrange("p (b s l) -> p b s l", b=2, s=2)
        hs = view(25088, 2048).rearrange("p (b s l) -> p b s l", b=2, s=2)
        w_in = view(27136, 2 * INNER)
        w_conv = view(27392, TAPS * INNER).rearrange("p (s c) -> p s c", s=TAPS)
        w_xdt = view(28544, DIRS * P)[0:RANK].rearrange("p (k c) -> p k c", k=DIRS)
        w_dt = view(29056, DIRS * P)[0:RANK].rearrange("p (k c) -> p k c", k=DIRS)
        w_fdt = view(29568, DIRS * P).rearrange("p (k c) -> p k c", k=DIRS)
        d_mix = view(30080, 2 * P).rearrange("p (k c) -> p k c", k=2)
        alog = view(30592, P)[0:64]
        hc = view(27136, HC_SLOTS * 1024).rearrange("p (b s l) -> p b s l", b=HC_SLOTS, s=2)
        ub = view(27136 + HC_SLOTS * 1024, 2048).rearrange("p (b s l) -> p b s l", b=2, s=2)
        z_ = [view(25088, 512)] + [sb(f"z_{k}", [P, 512])[:] for k in range(1, DIRS)]
        z1 = [view(30720, 512)] + [sb(f"z1_{k}", [P, 512])[:] for k in range(1, DIRS)]
        zmax = view(14848, 2048).rearrange("p (k l) -> p k l", k=DIRS)
        zmin = [view(16896, 512)] + [xn.rearrange("p t c -> p (t c)"), xt[:], sb("zmin_3", [P, 512])[:]]
        gated = view(2560, 512)
        hid = view(0, RING * 512).rearrange("p (r l) -> p r l", r=RING)
        wb = view(4096, 4096).rearrange("p (q l) -> p q l", q=8)
        acc = view(8192, 512)
        tmp = view(8704, 1024).rearrange("p (r l) -> p r l", r=2)
        gate = view(9728, 1024).rearrange("p (r l) -> p r l", r=2)
        w1 = [sb("w1_0", [P, 16 * P])[:]] + [view(11264 + 2048 * f, 2048) for f in range(2)] + [view(15360, 4096)]
        w2 = [sb("w2_0", [P, 16, CH])[:]] + [view(19456 + 1024 * f, 1024).rearrange("p (b c) -> p b c", c=CH) for f in range(3)]
        qf, kf = view(0, 512), view(512, 512)
        qz = view(1024, 4096).rearrange("p (h l) -> p h l", h=HEADS)
        sm = view(5120, 16 * KEYS).rearrange("p (r k) -> p r k", r=16)
        pr = view(7936, 16 * KEYS).rearrange("p (r k) -> p r k", r=16)
        pt = view(23688, 4 * 512)[0:KEY_HALF].rearrange("p (r l) -> p r l", r=4)
        vz = view(26248, 2048)[0:KEY_HALF].rearrange("p (u h c) -> p u h c", u=8, h=HEADS)
        at = view(28296, 1024).rearrange("p (a l) -> p a l", a=2)
        xpp = view(22528, 2 * PAD * PAD).rearrange("p (b h w) -> p b h w", b=2, h=PAD)
        ih = view(23176, 512)[0:INV_HID + 1]
        prod = view(23688, 5 * 512).rearrange("p (r l) -> p r l", r=5)

        lg = sb("lg", [P, 64]); dl = sb("dl", [P, 64]); c1 = sb("c1", [P, 64]); oh1 = sb("oh1", [P, 64])
        d2 = sb("d2", [P, 64]); g2 = sb("g2", [P, 64]); c2 = sb("c2", [P, 64]); oh2 = sb("oh2", [P, 64])
        ex = sb("ex", [P, 64]); ww = sb("ww", [P, 64]); wr1 = sb("wr1", [P, 64]); wr2 = sb("wr2", [P, 64])
        m1 = sb("m1", [P, TB]); i1 = sb("i1", [P, TB]); m2 = sb("m2", [P, TB]); i2 = sb("i2", [P, TB])
        th = sb("th", [P, TB]); wa = sb("wa", [P, TB]); wc = sb("wc", [P, TB])
        oh16 = sb("oh16", [P, 32], BF16)
        wp = sb("wp", [P, TB, 48], BF16)
        wt = view(10752, 256).bitcast(BF16)[0:48]
        nan_a = view(11008, 256)
        nan_b, finite = view(23688, 256), view(23944, 256).bitcast(mybir.dt.uint32)
        mx = sb("mx", [P, UNITS]); nmx = sb("nmx", [P, UNITS]); rsum = sb("rsum", [P, UNITS]); rrec = sb("rrec", [P, UNITS])

        load = {n: sem("l_" + n) for n in LOADS}
        dve_step, pool_step = sem("dve_step"), sem("pool_step")
        var_ready, rstd_ready, ln_ready = sem("var_ready"), sem("rstd_ready"), sem("ln_ready")
        xt_ps, xt_sb, resid = sem("xt_ps"), sem("xt_sb"), sem("resid")
        zeroed = sem("zeroed")
        zmax_ready, log_at_ready = sem("zmax_ready"), sem("log_at_ready")
        prep_ps, fdt_ps, aexp_ready, aneg_ready = sem("prep_ps"), sem("fdt_ps"), sem("aexp_ready"), sem("aneg_ready")
        fdt_sb, bias_seen, w1_scaled = sem("fdt_sb"), sem("bias_seen"), sem("w1_scaled")
        xi_ps, z_ps, xp_ready, conv_ps, u0_ready = sem("xi_ps"), sem("z_ps"), sem("xp_ready"), sem("conv_ps"), sem("u0_ready")
        zs_ready = sem("zs_ready")
        rev_ps, u_ready, dts_ps, delta_ready = sem("rev_ps"), sem("u_ready"), sem("dts_ps"), sem("delta_ready")
        delta_u_ready, rest_ready, rest_pool = [sem("delta_u_dve"), sem("delta_u_pool")], sem("rest_ready"), sem("rest_pool")
        abs_ready, z_ready, log_ready, z1_ready = sem("abs_ready"), sem("z_ready"), sem("log_ready"), sem("z1_ready")
        b1f_ready, hc_last = sem("b1f_ready"), sem("hc_last")
        lost_ready, log1p_ready, relu_ready = [sem("lost_dve"), sem("lost_pool")], [sem("log1p_dve"), sem("log1p_pool")], sem("relu_ready")
        stacked = [sem("stacked0"), sem("stacked1")]
        bc_ps, bc_sb, diag_ready = sem("bc_ps"), sem("bc_sb"), sem("diag_ready")
        dspread, uspread, exp_done = sem("dspread"), sem("uspread"), sem("exp_done")
        mul_done, scan_done, hc_done, sum_done = sem("mul_done"), sem("scan_done"), sem("hc_done"), sem("sum_done")
        gated_ready, proj_ps = sem("gated_ready"), sem("proj_ps")
        logits, gap, gap_act, w_ready, wt_ps, wt_sb = (sem(n) for n in ("logits", "gap", "gap_act", "w_ready", "wt_ps", "wt_sb"))
        hid_ps, hid_ready, y_ready, wb_ps, wb_sb, comb = (sem(n) for n in ("hid_ps", "hid_ready", "y_ready", "wb_ps", "wb_sb", "comb"))
        acc_ready, out_ps, gate_ready = sem("acc_ready"), sem("out_ps"), sem("gate_ready")
        oh_ready, count_ps = sem("oh_ready"), sem("count_ps")
        bias_ready = sem("bias_ready")
        qk_ps, v_ps, q_sb, k_sb, v_sb = (sem(n) for n in ("qk_ps", "v_ps", "q_sb", "k_sb", "v_sb"))
        score, masked, negmax, prob, pt_ps, pt_sb, pv = (sem(n) for n in ("score", "masked", "negmax", "prob", "pt_ps", "pt_sb", "pv"))
        inverse, normed, at_sb, apr_ps = (sem(n) for n in ("inverse", "normed", "at_sb", "apr_ps"))
        ih_ps, ih_sb, pad_ready, wq_ps, prod_ready, inv_ps = (sem(n) for n in ("ih_ps", "ih_sb", "pad_ready", "wq_ps", "prod_ready", "inv_ps"))
        stored = sem("stored")

        block = ctx.enter_context(nc.Block())

        def high(v2d):
            return v2d.bitcast(BF16).rearrange("p (l two) -> p l two", two=2)[:, :, 1]

        def tiles(v, n=TB):
            return v.rearrange("p (t e) -> p t e", t=n)

        def spread_last(v, n):
            return v.unsqueeze(2).to_broadcast([v.shape[0], v.shape[1], n])

        def probs_copy(eng, h, g):
            eng.wait_ge(pt_ps, 2 * h + g + 1)
            if h >= 2:
                eng.wait_ge(pv, h - 1)
            src, dst = bank(5 + g)[0:KEY_HALF], pt[:, 2 * (h % 2) + g]
            if g == 0:
                eng.activation(dst, src, ACT.Copy).then_inc(pt_sb[0], 1)
            else:
                eng.tensor_copy(dst, src).then_inc(pt_sb[1], 1)

        pt_sb = [sem("pt_sb_act"), sem("pt_sb_dve")]
        qz_ready = [sem("qz_ready_dve"), sem("qz_ready_act")]

        def delta_u(eng, k):
            on = int(k > 0)
            eng.wait_ge(u_ready, 3 if k else 1)
            eng.wait_ge(delta_ready, k + 1)
            eng.tensor_tensor(dd[:, k, 1], dd[:, k, 0], u[:, k], ALU.mult).then_inc(delta_u_ready[on], 1)

        def lost(eng, k):
            on = int(k > 0)
            eng.wait_ge(z1_ready, k + 1)
            eng.tensor_tensor(z1[k], zmax[:, k], z1[k], ALU.subtract).then_inc(lost_ready[on], 1)

        def log1p(eng, k):
            on, count = int(k > 0), max(k, 1)
            eng.wait_ge(lost_ready[on], count)
            eng.wait_ge(log_ready, k + 1)
            eng.tensor_tensor(z1[k], z1[k], dd[:, k, 1], ALU.add).then_inc(log1p_ready[on], 1)

        pair_tiles = [[(2 * (i % 2) + s, (i % PAIRS_PER_DIR) // 2) for s in range(2)] for i in range(PAIRS)]

        @block.sync
        def _(sp):
            def get(name, dst, src):
                sp.dma_start(dst, src).then_inc(load[name], 16)

            get("x", x[:, 0], d["x"].rearrange("(t p) c -> p t c", p=P))
            get("c32", c32[:], d["c32"])
            get("cols", cols[:], d["cols"])
            get("w_in", w_in, d["w_in"])
            get("alog", alog, d["alog"])
            get("w_xdt", w_xdt, d["w_xdt"])
            get("w_dt", w_dt, d["w_dt"])
            get("w_conv", w_conv, d["w_conv"])
            get("w_bc", w_bc[:], d["w_bc"])
            get("c16", c16[:], d["c16"])
            get("rows", rows[:], d["rows"].partition_broadcast(P))
            get("w1_0", w1[0][CH:P, :], d["w1_0"])
            def stack(k):
                if k == 1:
                    sp.wait_ge(lost_ready[1], DIRS - 1)
                    sp.wait_ge(log_ready, DIRS)
                if k >= 2:
                    sp.wait_ge(dspread, 2 * PAIRS_PER_DIR * (k - 1))
                    sp.wait_ge(uspread, PAIRS_PER_DIR * (k - 1))
                for part in range(PARTS):
                    if part == 0:
                        sp.wait_ge(delta_u_ready[k > 0], max(k, 1))
                    else:
                        sp.wait_ge(rest_ready, 2 * k + part)
                    if part == 2 and k:
                        sp.wait_ge(rest_pool, k)
                    src = dd[:, k] if part == 0 else res[:, k % 2, part - 1]
                    sp.dma_start(stk[32 * part:32 * part + 32, k % 2], src).then_inc(stacked[k % 2], 16)

            get("w_out", w_out[:], d["w_out"])
            for f in range(4):
                get(f"wr_{f}", wr[f][:], d[f"wr_{f}"])
            stack(0)
            get("w2_0", w2[0], d["w2_0"])
            get("rpb", bias[:], d["rpb"])
            stack(1)
            get("w_qk", w_qk[:], d["w_qk"])
            get("w_v", w_v[:], d["w_v"])
            get("w_pr", w_pr[:], d["w_pr"])
            stack(2)
            get("w_i1", w_i1[:], d["w_i1"])
            get("w_i2", w_i2[:], d["w_i2"])
            get("w_pt", w_pt[:], d["w_pt"])
            stack(3)
            sp.wait_ge(sum_done, PAIRS // 2)
            for f in (1, 2, 3):
                get(f"w1_{f}", w1[f][0:CH, :], d[f"w1_{f}"])
                get(f"w2_{f}", w2[f], d[f"w2_{f}"])
            sp.wait_ge(resid, 8)
            sp.dma_start(out.rearrange("(t p) c -> p t c", p=P), x[:, 8]).then_inc(stored, 16)
            sp.wait_ge(stored, 16)

        @block.gpsimd
        def _(pool):
            def rsqrt(n):
                w = 2 if n == 1 else 1
                pool.wait_ge(var_ready, n + 1)
                pool.tensor_tensor(rstd[:, 0:w], ve[:, 0:w], mhalf[:, 0:w], ALU.pow).then_inc(rstd_ready, 1)

            pool.memset(mhalf[:], -0.5).then_inc(pool_step, 1)
            pool.memset(idle[:], 0.0).then_inc(pool_step, 1)
            pool.memset(xp, 0.0).then_inc(zeroed, 1)
            pool.memset(da.rearrange("p b s (i l) -> p (b s i) l", l=SEQ)[:, :, 0:1], 0.0).then_inc(zeroed, 1)
            pool.memset(log_from[:], LOG_FROM).then_inc(zeroed, 1)
            pool.wait_ge(pool_step, 1)
            rsqrt(0)
            pool.memset(w1[0][0:CH, :], 0.0).then_inc(zeroed, 1)
            for k in range(1, DIRS):
                lost(pool, k)
            for k in range(1, DIRS):
                log1p(pool, k)
            for i in range(PAIRS):
                k = i // PAIRS_PER_DIR
                if i == 0:
                    pool.wait_ge(bc_sb, 2)
                elif i % PAIRS_PER_DIR == 0:
                    pool.wait_ge(bc_sb, 2 * k + 2)
                if i >= HC_SLOTS:
                    pool.wait_ge(sum_done, (i - HC_SLOTS) // 2 + 1)
                pool.wait_ge(scan_done, i + 1)
                if i == PAIRS - 1:
                    pool.tensor_tensor(hc[:, i % HC_SLOTS, 0], hs[:, i % 2, 0], bc[:, k, 1], ALU.mult).then_inc(hc_done, 1)
                    break
                c_all = bc[:, k, 1].unsqueeze(1).to_broadcast([P, 2, 2 * SEQ])
                pool.tensor_tensor(hc[:, i % HC_SLOTS], hs[:, i % 2], c_all, ALU.mult).then_inc(hc_done, 1)
                if k < DIRS - 1 and i % PAIRS_PER_DIR == 0:
                    delta_u(pool, k + 1)
                if k < DIRS - 1 and i % PAIRS_PER_DIR == 3:
                    pool.wait_ge(rest_ready, 2 * k + 3)
                    src = res[:, (k + 1) % 2, 0, 0]
                    pool.tensor_tensor(res[:, (k + 1) % 2, 1, 0], src, high(src), ALU.subtract).then_inc(rest_pool, 1)
            rsqrt(1)
            pool.wait_ge(load["rpb"], 16)
            pool.wait_ge(load["c32"], 16)
            for q in range(2):
                outside = window[:, q].unsqueeze(1).to_broadcast([P, HEADS, KEYS])
                pool.tensor_tensor(bias[:, q], bias[:, q], outside, ALU.add).then_inc(bias_ready, 1)
            pool.wait_ge(bias_ready, 2)
            pool.wait_ge(sum_done, PAIRS // 2)
            for f in (1, 2, 3):
                pool.memset(w1[f][CH:P, :], 0.0).then_inc(zeroed, 1)
            pool.wait_ge(zeroed, 7)
            pool.memset(view(22528, 2 * PAD * PAD), 0.0).then_inc(zeroed, 1)
            pool.memset(ih, 1.0).then_inc(zeroed, 1)
            pool.wait_ge(zeroed, 9)
            pool.memset(view(26248, 2048)[0:KEY_HALF], 0.0).then_inc(zeroed, 1)
            pool.wait_ge(zeroed, 10)
            for n in range(2, 8):
                rsqrt(n)
                if n == 2:
                    for h in range(HEADS):
                        pool.wait_ge(inverse, h + 1)
                        w = pr[:, TB * (h % 4):TB * (h % 4) + TB]
                        pool.tensor_tensor(w, w, spread_last(rrec[:, TB * h:TB * h + TB], KEYS), ALU.mult).then_inc(normed, 1)

        @block.scalar
        def _(act):
            def turned(n):
                act.wait_ge(xt_ps, n + 1)
                act.activation(xt[:], bank(0), ACT.Copy).then_inc(xt_sb, 1)

            act.preload_act_table(ACT.Silu)
            turned(0)
            act.wait_ge(z_ps, 1)
            act.activation(zs, bank(2), ACT.Silu).then_inc(zs_ready, 1)
            act.wait_ge(load["cols"], 16)
            act.wait_ge(conv_ps, 1)
            act.activation(u[:, 0], bank(3), ACT.Silu, bias=col("conv_b")).then_inc(u0_ready, 1)
            act.preload_act_table_set("natural_log_exp_and_others")
            act.wait_ge(zeroed, 3)
            act.activation(log_at[:], log_from[:], ACT.Ln, bias=1.0).then_inc(log_at_ready, 1)

            def bc_copy(q):
                act.wait_ge(bc_ps, q + 1)
                if q == 4:
                    act.wait_ge(conv_ps, 1)
                act.activation(bc[:, q // 2, q % 2], bank(7), ACT.Copy).then_inc(bc_sb, 1)

            def log_of(k):
                act.wait_ge(zmax_ready, k + 1)
                act.activation(dd[:, k, 1], zmax[:, k], ACT.Ln, bias=1.0).then_inc(log_ready, 1)

            for k in range(DIRS):
                act.wait_ge(dts_ps, k + 1)
                act.activation(dd[:, k, 1], bank(k), ACT.Abs, bias=col("dt_b", k)).then_inc(abs_ready, 1)
                act.wait_ge(abs_ready, k + 1)
                act.activation(z_[k], dd[:, k, 1], ACT.Exp, scale=-1.0).then_inc(z_ready, 1)
                act.activation(dd[:, k, 0], bank(k), ACT.Relu, bias=col("dt_b", k)).then_inc(relu_ready, 1)
                if k == 0:
                    log_of(0)
                if k == 1:
                    act.wait_ge(prep_ps, 1)
                    act.activation(aexp[:], bank(4)[:, 0:64], ACT.Exp).then_inc(aexp_ready, 1)
                    bc_copy(0)

            bc_copy(1)
            for k in range(1, DIRS):
                act.wait_ge(z_ready, k + 1)
                log_of(k)
            for i in range(PAIRS):
                k, ii = divmod(i, PAIRS_PER_DIR)
                if i == 0:
                    act.wait_ge(aneg_ready, 1)
                    act.wait_ge(zeroed, 2)
                if i >= 2:
                    act.wait_ge(scan_done, i - 1)
                for s, (g, m) in enumerate(pair_tiles[i]):
                    act.wait_ge(dspread, 2 * i + s + 1)
                    q = 16 * k + PER_GROUP * g + m
                    act.activation(da[:, i % 2, s].rearrange("p (b l) -> p b l", b=2)[:, :, 1:SEQ],
                                   bank(s).rearrange("p (b l) -> p b l", b=2)[:, :, 1:SEQ],
                                   ACT.Exp, scale=aneg[:, q:q + 1]).then_inc(exp_done, 1)
                if k < DIRS - 1 and ii in (3, 5):
                    bc_copy(2 * (k + 1) + (ii == 5))

            def experts(f, func):
                base, base_w = 16 * f, 4 * f
                if f == 2:
                    act.wait_ge(gap, f + 1)
                    act.activation(ex[:, 0:32], dl[:, 0:32], ACT.Exp).then_inc(gap_act, 1)
                for j in range(16):
                    act.wait_ge(hid_ps, base + j + 1)
                    if j >= RING:
                        act.wait_ge(y_ready, base_w + (j - RING) // 4 + 1)
                    p, q = divmod(j, 4)
                    blk = 4 * p + 2 * (q % 2) + q // 2
                    b1 = b1f[:, blk:blk + 1] if f == 0 else col(f"b1_{f}", blk)
                    act.activation(hid[:, j % RING], bank(1 + j % 4), func, bias=b1).then_inc(hid_ready, 1)
                    if j == 2 and f < 2:
                        act.wait_ge(gap, f + 1)
                        act.activation(th[:], m2[:], ACT.Tanh, scale=-0.5).then_inc(gap_act, 1)
                    if j % 4 == 3 and j > 3:
                        weight_copy(base_w, p - 1)
                weight_copy(base_w, 3)

            def weight_copy(base_w, p):
                act.wait_ge(wb_ps, base_w + p + 1)
                act.activation(wb[:, p], bank(7), ACT.Copy).then_inc(wb_sb, 1)

            act.wait_ge(bias_seen, 1)
            for e in range(8):
                o = w1[0][CH:P, 2 * e * P:(2 * e + 2) * P]
                last = act.activation(o, o, ACT.Copy, scale=col("ln_g", e)[CH:P])
            last.then_inc(w1_scaled, 1)
            act.preload_act_table(ACT.Gelu)
            turned(1)
            act.wait_ge(b1f_ready, 1)
            experts(0, ACT.Gelu)

            act.preload_act_table(ACT.Exp)
            turned(2)
            act.wait_ge(qk_ps, 1)
            act.activation(qf, bank(1), ACT.Identity, bias=col("q_b")).then_inc(q_sb, 1)
            act.wait_ge(q_sb, 1)
            for h in range(1, HEADS, 2):
                act.activation(qz[:, h], qf, ACT.Copy, scale=head_mask[:, h:h + 1]).then_inc(qz_ready[1], 1)
            for h in range(HEADS):
                act.wait_ge(negmax, h + 1)
                if h >= 4:
                    act.wait_ge(pt_ps, 2 * (h - 4) + 2)
                for unit in range(TB * h, TB * h + TB):
                    act.activation(pr[:, unit % 16], sm[:, unit % 16], ACT.Exp, bias=nmx[:, unit:unit + 1],
                                   accum_out=rsum[:, unit:unit + 1]).then_inc(prob, 1)
                if h >= 2:
                    probs_copy(act, h - 2, 0)
            probs_copy(act, HEADS - 2, 0)
            probs_copy(act, HEADS - 1, 0)
            act.wait_ge(pv, 8)
            act.activation(at[:, 1], bank(7), ACT.Copy).then_inc(at_sb, 1)
            act.preload_act_table(ACT.Gelu)
            turned(3)
            experts(1, ACT.Gelu)

            act.preload_act_table(ACT.Exp)
            turned(4)
            act.wait_ge(zeroed, 9)
            act.wait_ge(xt_sb, 5)
            act.activation(xpp[0:CH, :, 1:SIDE + 1, 1:SIDE + 1],
                           xt[0:CH].rearrange("p (b h w) -> p b h w", b=2, h=SIDE), ACT.Copy).then_inc(pad_ready, 1)
            act.wait_ge(ih_ps, 1)
            act.activation(ih[0:INV_HID], bank(1)[0:INV_HID], ACT.Identity,
                           bias=col("b_i1")[0:INV_HID]).then_inc(ih_sb, 1)
            turned(5)
            experts(2, ACT.Relu)

            act.preload_act_table(ACT.Silu)
            turned(6)
            turned(7)
            for j in range(16):
                act.wait_ge(hid_ps, 48 + j + 1)
                if j >= 2:
                    act.wait_ge(hid_ready, 48 + j - 1)
                act.activation(gate[:, j % 2], bank(1 + 2 * (j % 2)), ACT.Silu).then_inc(gate_ready, 1)
                if j == 3:
                    act.wait_ge(gap, 4)
                    act.activation(th[:], m2[:], ACT.Tanh, scale=-0.5).then_inc(gap_act, 1)
                if j % 2 == 1 and j >= 5:
                    weight_copy(12, (j - 5) // 2)
            weight_copy(12, 6)
            weight_copy(12, 7)

        @block.tensor
        def _(pe):
            def keep_warm(n):
                for _ in range(n):
                    pe.matmul(bank(5), idle[:, 0:P], idle[:], start=True, stop=True)

            def turn(n):
                if n:
                    keep_warm(WARM_NORM)
                pe.wait_ge(ln_ready, n + 1)
                if n:
                    pe.wait_ge(xt_sb, n)
                for t in range(TB):
                    last = pe.transpose(bank(0)[:, t * P:(t + 1) * P], xn[:, t], ident)
                last.then_inc(xt_ps, 1)

            def got(*names):
                for n in names:
                    pe.wait_ge(load[n], 16)

            pe.wait_ge(pool_step, 2)
            keep_warm(12)
            got("c32", "alog", "w_xdt", "w_dt")
            pe.transpose(bank(4)[:, 0:64], alog, ident[0:64, 0:64]).then_inc(prep_ps, 1)
            for k in range(DIRS):
                last = pe.matmul(bank(5)[:, k * P:(k + 1) * P], w_xdt[:, k], w_dt[:, k], start=True, stop=True)
            last.then_inc(fdt_ps, 1)
            turn(0)
            got("w_in")
            pe.wait_ge(xt_sb, 1)
            pe.matmul(bank(1), w_in[:, 0:INNER], xt[:], start=True, stop=True).then_inc(xi_ps, 1)
            pe.matmul(bank(2), w_in[:, INNER:], xt[:], start=True, stop=True).then_inc(z_ps, 1)
            got("w_conv")
            pe.wait_ge(xp_ready, 1)
            for s in range(TAPS):
                dy, dx = divmod(s, 3)
                last = pe.matmul(bank(3), w_conv[:, s], xp[:, :, dy:dy + SIDE, dx:dx + SIDE],
                                 start=(s == 0), stop=(s == TAPS - 1))
            last.then_inc(conv_ps, 1)
            pe.wait_ge(u0_ready, 1)
            pe.wait_ge(fdt_sb, 1)

            def dts(k):
                pe.matmul(bank(k), w_fdt[:, k], u[:, 0 if k < 2 else 2], start=True, stop=True).then_inc(dts_ps, 1)

            def bc_mm(q):
                if q:
                    pe.wait_ge(bc_sb, q)
                pe.matmul(bank(7), w_bc[:, q // 2, q % 2], u[:, 0 if q < 4 else 2], start=True, stop=True).then_inc(bc_ps, 1)

            dts(0)
            dts(1)
            pe.matmul(bank(5), anti, u[:, 0], start=True, stop=True).then_inc(rev_ps, 1)
            got("w_bc")
            bc_mm(0)
            pe.wait_ge(u_ready, 1)
            pe.wait_ge(zs_ready, 1)
            dts(2)
            dts(3)
            pe.wait_ge(diag_ready, 1)
            for a in range(2):
                pe.matmul(bank(6), d_mix[:, a], u[:, 2 * a], start=(a == 0), stop=False, skip_group_check=True)
            bc_mm(1)

            def ln_b_through_w1(first):
                for blk in range(first, first + 8):
                    last = pe.matmul(bank(7)[:, blk:blk + 1], w1[0][:, blk * P:(blk + 1) * P], col("ln_b", blk // 2),
                                     start=True, stop=True)
                if first == 8:
                    last.then_inc(bias_seen, 1)

            def spread_pair(i):
                k = i // PAIRS_PER_DIR
                if i % PAIRS_PER_DIR == 0:
                    pe.wait_ge(stacked[k % 2], 16 * PARTS * (k // 2 + 1))
                if i >= 2:
                    pe.wait_ge(mul_done, i - 1)
                for s, (g, m) in enumerate(pair_tiles[i]):
                    last = pe.matmul(bank(2 + 2 * (i % 2) + s), spread[0:96, m], high(stk[0:96, k % 2, g, 1]),
                                     start=True, stop=True)
                last.then_inc(uspread, 1)
                for s, (g, m) in enumerate(pair_tiles[i]):
                    if i:
                        pe.wait_ge(exp_done, 2 * (i - 1) + s + 1)
                    pe.matmul(bank(s), spread[0:96, m], high(stk[0:96, k % 2, g, 0]),
                              start=True, stop=True).then_inc(dspread, 1)

            def sum_states(q):
                pe.wait_ge(hc_done, 2 * q + 2)
                if q == PAIRS // 2 - 1:
                    pe.wait_ge(hc_last, 1)
                for i in (2 * q, 2 * q + 1):
                    for s, (g, m) in enumerate(pair_tiles[i]):
                        last = pe.matmul(ps[32 * g:32 * g + 32, 6, :], state_sum[:, m], hc[:, i % HC_SLOTS, s],
                                         start=False, stop=(q == PAIRS // 2 - 1), skip_group_check=True)
                last.then_inc(sum_done, 1)

            got("c16")
            pe.wait_ge(relu_ready, DIRS)
            pe.wait_ge(u_ready, 3)
            pe.wait_ge(aexp_ready, 1)
            spread_pair(0)
            spread_pair(1)
            for i in range(PAIRS):
                k, ii = divmod(i, PAIRS_PER_DIR)
                if i + 2 < PAIRS:
                    spread_pair(i + 2)
                if i >= 3 and i % 2:
                    sum_states((i - 3) // 2)
                if i == PAIRS - 2:
                    got("w1_0", "cols")
                    pe.wait_ge(zeroed, 4)
                    pe.wait_ge(bc_sb, 2 * DIRS)
                if i >= PAIRS - 2:
                    ln_b_through_w1(8 * (i - PAIRS + 2))
                if k < DIRS - 1 and ii in (2, 4):
                    bc_mm(2 * (k + 1) + (ii == 4))
            sum_states(PAIRS // 2 - 1)
            pe.wait_ge(gated_ready, 1)
            got("w_out")
            for t in range(TB):
                last = pe.matmul(bank(1)[:, t * CH:(t + 1) * CH], gated[:, t * P:(t + 1) * P], w_out[:], start=True, stop=True)
            last.then_inc(proj_ps, 1)

            def experts(f):
                n, e_n = LN_OF_FFN[f], E_OF[f]
                pairs = e_n // 2
                base, base_w = 16 * f, 4 * f
                got(f"wr_{f}", f"w1_{f}", f"w2_{f}")
                turn(n)
                pe.wait_ge(xt_sb, n + 1)
                if f == 0:
                    pe.wait_ge(b1f_ready, 1)
                if f == 1:
                    pe.wait_ge(zeroed, 9)
                for t in range(TB):
                    last = pe.matmul(bank(7)[:, t * e_n:(t + 1) * e_n], xt[:, t * P:(t + 1) * P], wr[f][:], start=True, stop=True)
                last.then_inc(logits, 1)
                if f == 0:
                    pe.wait_ge(w1_scaled, 1)
                per = 16 // pairs

                def hidden(p):
                    for q in range(per):
                        j = per * p + q
                        if f < 3:
                            if j >= 4:
                                pe.wait_ge(hid_ready, base + j - 3)
                            blk = 4 * p + 2 * (q % 2) + q // 2
                            pe.matmul(bank(1 + j % 4), w1[f][:, blk * P:(blk + 1) * P], xt[:], start=True, stop=True)\
                              .then_inc(hid_ps, 1)
                        else:
                            if j >= 2:
                                pe.wait_ge(hid_ready, base + j - 1)
                            pe.matmul(bank(1 + 2 * (j % 2)), w1[3][:, j * P:(j + 1) * P], xt[:], start=True, stop=True)
                            pe.matmul(bank(2 + 2 * (j % 2)), w1[3][:, (16 + j) * P:(17 + j) * P], xt[:], start=True, stop=True)\
                              .then_inc(hid_ps, 1)

                def down(p):
                    if p >= 2:
                        pe.wait_ge(comb, base_w + p - 1)
                    for q in range(per):
                        j = per * p + q
                        blk = 4 * p + 2 * (q % 2) + q // 2 if f < 3 else j
                        pe.wait_ge(hid_ready, base + j + 1)
                        o = CH * (q % 2)
                        last = pe.matmul(ps[o:o + CH, 5 + p % 2, :], w2[f][:, blk], hid[:, j % RING],
                                         start=(q < 2), stop=(q >= per - 2), skip_group_check=True)
                    last.then_inc(y_ready, 1)

                def weights(p):
                    if p == 0:
                        pe.wait_ge(w_ready, f + 1)
                        for t in range(TB):
                            last = pe.transpose(bank(7).bitcast(BF16)[0:PARTS * e_n, t * P:(t + 1) * P],
                                                wp[:, t, 0:PARTS * e_n], ident16)
                        last.then_inc(wt_ps, 1)
                        pe.wait_ge(wt_sb, f + 1)
                    elif p:
                        pe.wait_ge(wb_sb, base_w + p)
                    pe.matmul(bank(7), spread_w[e_n][0:PARTS * e_n, p], wt[0:PARTS * e_n, :], start=True, stop=True).then_inc(wb_ps, 1)

                hidden(0)
                if f == 2:
                    pe.wait_ge(oh_ready, 1)
                    for t in range(TB):
                        for t2 in range(t + 1):
                            last = pe.matmul(bank(0)[:, t * 8:t * 8 + 8], tri16 if t2 == t else ones16,
                                             oh16[:, t2 * 8:t2 * 8 + 8], start=(t2 == 0), stop=(t2 == t))
                    last.then_inc(count_ps, 1)
                lag = 0 if f < 3 else 1
                for p in range(1, pairs):
                    hidden(p)
                    if p - 1 - lag >= 0:
                        down(p - 1 - lag)
                        weights(p - 1 - lag)
                for p in range(pairs - 1 - lag, pairs):
                    down(p)
                    weights(p)
                pe.wait_ge(acc_ready, f + 1)
                for t in range(TB):
                    pe.matmul(bank(0)[:, t * CH:(t + 1) * CH], acc[:, t * P:(t + 1) * P], stack_i,
                              start=(t == 0), stop=False, skip_group_check=True)
                pe.wait_ge(comb, base_w + pairs)
                for t in range(TB):
                    last = pe.matmul(bank(0)[:, t * CH:(t + 1) * CH], tmp[:, (pairs - 1) % 2, t * P:(t + 1) * P], stack_i,
                                     start=False, stop=(t == TB - 1), skip_group_check=True)
                last.then_inc(out_ps, 1)

            experts(0)

            got("w_qk", "w_v", "w_pr")
            turn(2)
            pe.wait_ge(xt_sb, 3)
            for a in range(2):
                pe.matmul(bank(1 + a), w_qk[:, a], xt[:], start=True, stop=True).then_inc(qk_ps, 1)
            for t in range(TB):
                for kb in range(2):
                    k0 = (t // 2) * SEQ + KEY_ROW0[t % 2] * SIDE + kb * KEY_HALF
                    last = pe.matmul(bank(5)[0:KEY_HALF, (2 * t + kb) * CH:(2 * t + kb + 1) * CH],
                                     xt[:, k0:k0 + KEY_HALF], w_v[:], start=True, stop=True)
            last.then_inc(v_ps, 1)

            def scores(h):
                pe.wait_ge(qz_ready[h % 2], h // 2 + 1)
                if h >= 2:
                    pe.wait_ge(masked, TB * (h - 2) + TB)
                for t in range(TB):
                    unit = TB * h + t
                    k0 = (t // 2) * SEQ + KEY_ROW0[t % 2] * SIDE
                    o = 256 * (unit % 2)
                    last = pe.matmul(bank(1 + (unit // 2) % 4)[:, o:o + KEYS], qz[:, h, t * P:(t + 1) * P],
                                     kf[:, k0:k0 + KEYS], start=True, stop=True)
                    if t % 2:
                        last.then_inc(score, 1)

            def probs_turn(h):
                pe.wait_ge(normed, h + 1)
                for g in range(2):
                    if h:
                        pe.wait_ge(pt_sb[g], h)
                    for w in range(2):
                        for kb in range(2):
                            o = (2 * w + kb) * P
                            last = pe.transpose(bank(5 + g)[0:KEY_HALF, o:o + P],
                                                pr[:, (TB * h + 2 * g + w) % 16, kb * KEY_HALF:(kb + 1) * KEY_HALF], ident)
                    last.then_inc(pt_ps, 1)

            def values(h):
                o = 32 * (h % 4)
                for g in range(2):
                    pe.wait_ge(pt_sb[g], h + 1)
                    for w in range(2):
                        t = 2 * g + w
                        for kb in range(2):
                            last = pe.matmul(ps[o:o + 32, 7 * (h // 4), t * P:(t + 1) * P],
                                             vz[:, 2 * t + kb, h], pt[:, 2 * (h % 2) + g, (2 * w + kb) * P:(2 * w + kb + 1) * P],
                                             start=(kb == 0), stop=(kb == 1))
                last.then_inc(pv, 1)

            pe.wait_ge(q_sb, 1)
            pe.wait_ge(k_sb, 1)
            scores(0)
            scores(1)
            pe.wait_ge(v_sb, 1)
            for h in range(HEADS):
                if h + 2 < HEADS:
                    scores(h + 2)
                probs_turn(h)
                if h:
                    values(h - 1)
            values(HEADS - 1)
            pe.wait_ge(at_sb, 2)
            for t in range(TB):
                for a in range(2):
                    last = pe.matmul(bank(1)[:, t * CH:(t + 1) * CH], at[:, a, t * P:(t + 1) * P], w_pr[:, a],
                                     start=(a == 0), stop=(a == 1))
            last.then_inc(apr_ps, 1)

            experts(1)

            got("w_i1", "w_i2")
            turn(4)
            pe.wait_ge(xt_sb, 5)
            pe.matmul(bank(1)[0:INV_HID], w_i1[:], xt[:], start=True, stop=True).then_inc(ih_ps, 1)
            pe.wait_ge(ih_sb, 1)
            for r in range(5):
                m = P if r < 4 else CH
                pe.matmul(bank(2 + r)[0:m], w_i2[:, r, 0:m], ih, start=True, stop=True).then_inc(wq_ps, 1)
            pe.wait_ge(prod_ready, 5)
            for t in range(TB):
                for r in range(5):
                    m = P if r < 4 else CH
                    last = pe.matmul(bank(7)[:, t * CH:(t + 1) * CH], prod[0:m, r, t * P:(t + 1) * P], tap_sum[0:m, r],
                                     start=(r == 0), stop=(r == 4))
            last.then_inc(inv_ps, 1)

            experts(2)

            got("w_pt")
            turn(6)
            pe.wait_ge(xt_sb, 7)
            for t in range(TB):
                last = pe.matmul(bank(1)[:, t * CH:(t + 1) * CH], xt[:, t * P:(t + 1) * P], w_pt[:], start=True, stop=True)
            last.then_inc(proj_ps, 1)
            experts(3)

        @block.vector
        def _(dve):
            steps = [0]

            def mark(ins):
                steps[0] += 1
                ins.then_inc(dve_step, 1)

            def settle():
                dve.wait_ge(dve_step, steps[0])

            def link(ins):
                mark(ins)
                settle()

            def norm(n):
                src = x[:, n]
                if n == 0:
                    dve.wait_ge(load["x"], 16)
                else:
                    dve.wait_ge(resid, n)
                for t in range(TB):
                    mark(dve.bn_stats(stats[:, t], src[:, t]))
                settle()
                for t in range(TB):
                    mark(dve.bn_aggr(mv[:, t], stats[:, t]))
                settle()
                if n == 1:
                    link(dve.tensor_scalar(ve[:, 0], mv[:, :, 1], EPS[n], None, ALU.add))
                    link(dve.reciprocal(sq[:], ve[:, 0]))
                    link(dve.tensor_tensor(sq[:], sq[:], mv[:, :, 1], ALU.mult))
                    dve.tensor_scalar(ve[:, 1], sq[:], EPS[1], None, ALU.add).then_inc(var_ready, 1)
                else:
                    dve.tensor_scalar(ve[:, 0], mv[:, :, 1], EPS[n], None, ALU.add).then_inc(var_ready, 1)
                dve.wait_ge(rstd_ready, n + 1)
                for t in range(TB):
                    half = CH if n == 1 else HALVES * CH
                    o = xn[:, t, 0:half].rearrange("p (w c) -> p w c", c=CH)
                    i = src[:, t].unsqueeze(1).to_broadcast([P, half // CH, CH])
                    last = dve.tensor_scalar(o, i, mv[:, t, 0:1], rstd[:, 0, t:t + 1], ALU.subtract, ALU.mult)
                    if n == 1:
                        mark(last)
                if n == 1:
                    settle()
                    for t in range(TB):
                        last = dve.tensor_scalar(xn[:, t, CH:P], xn[:, t, 0:CH], rstd[:, 1, t:t + 1], None, ALU.mult)
                last.then_inc(ln_ready, 1)

            norm(0)
            dve.wait_ge(zeroed, 1)
            dve.wait_ge(xi_ps, 1)
            dve.tensor_copy(xp[:, :, 1:SIDE + 1, 1:SIDE + 1],
                            bank(1).rearrange("p (b h w) -> p b h w", b=2, h=SIDE)).then_inc(xp_ready, 1)
            dve.wait_ge(fdt_ps, 1)
            dve.tensor_copy(w_fdt.rearrange("p k c -> p (k c)"), bank(5)).then_inc(fdt_sb, 1)
            dve.wait_ge(load["cols"], 16)
            dve.wait_ge(load["c32"], 16)
            for a in range(2):
                mark(dve.tensor_scalar(d_mix[:, a], to_scan, col("ds", 2 * a), None, ALU.mult))
            settle()
            for a in range(2):
                last = dve.scalar_tensor_tensor(out=d_mix[:, a], in0=anti_to_scan, scalar=col("ds", 2 * a + 1),
                                                in1=d_mix[:, a], op0=ALU.mult, op1=ALU.add)
            last.then_inc(diag_ready, 1)
            dve.wait_ge(u0_ready, 1)

            def columns_first(v):
                return v.rearrange("p (b h w) -> p b w h", b=2, h=SIDE)

            def grid(v):
                return v.rearrange("p (b h w) -> p b h w", b=2, h=SIDE)

            dve.tensor_copy(grid(u[:, 2]), columns_first(u[:, 0])).then_inc(u_ready, 1)
            def part(k, r):
                if k >= 2 and r == 0:
                    dve.wait_ge(stacked[k % 2], 16 * PARTS)
                if r == 0:
                    dve.wait_ge(delta_u_ready[k > 0], max(k, 1))
                else:
                    dve.wait_ge(rest_ready, 2 * k + 1)
                halves = slice(0, 2) if r == 0 or k == 0 else slice(1, 2)
                src = (dd[:, k] if r == 0 else res[:, k % 2, 0])[:, halves].rearrange("p v l -> p (v l)")
                dve.tensor_tensor(res[:, k % 2, r, halves].rearrange("p v l -> p (v l)"), src, high(src), ALU.subtract)\
                   .then_inc(rest_ready, 1)

            def bounded(k):
                dve.wait_ge(z_ready, k + 1)
                dve.tensor_scalar(zmax[:, k], z_[k], LOG_FROM, None, ALU.max).then_inc(zmax_ready, 1)
                mark(dve.tensor_scalar(zmin[k], z_[k], LOG_FROM, None, ALU.min))
                dve.wait_ge(zmax_ready, k + 1)
                dve.tensor_scalar(z1[k], zmax[:, k], 1.0, -1.0, ALU.add, ALU.add).then_inc(z1_ready, 1)

            def small_log(k):
                if k == 0:
                    settle()
                link(dve.scalar_tensor_tensor(out=z_[k], in0=zmin[k], scalar=LOG_C1, in1=zmin[k],
                                              op0=ALU.add, op1=ALU.mult))
                link(dve.scalar_tensor_tensor(out=z_[k], in0=z_[k], scalar=LOG_C0, in1=zmin[k],
                                              op0=ALU.add, op1=ALU.mult))

            def delta(k):
                dve.wait_ge(log1p_ready[k > 0], max(k, 1))
                dve.wait_ge(relu_ready, k + 1)
                dve.wait_ge(log_at_ready, 1)
                link(dve.scalar_tensor_tensor(out=z1[k], in0=z1[k], scalar=log_at[:], in1=dd[:, k, 0],
                                              op0=ALU.subtract, op1=ALU.add))
                dve.scalar_tensor_tensor(out=dd[:, k, 0], in0=z_[k], scalar=LOG_C2, in1=z1[k],
                                         op0=ALU.mult, op1=ALU.add).then_inc(delta_ready, 1)

            bounded(0)
            small_log(0)
            lost(dve, 0)
            log1p(dve, 0)
            delta(0)
            delta_u(dve, 0)
            part(0, 0)
            part(0, 1)
            for k in range(1, DIRS):
                bounded(k)
            dve.wait_ge(aexp_ready, 1)
            dve.tensor_scalar(aneg[:], aexp[:], -1.0, None, ALU.mult).then_inc(aneg_ready, 1)
            dve.wait_ge(rev_ps, 1)
            dve.tensor_copy(u[:, 1], bank(5)).then_inc(u_ready, 1)
            dve.tensor_copy(grid(u[:, 3]), columns_first(bank(5))).then_inc(u_ready, 1)

            def times_b(i):
                dve.wait_ge(uspread, i + 1)
                if i % PAIRS_PER_DIR == 0:
                    dve.wait_ge(bc_sb, 2 * (i // PAIRS_PER_DIR) + 1)
                b_all = bc[:, i // PAIRS_PER_DIR, 0].unsqueeze(1).to_broadcast([P, 2, 2 * SEQ])
                if i >= 2:
                    dve.wait_ge(scan_done, i - 1)
                dve.tensor_tensor(ub[:, i % 2], ps[:, 2 + 2 * (i % 2):4 + 2 * (i % 2), :], b_all, ALU.mult).then_inc(mul_done, 1)

            times_b(0)
            for i in range(PAIRS):
                k, ii = divmod(i, PAIRS_PER_DIR)
                if i + 1 < PAIRS:
                    times_b(i + 1)
                dve.wait_ge(mul_done, i + 1)
                dve.wait_ge(exp_done, 2 * i + 2)
                if i >= 2:
                    dve.wait_ge(hc_done, i - 1)
                dve.tensor_tensor_scan(hs[:, i % 2].rearrange("p s l -> p (s l)"),
                                       da[:, i % 2].rearrange("p s l -> p (s l)"),
                                       ub[:, i % 2].rearrange("p s l -> p (s l)"),
                                       0.0, ALU.mult, ALU.add).then_inc(scan_done, 1)
                if k < DIRS - 1:
                    if i == 0:
                        small_log(1)
                        delta(1)
                    if ii == 2:
                        part(k + 1, 0)
                    if ii == 3:
                        part(k + 1, 1)
                    if k == 0 and ii in (4, 6):
                        small_log(ii // 2)
                    if k == 0 and ii in (5, 7):
                        delta(ii // 2)
            dve.wait_ge(scan_done, PAIRS)
            dve.wait_ge(sum_done, (PAIRS - 1 - HC_SLOTS) // 2 + 1)
            dve.tensor_tensor(hc[:, (PAIRS - 1) % HC_SLOTS, 1], hs[:, (PAIRS - 1) % 2, 1], bc[:, DIRS - 1, 1], ALU.mult)\
               .then_inc(hc_last, 1)
            dve.wait_ge(bias_seen, 1)
            dve.tensor_tensor(b1f[:], bank(7)[:, 0:16], colv("b1_0"), ALU.add).then_inc(b1f_ready, 1)
            dve.wait_ge(sum_done, PAIRS // 2)
            dve.wait_ge(zs_ready, 1)
            dve.tensor_tensor(gated, bank(6), zs, ALU.mult).then_inc(gated_ready, 1)

            def add(n, src, sem_, count):
                dve.wait_ge(sem_, count)
                dve.tensor_tensor(x[:, n + 1], x[:, n], src.rearrange("p (t c) -> p t c", t=TB), ALU.add)\
                   .then_inc(resid, 1)

            add(0, bank(1)[:, 0:TB * CH], proj_ps, 1)

            def router(f):
                e_n = E_OF[f]
                n = TB * e_n
                dve.wait_ge(load["rows"], 16)
                dve.wait_ge(logits, f + 1)
                link(dve.tensor_tensor(lg[:, 0:n], bank(7)[:, 0:n], row(f"br_{f}"), ALU.add))
                link(dve.tensor_reduce(m1[:], tiles(lg[:, 0:n]), X_AXIS, ALU.max))
                link(dve.tensor_tensor(tiles(dl[:, 0:n]), tiles(lg[:, 0:n]), spread_last(m1[:], e_n), ALU.subtract))
                link(dve.scalar_tensor_tensor(out=c1[:, 0:n], in0=dl[:, 0:n], scalar=0.0, in1=rank_of[e_n],
                                              op0=ALU.is_ge, op1=ALU.mult))
                link(dve.tensor_reduce(i1[:], tiles(c1[:, 0:n]), X_AXIS, ALU.max))
                if f == 2:
                    dve.tensor_tensor(tiles(oh16[:]), tiles(c1[:, 0:n]), spread_last(i1[:], e_n), ALU.is_equal)\
                       .then_inc(oh_ready, 1)
                link(dve.tensor_tensor(tiles(oh1[:, 0:n]), tiles(c1[:, 0:n]), spread_last(i1[:], e_n), ALU.is_equal))
                if f == 2:
                    dve.sem_inc(gap, 1)
                    dve.wait_ge(gap_act, 3)
                    link(dve.tensor_reduce(m2[:], tiles(ex[:, 0:n]), X_AXIS, ALU.add))
                    link(dve.reciprocal(i2[:], m2[:]))
                    dve.wait_ge(count_ps, 1)
                    link(dve.scalar_tensor_tensor(out=c2[:, 0:n], in0=bank(0)[:, 0:n], scalar=float(CAPACITY), in1=oh1[:, 0:n],
                                                  op0=ALU.is_le, op1=ALU.mult))
                    link(dve.tensor_tensor(tiles(ww[:, 0:n]), tiles(c2[:, 0:n]), spread_last(i2[:], e_n), ALU.mult))
                else:
                    link(dve.scalar_tensor_tensor(out=d2[:, 0:n], in0=oh1[:, 0:n], scalar=-BIG, in1=dl[:, 0:n],
                                                  op0=ALU.mult, op1=ALU.add))
                    dve.tensor_reduce(m2[:], tiles(d2[:, 0:n]), X_AXIS, ALU.max).then_inc(gap, 1)
                    dve.wait_ge(gap, f + 1)
                    link(dve.tensor_tensor(tiles(g2[:, 0:n]), tiles(d2[:, 0:n]), spread_last(m2[:], e_n), ALU.is_ge))
                    link(dve.tensor_tensor(c2[:, 0:n], g2[:, 0:n], rank_of[e_n], ALU.mult))
                    link(dve.tensor_reduce(i2[:], tiles(c2[:, 0:n]), X_AXIS, ALU.max))
                    link(dve.tensor_tensor(tiles(oh2[:, 0:n]), tiles(c2[:, 0:n]), spread_last(i2[:], e_n), ALU.is_equal))
                    dve.wait_ge(gap_act, f + 1)
                    mark(dve.tensor_scalar(wa[:], th[:], 0.5, 0.5, ALU.mult, ALU.add))
                    link(dve.tensor_scalar(wc[:], th[:], -0.5, 0.5, ALU.mult, ALU.add))
                    mark(dve.tensor_tensor(tiles(wr1[:, 0:n]), tiles(oh1[:, 0:n]), spread_last(wa[:], e_n), ALU.mult))
                    link(dve.tensor_tensor(tiles(wr2[:, 0:n]), tiles(oh2[:, 0:n]), spread_last(wc[:], e_n), ALU.mult))
                    link(dve.tensor_tensor(ww[:, 0:n], wr1[:, 0:n], wr2[:, 0:n], ALU.add))
                w3 = tiles(ww[:, 0:n])
                r3 = tiles(wr1[:, 0:n])
                link(dve.tensor_copy(wp[:, :, 0:e_n], w3))
                link(dve.tensor_tensor(r3, w3, wp[:, :, 0:e_n], ALU.subtract))
                link(dve.tensor_copy(wp[:, :, e_n:2 * e_n], r3))
                dve.tensor_tensor(wp[:, :, 2 * e_n:3 * e_n], r3, wp[:, :, e_n:2 * e_n], ALU.subtract).then_inc(w_ready, 1)
                dve.wait_ge(wt_ps, f + 1)
                dve.tensor_copy(wt[0:PARTS * e_n, :], bank(7).bitcast(BF16)[0:PARTS * e_n, 0:TOKENS]).then_inc(wt_sb, 1)

            def combine(f, p):
                base_w, pairs = 4 * f, E_OF[f] // 2
                dve.wait_ge(wb_sb, base_w + p + 1)
                dve.wait_ge(y_ready, base_w + p + 1)
                o = acc if p == 0 else tmp[:, p % 2]
                b2 = col(f"b2_{f}", p) if f < 3 else 0.0
                dve.scalar_tensor_tensor(out=o, in0=bank(5 + p % 2), scalar=b2, in1=wb[:, p],
                                         op0=ALU.add, op1=ALU.mult).then_inc(comb, 1)
                if 0 < p < pairs - 1:
                    dve.wait_ge(comb, base_w + p + 1)
                    last = dve.tensor_tensor(acc, acc, tmp[:, p % 2], ALU.add)
                    if p == pairs - 2:
                        last.then_inc(acc_ready, 1)
                    else:
                        link(last)

            def finish(f):
                n = LN_OF_FFN[f]
                if f < 2 or f == 3:
                    add(n, bank(0)[:, 0:TB * CH], out_ps, f + 1)
                    return
                dve.wait_ge(out_ps, f + 1)
                y = bank(0)[:, 0:TB * CH]
                mark(dve.tensor_scalar(nan_a, y, FLT_MAX, 1.0e4, ALU.is_gt, ALU.mult))
                mark(dve.tensor_scalar(nan_b, y, -FLT_MAX, -1.0e4, ALU.is_lt, ALU.mult))
                link(dve.tensor_scalar(finite, y, 0.0, 0.0, ALU.mult, ALU.is_equal))
                link(dve.tensor_tensor(nan_a, nan_a, nan_b, ALU.add))
                link(dve.copy_predicated(nan_a, finite, y))
                dve.tensor_tensor(x[:, n + 1], x[:, n], nan_a.rearrange("p (t c) -> p t c", t=TB), ALU.add).then_inc(resid, 1)

            norm(1)
            router(0)
            for p in range(4):
                combine(0, p)
            finish(0)

            norm(2)
            dve.wait_ge(qk_ps, 2)
            dve.tensor_scalar(kf, bank(2), col("k_b"), None, ALU.add).then_inc(k_sb, 1)
            dve.wait_ge(q_sb, 1)
            for h in range(0, HEADS, 2):
                dve.tensor_scalar(qz[:, h], qf, head_mask[:, h:h + 1], None, ALU.mult).then_inc(qz_ready[0], 1)
            dve.wait_ge(v_ps, 1)
            v_b = row("v_b")[0:KEY_HALF].unsqueeze(1).to_broadcast([KEY_HALF, 8, CH])
            dve.wait_ge(zeroed, 10)
            dve.tensor_tensor(vz[:, :, :, 0:HEAD_CH], bank(5)[0:KEY_HALF].rearrange("p (u h c) -> p u h c", u=8, h=HEADS),
                              v_b.rearrange("p u (h c) -> p u h c", h=HEADS), ALU.add).then_inc(v_sb, 1)
            pr_b = row("pr_b").unsqueeze(1).to_broadcast([P, TB, CH])
            xb = nan_a.rearrange("p (t c) -> p t c", t=TB)
            mark(dve.tensor_tensor(xb, x[:, 2], pr_b, ALU.add))
            dve.wait_ge(bias_ready, 2)

            def inverse_sums(h):
                dve.wait_ge(prob, TB * h + TB)
                dve.reciprocal(rrec[:, TB * h:TB * h + TB], rsum[:, TB * h:TB * h + TB]).then_inc(inverse, 1)

            for h in range(HEADS):
                for t in range(TB):
                    unit = TB * h + t
                    dve.wait_ge(score, unit // 2 + 1)
                    if unit >= 16:
                        dve.wait_ge(prob, unit - 15)
                    o = 256 * (unit % 2)
                    dve.tensor_tensor_reduce(sm[:, unit % 16], bank(1 + (unit // 2) % 4)[:, o:o + KEYS], bias[:, t % 2, h],
                                             1.0, -3.0e38, ALU.add, ALU.max, mx[:, unit:unit + 1]).then_inc(masked, 1)
                dve.wait_ge(masked, TB * h + TB)
                dve.tensor_scalar(nmx[:, TB * h:TB * h + TB], mx[:, TB * h:TB * h + TB], -1.0, None, ALU.mult)\
                   .then_inc(negmax, 1)
                if h >= 1:
                    inverse_sums(h - 1)
                if h >= 2:
                    probs_copy(dve, h - 2, 1)
            inverse_sums(HEADS - 1)
            dve.wait_ge(pv, 4)
            dve.tensor_copy(at[:, 0], bank(0)).then_inc(at_sb, 1)
            probs_copy(dve, HEADS - 2, 1)
            probs_copy(dve, HEADS - 1, 1)
            dve.wait_ge(apr_ps, 1)
            settle()
            dve.tensor_tensor(x[:, 3], xb, bank(1)[:, 0:256].rearrange("p (t c) -> p t c", t=TB), ALU.add).then_inc(resid, 1)

            norm(3)
            router(1)
            for p in range(4):
                combine(1, p)
            finish(1)

            norm(4)
            dve.wait_ge(xt_sb, 5)
            dve.wait_ge(zeroed, 9)
            dve.tensor_copy(xpp[CH:P, :, 1:SIDE + 1, 0:SIDE],
                            xt[CH:P].rearrange("p (b h w) -> p b h w", b=2, h=SIDE)).then_inc(pad_ready, 1)
            dve.wait_ge(pad_ready, 2)
            for r, taps in enumerate(TAP_BLOCKS):
                dve.wait_ge(wq_ps, r + 1)
                whole = len(taps) == 2 and taps[1] == taps[0] + 1
                for half, tap in enumerate(taps[:1] if whole else taps):
                    dy, dx = divmod(tap, 3)
                    rows_ = slice(0, P) if whole else slice(CH * half, CH * half + CH)
                    dx -= half
                    last = dve.tensor_tensor(grid(prod[rows_, r]), grid(bank(2 + r)[rows_]),
                                             xpp[rows_, :, dy:dy + SIDE, dx:dx + SIDE], ALU.mult)
                last.then_inc(prod_ready, 1)
            add(4, bank(7)[:, 0:256], inv_ps, 1)

            norm(5)
            router(2)
            for p in range(4):
                combine(2, p)
            finish(2)

            norm(6)
            add(6, bank(1)[:, 0:256], proj_ps, 2)
            norm(7)

            def gate_mul(j):
                dve.wait_ge(gate_ready, j + 1)
                if j >= RING:
                    dve.wait_ge(y_ready, 12 + (j - RING) // 2 + 1)
                dve.tensor_tensor(hid[:, j % RING], gate[:, j % 2], bank(2 + 2 * (j % 2)), ALU.mult).then_inc(hid_ready, 1)

            for j in range(4):
                gate_mul(j)
            router(3)
            for p in range(8):
                if p < 6:
                    gate_mul(2 * p + 4)
                    gate_mul(2 * p + 5)
                combine(3, p)
            finish(3)


def _places(sizes):
    at, o = {}, 0
    for n, s in sizes:
        at[n] = (o, s)
        o += s
    return at, o


C32_AT, C32_COLS = _places([("ident", P), ("anti", P), ("to_scan", P), ("anti_to_scan", P), ("stack_i", CH), ("state_sum", PER_GROUP * 32),
                            ("tap_sum", 5 * CH), ("window", 2 * KEYS), ("head_mask", HEADS), ("rank8", TB * 8), ("rank16", TB * 16)])
C16_AT, C16_COLS = _places([("ident", P), ("tri", P), ("ones", P), ("spread", PER_GROUP * P),
                            ("spread_w8", 4 * P), ("spread_w16", 8 * P)])
COLS_AT, COLS_N = _places([("conv_b", 1), ("dt_b", 4), ("ds", 4), ("b1_0", 16), ("b1_1", 16), ("b1_2", 16),
                           ("b2_0", 4), ("b2_1", 4), ("b2_2", 4), ("q_b", 1), ("k_b", 1), ("b_i1", 1),
                           ("ln_g", 8), ("ln_b", 8)])
ROWS_AT, ROWS_N = _places([("br_0", 32), ("br_1", 32), ("br_2", 32), ("br_3", 64), ("v_b", CH), ("pr_b", CH)])
LOADS = ["x", "c32", "c16", "cols", "rows", "w_in", "alog", "w_xdt", "w_dt", "w_conv", "w_bc", "w_out", "rpb",
         "w_qk", "w_v", "w_pr", "w_i1", "w_i2", "w_pt"] + [f"{a}_{f}" for a in ("w1", "w2", "wr") for f in range(4)]
ARENA = 27136 + (HC_SLOTS + 2) * 1024


def scan_order():
    i = np.arange(INNER)
    return GROUPS * (i % 32) + i // 32


def tap_rows():
    rows = np.full((5, P), -1)
    for r, taps in enumerate(TAP_BLOCKS):
        for half, tap in enumerate(taps):
            rows[r, CH * half:CH * half + CH] = tap * CH + np.arange(CH)
    return rows


def constants():
    c = {n: np.zeros((P, s), np.float32) for n, (_, s) in C32_AT.items()}
    i = np.arange(P)
    c["ident"][:] = np.eye(P)
    c["anti"][:] = np.eye(P)[::-1]
    c["to_scan"][scan_order(), i] = 1
    c["anti_to_scan"][P - 1 - scan_order(), i] = 1
    c["stack_i"][:] = np.tile(np.eye(CH), (2, 1))
    for m in range(PER_GROUP):
        c["state_sum"][i, m * 32 + m * TILE_CH + i // STATE] = 1
    rows = tap_rows()
    for r in range(5):
        ok = rows[r] >= 0
        c["tap_sum"][i[ok], r * CH + rows[r][ok] // TAPS] = 1
    start = np.clip(np.arange(SIDE) - WIN // 2, 0, SIDE - WIN)
    for q in range(2):
        qi, qj = 8 * q + i // SIDE, i % SIDE
        key = np.arange(KEYS)
        ki, kj = KEY_ROW0[q] + key // SIDE, key % SIDE
        inside = ((ki[None] >= start[qi][:, None]) & (ki[None] < start[qi][:, None] + WIN)
                  & (kj[None] >= start[qj][:, None]) & (kj[None] < start[qj][:, None] + WIN))
        c["window"][:, q * KEYS:(q + 1) * KEYS] = np.where(inside, 0.0, -BIG)
    for h in range(HEADS):
        c["head_mask"][HEAD_CH * h:HEAD_CH * (h + 1), h] = float(HEAD_CH) ** -0.5
    c["rank8"][:] = np.tile(8 - np.arange(8), TB)
    c["rank16"][:] = np.tile(16 - np.arange(16), TB)
    h = {n: np.zeros((P, s), np.float32) for n, (_, s) in C16_AT.items()}
    h["ident"][:] = np.eye(P)
    h["tri"][:] = np.triu(np.ones((P, P)))
    h["ones"][:] = 1
    for m in range(PER_GROUP):
        for part in range(PARTS):
            for ch in range(TILE_CH):
                o = m * P + ch * STATE
                h["spread"][32 * part + TILE_CH * m + ch, o:o + STATE] = 1
    for e_n in (8, 16):
        for p in range(e_n // 2):
            for part in range(PARTS):
                for half in range(2):
                    o = p * P + CH * half
                    h[f"spread_w{e_n}"][part * e_n + 2 * p + half, o:o + CH] = 1
    return np.concatenate(list(c.values()), 1), np.concatenate(list(h.values()), 1).astype(mybir.dt.np(BF16))


def lay_out(a):
    def rows_to(w, n=P):
        return np.concatenate([w, np.zeros((n - w.shape[0], *w.shape[1:]), w.dtype)], 0)

    o = {}
    o["c32"], o["c16"] = constants()
    o["x"] = a["x"].reshape(TOKENS, CH)
    w_in = a["L0_conv_in_proj_w"]
    o["w_in"] = rows_to(np.concatenate([w_in[:, :INNER], w_in[:, INNER:][:, scan_order()]], 1))
    o["w_conv"] = a["L0_conv_conv_w"].transpose(1, 2, 3, 0).reshape(INNER, TAPS, INNER)
    xproj = a["L0_conv_xproj_w"]
    half = xproj.shape[0] // 2
    o["w_xdt"] = np.stack([xproj[half * (k // 2) + RANK * (k % 2):][:RANK] for k in range(DIRS)], 1)
    o["w_dt"] = a["L0_conv_dt_w"].transpose(2, 0, 1)
    o["w_bc"] = np.stack([np.stack([np.tile(xproj[half * (k // 2) + 2 * RANK + 2 * STATE * v + STATE * (k % 2):][:STATE].T, (1, TILE_CH))
                                    for v in range(2)], 1) for k in range(DIRS)], 1)
    o["alog"] = a["L0_conv_A_logs"][:, scan_order()].reshape(64, P)
    o["w_out"] = a["L0_conv_out_proj_w"][scan_order()]
    for f, n in enumerate(("L0_ffn_W1", "L1_ffn_W1", "L2_ffn_w1")):
        o[f"w1_{f}"] = a[n].transpose(1, 0, 2).reshape(CH, -1)
        w = a[n[:-2] + ("W2" if f < 2 else "w2")]
        o[f"w2_{f}"] = w.reshape(16, P, CH).transpose(1, 0, 2)
    o["w1_3"] = np.concatenate([a["L3_ffn_" + n].transpose(1, 0, 2).reshape(CH, -1) for n in ("w1", "w2")], 1)
    o["w2_3"] = a["L3_ffn_w3"].transpose(1, 0, 2)
    for f, n in enumerate(("L0_ffn_Wr", "L1_ffn_Wg", "L2_ffn_gate_w", "L3_ffn_gate_w")):
        o[f"wr_{f}"] = rows_to(a[n])
    i, key = np.arange(P)[:, None], np.arange(KEYS)
    o["rpb"] = np.zeros((P, 2, HEADS, KEYS), np.float32)
    for q in range(2):
        di = KEY_ROW0[q] + key // SIDE - (8 * q + i // SIDE) + WIN - 1
        dj = key % SIDE - i % SIDE + WIN - 1
        di, dj = np.broadcast_arrays(di, dj)
        near = (di >= 0) & (di < 2 * WIN - 1) & (dj >= 0) & (dj < 2 * WIN - 1)
        token, at = np.nonzero(near)
        o["rpb"][token, q, :, at] = a["L1_conv_rpb"][:, di[near], dj[near]].T
    qkv, qkv_b = a["L1_conv_qkv_w"], a["L1_conv_qkv_b"]
    o["w_qk"] = rows_to(np.stack([np.tile(qkv[CH * w:CH * (w + 1)].T, (1, 2)) for w in range(2)], 1))
    o["w_v"] = rows_to(qkv[2 * CH:].T)
    o["w_pr"] = np.zeros((P, 2, CH), np.float32)
    for h in range(HEADS):
        o["w_pr"][32 * (h % 4):32 * (h % 4) + HEAD_CH, h // 4] = a["L1_conv_proj_w"].T[HEAD_CH * h:HEAD_CH * (h + 1)]
    o["w_i1"] = rows_to(a["L2_conv_W1"])
    w_i2 = np.concatenate([a["L2_conv_W2"], a["L2_conv_b2"][None]], 0)
    rows = tap_rows()
    of = np.where(rows < 0, 0, rows // (TAPS * CH // INV_GROUPS) * TAPS + rows % TAPS)
    o["w_i2"] = w_i2[:, of]
    o["w_pt"] = rows_to(a["L3_conv_W"])
    c = {n: np.zeros((P, s), np.float32) for n, (_, s) in COLS_AT.items()}
    c["conv_b"][:, 0] = a["L0_conv_conv_b"]
    c["dt_b"][:] = a["L0_conv_dt_b"].T
    c["ds"][:] = a["L0_conv_Ds"].T
    c["ds"][:, 1::2] = c["ds"][::-1, 1::2]
    for f, n in enumerate(("L0_ffn_b1", "L1_ffn_b1", "L2_ffn_b1")):
        c[f"b1_{f}"][:] = a[n].reshape(16, P).T
        c[f"b2_{f}"][:] = a[n[:-1] + "2"].reshape(4, P).T
    c["q_b"][:, 0], c["k_b"][:, 0] = np.tile(qkv_b[0:CH], 2), np.tile(qkv_b[CH:2 * CH], 2)
    c["b_i1"][:INV_HID, 0] = a["L2_conv_b1"]
    c["ln_g"][CH:] = a["L0_ffn_ln_g"].T
    c["ln_b"][CH:] = a["L0_ffn_ln_b"].T
    o["cols"] = np.concatenate(list(c.values()), 1)
    r = [np.tile(a[n], TB) for n in ("L0_ffn_br", "L1_ffn_bg", "L2_ffn_gate_b", "L3_ffn_gate_b")]
    o["rows"] = np.concatenate([*r, qkv_b[2 * CH:], a["L1_conv_proj_b"]])
    return {n: np.ascontiguousarray(v) for n, v in o.items()}


def kernel(**inputs):
    import concourse.bacc as bacc
    from concourse.bass_utils import run_bass_kernel_spmd

    arrays = lay_out({n: np.asarray(v) for n, v in inputs.items()})
    nc = bacc.Bacc("TRN2", target_bir_lowering=False, num_devices=1)
    d = {n: nc.dram_tensor("in_" + n, v.shape, mybir.dt.from_np(v.dtype), kind="ExternalInput").ap()
         for n, v in arrays.items()}
    out = nc.dram_tensor("out", (TOKENS, CH), F32, kind="ExternalOutput").ap()
    build(nc, d, out)
    r = run_bass_kernel_spmd(nc, [{"in_" + n: v for n, v in arrays.items()}], core_ids=[0])
    return r.results[0]["out"].reshape(BATCH, SIDE, SIDE, CH)
```

```python
from contextlib import ExitStack

import concourse.bass as bass
from concourse import mybir
import numpy as np

ALU = mybir.AluOpType
ACT = mybir.ActivationFunctionType
F32 = mybir.dt.float32
BF16 = mybir.dt.bfloat16
X_AXIS = mybir.AxisListType.X

P = 128
BATCH, SIDE, CH = 2, 16, 64
TOKENS = BATCH * SIDE * SIDE
TB = TOKENS // P
HALVES = P // CH
BANK = 512
BIG = 1.0e30
FLT_MAX = 3.4028234663852886e38

INNER, STATE, RANK, DIRS = 128, 16, 16, 4
TILE_CH = P // STATE
GROUPS = 4
PER_GROUP = 32 // TILE_CH
SEQ = SIDE * SIDE
PARTS = 3
PAIRS_PER_DIR = GROUPS * PER_GROUP // 2
PAIRS = DIRS * PAIRS_PER_DIR
HC_SLOTS = 4
PAD = SIDE + 2

HEADS, HEAD_CH, WIN = 8, 8, 7
KEY_ROWS = 11
KEYS = KEY_ROWS * SIDE
KEY_HALF = KEYS // 2
KEY_ROW0 = [0, 5]
UNITS = TB * HEADS
AHEAD = 3

TAPS, INV_GROUPS, INV_HID = 9, 4, 16
TAP_BLOCKS = [(0, 1), (4, 5), (6, 7), (3, 2), (8,)]
CAPACITY = 80

E_OF = [8, 8, 8, 16]
LN_OF_FFN = [1, 3, 5, 7]
EPS = [1e-6, 1e-5, 1e-6, 1e-5, 1e-6, 1e-5, 1e-6, 1e-5]
RING = 8
W1_CHUNKS = [(1, 0), (2, 0), (3, 0), (3, 2048)]
HC_ON_DVE = 2
WARM_NORM = [0, 23, 17, 13, 17, 17, 23, 17]

LOG_FROM = 2.0 ** -6
LOG_C2, LOG_C1, LOG_C0 = 0.32755528, -1.5263569653, 3.0529197377


def build(nc, d, out):
    ctx = ExitStack()
    with ctx:
        def sb(name, shape, dt=F32):
            return ctx.enter_context(nc.sbuf_tensor(name, shape, dt))

        def sem(name):
            return ctx.enter_context(nc.semaphore(name))

        ps = ctx.enter_context(nc.psum_tensor("ps", [P, 8, BANK], F32))

        def bank(i):
            return ps[:, i, :]

        def gate_bank(j):
            return 5 if j == 2 else 1 + 2 * (j % 2)

        def turn_bank(n, image):
            return bank((0, 5 if n % 2 else 1)[image])

        c32 = sb("c32", [P, C32_COLS])
        c16 = sb("c16", [P, C16_COLS], BF16)

        def k32(name):
            o, n = C32_AT[name]
            return c32[:, o:o + n]

        def k16(name):
            o, n = C16_AT[name]
            return c16[:, o:o + n]

        ident, anti, stack_i = k32("ident"), k32("anti"), k32("stack_i")
        to_scan, anti_to_scan = k32("to_scan"), k32("anti_to_scan")
        state_sum = k32("state_sum").rearrange("p (m c) -> p m c", c=32)
        tap_sum = k32("tap_sum").rearrange("p (r c) -> p r c", c=CH)
        window = k32("window").rearrange("p (q k) -> p q k", k=KEYS)
        ident16, tri16, ones16 = k16("ident"), k16("tri"), k16("ones")
        spread = k16("spread").rearrange("p (m c) -> p m c", c=P)
        spread_w = {8: k16("spread_w8").rearrange("p (m c) -> p m c", c=P),
                    16: k16("spread_w16").rearrange("p (m c) -> p m c", c=P)}
        head_mask = k32("head_mask")
        rank_of = {8: k32("rank8"), 16: k32("rank16")}

        cols = sb("cols", [P, COLS_N])
        rows = sb("rows", [P, ROWS_N])

        def col(name, i=0):
            o = COLS_AT[name][0] + i
            return cols[:, o:o + 1]

        def colv(name):
            o, n = COLS_AT[name]
            return cols[:, o:o + n]

        def row(name):
            o, n = ROWS_AT[name]
            return rows[:, o:o + n]

        x = sb("x", [P, 9, TB, CH])
        xn = sb("xn", [P, TB, HALVES * CH])
        xt = sb("xt", [P, TOKENS])
        stats = sb("stats", [P, TB, 6])
        mv = sb("mv", [P, TB, 2])
        ve = sb("ve", [P, 2, TB])
        rstd = sb("rstd", [P, 2, TB])
        sq = sb("sq", [P, TB])
        mhalf = sb("mhalf", [P, 2, TB])

        w_bc = sb("w_bc", [P, DIRS, 2, P])
        aexp = sb("aexp", [P, 64])
        aneg = sb("aneg", [P, 64])
        w_out = sb("w_out", [P, CH])
        idle = sb("idle", [P, 512], BF16)
        log_from, log_at = sb("log_from", [P, 1]), sb("log_at", [P, 1])
        half_c1 = sb("half_c1", [P, 1])

        wr = [sb(f"wr_{f}", [P, E_OF[f]]) for f in range(4)]
        b1f = sb("b1f", [P, 16])

        w_qk = sb("w_qk", [P, 2, P])
        w_v = sb("w_v", [P, CH])
        w_pr = sb("w_pr", [P, 2, CH])
        bias = sb("bias", [P, 2, HEADS, KEYS])
        w_i1 = sb("w_i1", [P, INV_HID])
        w_i2 = sb("w_i2", [P, 5, P])
        w_pt = sb("w_pt", [P, CH])

        arena = sb("arena", [P, ARENA])

        def view(at, n):
            return arena[:, at:at + n]

        u = view(0, 2048).rearrange("p (k l) -> p k l", k=DIRS)
        zs = view(2048, 512)
        dd = view(2560, 4096).rearrange("p (k v l) -> p k v l", k=DIRS, v=2)
        res = view(6656, 4096).rearrange("p (b r v l) -> p b r v l", b=2, r=2, v=2)
        stk = view(10752, 8192).rearrange("p (b g v l) -> p b g v l", b=2, g=GROUPS, v=2)
        bc = view(18944, 4096).rearrange("p (k v l) -> p k v l", k=DIRS, v=2)
        xp = view(18944 + 2048, 2 * PAD * PAD).rearrange("p (b h w) -> p b h w", b=2, h=PAD)
        da = view(23040, 2048).rearrange("p (b s l) -> p b s l", b=2, s=2)
        states = [view(o, 1024).rearrange("p (s l) -> p s l", s=2) for o in (25088, 26112, 31232, 32256)]
        w_in = view(27136, 2 * INNER)
        w_conv = view(27392, TAPS * INNER).rearrange("p (s c) -> p s c", s=TAPS)
        w_xdt = view(28544, DIRS * P)[0:RANK].rearrange("p (k c) -> p k c", k=DIRS)
        w_dt = view(29056, DIRS * P)[0:RANK].rearrange("p (k c) -> p k c", k=DIRS)
        w_fdt = view(29568, DIRS * P).rearrange("p (k c) -> p k c", k=DIRS)
        d_mix = view(30080, 2 * P).rearrange("p (k c) -> p k c", k=2)
        alog = view(30592, P)[0:64]
        hc = view(27136, HC_SLOTS * 1024).rearrange("p (b s l) -> p b s l", b=HC_SLOTS, s=2)
        z_ = [view(25088, 512)] + [sb(f"z_{k}", [P, 512])[:] for k in range(1, DIRS)]
        z1 = [view(30720, 512)] + [sb(f"z1_{k}", [P, 512])[:] for k in range(1, DIRS)]
        zmax = view(14848, 2048).rearrange("p (k l) -> p k l", k=DIRS)
        zmin = [view(16896, 512)] + [xn.rearrange("p t c -> p (t c)"), xt[:], sb("zmin_3", [P, 512])[:]]
        gated = view(2560, 512)
        hid = view(0, RING * 512).rearrange("p (r l) -> p r l", r=RING)
        wb = view(4096, 4096).rearrange("p (q l) -> p q l", q=8)
        acc = view(8192, 512)
        tmp = view(8704, 1024).rearrange("p (r l) -> p r l", r=2)
        gate = view(9728, 1024).rearrange("p (r l) -> p r l", r=2)
        w1 = sb("w1_0", [P, 16 * P])[:]
        w1_parts = {1: [view(o, 1024).bitcast(BF16) for o in (11264, 12288)],
                    2: [view(o, 1024).bitcast(BF16) for o in (13312, 14336)],
                    3: [view(o, 2048).bitcast(BF16) for o in (15360, 17408)]}
        stage = view(29320, 2048)
        x_rest = view(31368, 512)
        x_last = view(31880, 512)
        w2 = [sb("w2_0", [P, 16, CH])[:]] + [view(19456 + 1024 * f, 1024).rearrange("p (b c) -> p b c", c=CH) for f in range(3)]
        qf, kf = view(0, 512), view(512, 512)
        qz = view(1024, 4096).rearrange("p (h l) -> p h l", h=HEADS)
        sm = view(5120, 16 * KEYS).rearrange("p (r k) -> p r k", r=16)
        pr = view(7936, 16 * KEYS).rearrange("p (r k) -> p r k", r=16)
        pt = view(23688, 4 * 512)[0:KEY_HALF].rearrange("p (r l) -> p r l", r=4)
        vz = view(26248, 2048)[0:KEY_HALF].rearrange("p (u h c) -> p u h c", u=8, h=HEADS)
        at = view(28296, 1024).rearrange("p (a l) -> p a l", a=2)
        xpp = view(22528, 2 * PAD * PAD).rearrange("p (b h w) -> p b h w", b=2, h=PAD)
        ih = view(23176, 512)
        prod = view(23688, 5 * 512).rearrange("p (r l) -> p r l", r=5)

        lg = sb("lg", [P, 64]); dl = sb("dl", [P, 64]); c1 = sb("c1", [P, 64]); oh1 = sb("oh1", [P, 64])
        d2 = sb("d2", [P, 64]); g2 = sb("g2", [P, 64]); c2 = sb("c2", [P, 64]); oh2 = sb("oh2", [P, 64])
        ex = sb("ex", [P, 64]); ww = sb("ww", [P, 64]); wr1 = sb("wr1", [P, 64]); wr2 = sb("wr2", [P, 64])
        m1 = sb("m1", [P, TB]); i1 = sb("i1", [P, TB]); m2 = sb("m2", [P, TB]); i2 = sb("i2", [P, TB])
        th = sb("th", [P, TB]); wa = sb("wa", [P, TB]); wc = sb("wc", [P, TB])
        oh16 = sb("oh16", [P, 32], BF16)
        wp = sb("wp", [P, TB, 48], BF16)
        wt = view(10752, 256).bitcast(BF16)[0:48]
        nan_a = view(11008, 256)
        nan_b, finite = view(23688, 256), view(23944, 256).bitcast(mybir.dt.uint32)
        mx = sb("mx", [P, UNITS]); nmx = sb("nmx", [P, UNITS]); rsum = sb("rsum", [P, UNITS]); rrec = sb("rrec", [P, UNITS])

        load = {n: sem("l_" + n) for n in LOADS}
        dve_step, pool_step = sem("dve_step"), sem("pool_step")
        var_ready, rstd_ready, ln_ready = sem("var_ready"), sem("rstd_ready"), sem("ln_ready")
        xt_padded, w_i2_padded = sem("xt_padded"), sem("w_i2_padded")
        xt_ps, xt_sb, resid = sem("xt_ps"), [sem("xt_sb_act"), sem("xt_sb_dve")], sem("resid")
        zeroed = sem("zeroed")
        zmax_ready, square_ready, log_at_ready = sem("zmax_ready"), sem("square_ready"), sem("log_at_ready")
        half_c1_set = sem("half_c1_set")
        prep_ps, fdt_ps, aexp_ready, aneg_ready = sem("prep_ps"), sem("fdt_ps"), sem("aexp_ready"), sem("aneg_ready")
        fdt_sb, bias_seen, w1_scaled = sem("fdt_sb"), sem("bias_seen"), sem("w1_scaled")
        xi_ps, z_ps, xp_ready, conv_ps, u0_ready = sem("xi_ps"), sem("z_ps"), sem("xp_ready"), sem("conv_ps"), sem("u0_ready")
        zs_ready = sem("zs_ready")
        rev_ps, u_ready, dts_ps, delta_ready = sem("rev_ps"), sem("u_ready"), sem("dts_ps"), sem("delta_ready")
        delta_u_ready, rest_ready = [sem("delta_u_dve"), sem("delta_u_pool")], sem("rest_ready")
        abs_ready, z_ready, log_ready, z1_ready = sem("abs_ready"), sem("z_ready"), sem("log_ready"), sem("z1_ready")
        w_staged, w_rest, w_split = sem("w_staged"), sem("w_rest"), sem("w_split")
        x_rest_ready, x_last_ready, x_twice = sem("x_rest_ready"), sem("x_last_ready"), sem("x_twice")
        zmin_ready, u_back_ready = sem("zmin_ready"), sem("u_back_ready")
        b1f_ready, hc_last = sem("b1f_ready"), sem("hc_last")
        lost_ready, log1p_ready, relu_ready = sem("lost_ready"), [sem("log1p_dve"), sem("log1p_pool")], sem("relu_ready")
        stacked = [sem("stacked0"), sem("stacked1")]
        bc_ps, bc_sb, diag_ready = sem("bc_ps"), sem("bc_sb"), sem("diag_ready")
        dspread, uspread, exp_done = sem("dspread"), sem("uspread"), sem("exp_done")
        mul_done, scan_done, hc_done, sum_done = sem("mul_done"), sem("scan_done"), sem("hc_done"), sem("sum_done")
        gated_ready, proj_ps = sem("gated_ready"), sem("proj_ps")
        logits, gap, gap_act, w_ready, wt_ps, wt_sb = (sem(n) for n in ("logits", "gap", "gap_act", "w_ready", "wt_ps", "wt_sb"))
        hid_ps, hid_ready, y_ready, wb_ps, wb_sb, comb = (sem(n) for n in ("hid_ps", "hid_ready", "y_ready", "wb_ps", "wb_sb", "comb"))
        acc_ready, out_ps, gate_ready = sem("acc_ready"), sem("out_ps"), sem("gate_ready")
        oh_ready, count_ps = sem("oh_ready"), sem("count_ps")
        bias_ready = sem("bias_ready")
        qk_ps, v_ps, q_sb, k_sb, v_sb = (sem(n) for n in ("qk_ps", "v_ps", "q_sb", "k_sb", "v_sb"))
        score, masked, negmax, prob, pt_ps, pt_sb, pv = (sem(n) for n in ("score", "masked", "negmax", "prob", "pt_ps", "pt_sb", "pv"))
        inverse, normed, apr_ps = (sem(n) for n in ("inverse", "normed", "apr_ps"))
        at_sb = [sem("at_sb_dve"), sem("at_sb_act")]
        ih_ps, ih_sb, pad_ready, wq_ps, prod_ready, inv_ps = (sem(n) for n in ("ih_ps", "ih_sb", "pad_ready", "wq_ps", "prod_ready", "inv_ps"))
        stored = sem("stored")

        block = ctx.enter_context(nc.Block())

        def high(v2d):
            return v2d.bitcast(BF16).rearrange("p (l two) -> p l two", two=2)[:, :, 1]

        def tiles(v, n=TB):
            return v.rearrange("p (t e) -> p t e", t=n)

        def spread_last(v, n):
            return v.unsqueeze(2).to_broadcast([v.shape[0], v.shape[1], n])

        def probs_copy(eng, h, g):
            eng.wait_ge(pt_ps, 2 * h + g + 1)
            if h >= 2:
                eng.wait_ge(pv, h - 1)
            src, dst = bank(5 + g)[0:KEY_HALF], pt[:, 2 * (h % 2) + g]
            if g == 0:
                eng.activation(dst, src, ACT.Copy).then_inc(pt_sb[0], 1)
            else:
                eng.tensor_copy(dst, src).then_inc(pt_sb[1], 1)

        pt_sb = [sem("pt_sb_act"), sem("pt_sb_dve")]
        qz_ready = [sem("qz_ready_dve"), sem("qz_ready_act")]

        def columns_first(v):
            return v.rearrange("p (b h w) -> p b w h", b=2, h=SIDE)

        def grid(v):
            return v.rearrange("p (b h w) -> p b h w", b=2, h=SIDE)

        def delta_u(eng, k):
            if k:
                eng.wait_ge(u_ready, 1)
                eng.wait_ge(u_back_ready, 2)
            eng.wait_ge(delta_ready, k + 1)
            eng.tensor_tensor(dd[:, k, 1], dd[:, k, 0], u[:, k], ALU.mult).then_inc(u_made(k)[0], 1)

        def u_made(k):
            return delta_u_ready[k // 2], k % 2 + 1

        def lost(eng, k):
            eng.wait_ge(z1_ready, k + 1)
            eng.tensor_tensor(z1[k], zmax[:, k], z1[k], ALU.subtract).then_inc(lost_ready, 1)

        def log1p(eng, k):
            on = int(k > 0)
            eng.wait_ge(lost_ready, k + 1)
            eng.wait_ge(log_ready, k + 1)
            eng.tensor_tensor(z1[k], z1[k], dd[:, k, 1], ALU.add).then_inc(log1p_ready[on], 1)

        pair_tiles = [[(2 * (i % 2) + s, (i % PAIRS_PER_DIR) // 2) for s in range(2)] for i in range(PAIRS)]

        @block.sync
        def _(sp):
            def get(name, dst, src):
                sp.dma_start(dst, src).then_inc(load[name], 16)

            get("x", x[:, 0], d["x"].rearrange("(t p) c -> p t c", p=P))
            get("c32", c32[:], d["c32"])
            get("cols", cols[:], d["cols"])
            get("w_in", w_in, d["w_in"])
            get("alog", alog, d["alog"])
            get("w_xdt", w_xdt, d["w_xdt"])
            get("w_dt", w_dt, d["w_dt"])
            get("w_conv", w_conv, d["w_conv"])
            get("w_bc", w_bc[:], d["w_bc"])
            get("c16", c16[:], d["c16"])
            get("rows", rows[:], d["rows"].partition_broadcast(P))
            get("w1_0", w1[CH:P, :], d["w1_0"])
            def stack(k):
                if k == 1:
                    sp.wait_ge(lost_ready, DIRS)
                    sp.wait_ge(log_ready, DIRS)
                if k >= 2:
                    sp.wait_ge(dspread, 2 * PAIRS_PER_DIR * (k - 1))
                    sp.wait_ge(uspread, PAIRS_PER_DIR * (k - 1))
                for part in range(PARTS):
                    if part == 0:
                        sp.wait_ge(*u_made(k))
                    else:
                        sp.wait_ge(rest_ready, 2 * k + part)
                    src = dd[:, k] if part == 0 else res[:, k % 2, part - 1]
                    sp.dma_start(stk[32 * part:32 * part + 32, k % 2], src).then_inc(stacked[k % 2], 16)

            get("w_out", w_out[:], d["w_out"])
            for f in range(4):
                get(f"wr_{f}", wr[f][:], d[f"wr_{f}"])
            stack(0)
            get("w2_0", w2[0], d["w2_0"])
            get("rpb", bias[:], d["rpb"])
            stack(1)
            get("w_qk", w_qk[:], d["w_qk"])
            get("w_v", w_v[:], d["w_v"])
            get("w_pr", w_pr[:], d["w_pr"])
            stack(2)
            get("w_i1", w_i1[:], d["w_i1"])
            sp.wait_ge(w_i2_padded, 1)
            get("w_i2", w_i2[0:INV_HID + 1], d["w_i2"])
            get("w_pt", w_pt[:], d["w_pt"])
            stack(3)
            sp.wait_ge(sum_done, PAIRS // 2)
            for c, (f, first) in enumerate(W1_CHUNKS):
                if c:
                    sp.wait_ge(w_split, 2 * c)
                for half in range(2):
                    sp.dma_start(stage[CH * half:CH * half + CH], d[f"w1_{f}"][:, first:first + 2048]).then_inc(w_staged, 16)
                if f > c:
                    get(f"w2_{f}", w2[f], d[f"w2_{f}"])
            sp.wait_ge(resid, 8)
            sp.dma_start(out.rearrange("(t p) c -> p t c", p=P), x[:, 8]).then_inc(stored, 16)
            sp.wait_ge(stored, 16)

        @block.gpsimd
        def _(pool):
            def rsqrt(n):
                w = 2 if n == 1 else 1
                pool.wait_ge(var_ready, n + 1)
                pool.tensor_tensor(rstd[:, 0:w], ve[:, 0:w], mhalf[:, 0:w], ALU.pow).then_inc(rstd_ready, 1)

            pool.memset(mhalf[:], -0.5).then_inc(pool_step, 1)
            pool.memset(idle[:], 0.0).then_inc(pool_step, 1)
            pool.memset(xt[:], 0.0).then_inc(xt_padded, 1)
            pool.memset(xp, 0.0).then_inc(zeroed, 1)
            pool.memset(da.rearrange("p b s (i l) -> p (b s i) l", l=SEQ)[:, :, 0:1], 0.0).then_inc(zeroed, 1)
            pool.memset(log_from[:], LOG_FROM).then_inc(zeroed, 1)
            pool.memset(half_c1[:], LOG_C1 / 2).then_inc(half_c1_set, 1)
            pool.wait_ge(pool_step, 1)
            rsqrt(0)
            pool.memset(w_i2[:], 0.0).then_inc(w_i2_padded, 1)
            pool.memset(w1[0:CH, :], 0.0).then_inc(zeroed, 1)
            lost(pool, 0)
            for k in range(1, DIRS):
                lost(pool, k)
            for k in range(1, DIRS):
                log1p(pool, k)
            for i in range(PAIRS - HC_ON_DVE):
                k = i // PAIRS_PER_DIR
                if i == 0:
                    pool.wait_ge(bc_sb, 2)
                elif i % PAIRS_PER_DIR == 0:
                    pool.wait_ge(bc_sb, 2 * k + 2)
                if i >= HC_SLOTS:
                    pool.wait_ge(sum_done, (i - HC_SLOTS) // 2 + 1)
                pool.wait_ge(scan_done, i + 1)
                c_all = bc[:, k, 1].unsqueeze(1).to_broadcast([P, 2, 2 * SEQ])
                pool.tensor_tensor(hc[:, i % HC_SLOTS], states[i % 4], c_all, ALU.mult).then_inc(hc_done, 1)
                if i in (6, 12):
                    delta_u(pool, i // 6 + 1)


            def weight_rest(c, step):
                if step == 0:
                    pool.wait_ge(w_staged, 32 * (c + 1))
                else:
                    pool.wait_ge(w_split, 2 * c + 1)
                w = stage[CH:P]
                pool.tensor_tensor(w, w, high(w), ALU.subtract).then_inc(w_rest, 1)
                pool.wait_ge(w_rest, 2 * c + step + 1)

            rsqrt(1)
            pool.wait_ge(rstd_ready, 2)
            weight_rest(0, 0)
            pool.wait_ge(load["rpb"], 16)
            pool.wait_ge(load["c32"], 16)
            for q in range(2):
                outside = window[:, q].unsqueeze(1).to_broadcast([P, HEADS, KEYS])
                pool.tensor_tensor(bias[:, q], bias[:, q], outside, ALU.add).then_inc(bias_ready, 1)
            pool.wait_ge(bias_ready, 2)
            weight_rest(0, 1)
            pool.wait_ge(sum_done, PAIRS // 2)
            pool.memset(view(22528, 2 * PAD * PAD), 0.0).then_inc(zeroed, 1)
            pool.memset(ih, 1.0).then_inc(zeroed, 1)
            pool.wait_ge(zeroed, 6)
            pool.memset(view(26248, 2048)[0:KEY_HALF], 0.0).then_inc(zeroed, 1)
            pool.wait_ge(zeroed, 7)
            for n in range(2, 8):
                rsqrt(n)
                if 3 <= n <= 5:
                    pool.wait_ge(rstd_ready, n + 1)
                    weight_rest(n - 2, 0)
                    weight_rest(n - 2, 1)
                if n == 2:
                    for h in range(HEADS):
                        pool.wait_ge(inverse, h + 1)
                        w = pr[:, TB * (h % 4):TB * (h % 4) + TB]
                        pool.tensor_tensor(w, w, spread_last(rrec[:, TB * h:TB * h + TB], KEYS), ALU.mult).then_inc(normed, 1)

        @block.scalar
        def _(act):
            act.wait_ge(xt_padded, 1)

            def turned(n):
                m = P if n % 2 else CH
                act.wait_ge(xt_ps, 2 * n + 1)
                act.activation(xt[0:m, 0:SEQ], turn_bank(n, 0)[0:m, 0:SEQ], ACT.Copy).then_inc(xt_sb[0], 1)
                if n in (3, 5, 7):
                    act.activation(x_last[CH:P, 0:SEQ], turn_bank(n, 0)[CH:P, 0:SEQ], ACT.Copy).then_inc(x_twice, 1)
                    act.wait_ge(xt_sb[1], n + 1)
                    act.activation(x_last[CH:P, SEQ:], turn_bank(n, 1)[CH:P, 0:SEQ], ACT.Copy).then_inc(x_twice, 1)

            act.preload_act_table(ACT.Silu)
            turned(0)
            act.wait_ge(z_ps, 1)
            act.activation(zs, bank(2), ACT.Silu).then_inc(zs_ready, 1)
            act.wait_ge(load["cols"], 16)
            act.wait_ge(conv_ps, 1)
            act.activation(u[:, 0], bank(3), ACT.Silu, bias=col("conv_b")).then_inc(u0_ready, 1)
            act.preload_act_table_set("natural_log_exp_and_others")
            act.wait_ge(zeroed, 3)
            act.activation(log_at[:], log_from[:], ACT.Ln, bias=1.0).then_inc(log_at_ready, 1)

            def bc_copy(q):
                act.wait_ge(bc_ps, q + 1)
                if q == 4:
                    act.wait_ge(conv_ps, 1)
                act.activation(bc[:, q // 2, q % 2], bank(7), ACT.Copy).then_inc(bc_sb, 1)

            def log_of(k):
                act.wait_ge(zmax_ready, k + 1)
                act.activation(dd[:, k, 1], zmax[:, k], ACT.Ln, bias=1.0).then_inc(log_ready, 1)

            def square(k):
                act.wait_ge(zmin_ready, k + 1)
                act.activation(z_[k], zmin[k], ACT.Square, bias=half_c1[:]).then_inc(square_ready, 1)

            for k in range(DIRS):
                act.wait_ge(dts_ps, k + 1)
                act.activation(dd[:, k, 1], bank(k), ACT.Abs, bias=col("dt_b", k)).then_inc(abs_ready, 1)
                act.wait_ge(abs_ready, k + 1)
                act.activation(z_[k], dd[:, k, 1], ACT.Exp, scale=-1.0).then_inc(z_ready, 1)
                act.activation(dd[:, k, 0], bank(k), ACT.Relu, bias=col("dt_b", k)).then_inc(relu_ready, 1)
                if k == 0:
                    log_of(0)
                if k == 1:
                    act.wait_ge(prep_ps, 1)
                    act.activation(aexp[:], bank(4)[:, 0:64], ACT.Exp).then_inc(aexp_ready, 1)
                    bc_copy(0)
                    act.wait_ge(aexp_ready, 1)
                    act.activation(aneg[:], aexp[:], ACT.Copy, scale=-1.0).then_inc(aneg_ready, 1)

            act.wait_ge(rev_ps, 1)
            act.activation(u[:, 1], bank(5), ACT.Copy).then_inc(u_back_ready, 1)
            act.activation(grid(u[:, 3]), columns_first(bank(5)), ACT.Copy).then_inc(u_back_ready, 1)
            bc_copy(1)
            for k in range(1, DIRS):
                log_of(k)
            act.wait_ge(half_c1_set, 1)
            for i in range(PAIRS):
                k, ii = divmod(i, PAIRS_PER_DIR)
                if i == 0:
                    act.wait_ge(aneg_ready, 1)
                    act.wait_ge(zeroed, 2)
                if i >= 2:
                    act.wait_ge(scan_done, i - 1)
                for s, (g, m) in enumerate(pair_tiles[i]):
                    act.wait_ge(dspread, 2 * i + s + 1)
                    q = 16 * k + PER_GROUP * g + m
                    act.activation(da[:, i % 2, s].rearrange("p (b l) -> p b l", b=2)[:, :, 1:SEQ],
                                   bank(s).rearrange("p (b l) -> p b l", b=2)[:, :, 1:SEQ],
                                   ACT.Exp, scale=aneg[:, q:q + 1]).then_inc(exp_done, 1)
                if k == 0 and ii in (0, 2, 4):
                    square(1 + ii // 2)
                if k < DIRS - 1 and ii in (3, 5):
                    bc_copy(2 * (k + 1) + (ii == 5))

            def weight_split(c, step):
                f, first = W1_CHUNKS[c]
                act.wait_ge(w_rest, 2 * c + step + 1)
                act.activation(w1_parts[f][step][:, first:first + 2048], high(stage), ACT.Copy).then_inc(w_split, 1)

            def experts(f, func):
                base, base_w = 16 * f, 4 * f
                for j in range(16):
                    act.wait_ge(hid_ps, base + j + 1)
                    if j >= RING:
                        act.wait_ge(y_ready, base_w + (j - RING) // 4 + 1)
                    p, q = divmod(j, 4)
                    blk = 4 * p + 2 * (q % 2) + q // 2
                    b1 = b1f[:, blk:blk + 1] if f == 0 else col(f"b1_{f}", blk)
                    act.activation(hid[:, j % RING], bank(1 + j % 4), func, bias=b1).then_inc(hid_ready, 1)
                    if f < 2 and j in (4, 12):
                        weight_split(f, j // 12)
                    if f == 2 and j == 6:
                        weight_split(3, 0)
                    if f == 2 and j == 1:
                        act.wait_ge(gap, f + 1)
                        act.activation(ex[:, 0:32], dl[:, 0:32], ACT.Exp).then_inc(gap_act, 1)
                    if j == 2 and f < 2:
                        act.wait_ge(gap, f + 1)
                        act.activation(th[:], m2[:], ACT.Tanh, scale=-0.5).then_inc(gap_act, 1)
                    if j % 4 == 3 and j > 3:
                        weight_copy(base_w, p - 1)
                weight_copy(base_w, 3)

            def weight_copy(base_w, p):
                act.wait_ge(wb_ps, base_w + p + 1)
                act.activation(wb[:, p], bank(7), ACT.Copy).then_inc(wb_sb, 1)

            act.wait_ge(bias_seen, 1)
            for e in range(8):
                o = w1[CH:P, 2 * e * P:(2 * e + 2) * P]
                last = act.activation(o, o, ACT.Copy, scale=col("ln_g", e)[CH:P])
            last.then_inc(w1_scaled, 1)
            act.preload_act_table(ACT.Gelu)
            turned(1)
            act.wait_ge(b1f_ready, 1)
            experts(0, ACT.Gelu)

            act.preload_act_table(ACT.Exp)
            turned(2)
            act.wait_ge(qk_ps, 1)
            act.activation(qf, bank(1), ACT.Identity, bias=col("q_b")).then_inc(q_sb, 1)
            act.wait_ge(q_sb, 1)
            for h in range(1, HEADS, 2):
                act.activation(qz[:, h], qf, ACT.Copy, scale=head_mask[:, h:h + 1]).then_inc(qz_ready[1], 1)
            for h in range(HEADS):
                act.wait_ge(negmax, h + 1)
                if h >= 4:
                    act.wait_ge(pt_ps, 2 * (h - 4) + 2)
                for unit in range(TB * h, TB * h + TB):
                    act.activation(pr[:, unit % 16], sm[:, unit % 16], ACT.Exp, bias=nmx[:, unit:unit + 1],
                                   accum_out=rsum[:, unit:unit + 1]).then_inc(prob, 1)
                if h >= 1:
                    probs_copy(act, h - 1, 0)
            probs_copy(act, HEADS - 1, 0)
            act.wait_ge(pv, 8)
            act.activation(at[:, 1], bank(7), ACT.Copy).then_inc(at_sb[1], 1)
            act.preload_act_table(ACT.Gelu)
            turned(3)
            experts(1, ACT.Gelu)

            act.preload_act_table(ACT.Exp)
            turned(4)
            act.wait_ge(zeroed, 6)
            act.wait_ge(xt_sb[0], 5)
            act.wait_ge(xt_sb[1], 5)
            act.activation(xpp[0:CH, :, 1:SIDE + 1, 1:SIDE + 1],
                           xt[0:CH].rearrange("p (b h w) -> p b h w", b=2, h=SIDE), ACT.Copy).then_inc(pad_ready, 1)
            act.wait_ge(ih_ps, 1)
            act.activation(ih[0:INV_HID], bank(1)[0:INV_HID], ACT.Identity,
                           bias=col("b_i1")[0:INV_HID]).then_inc(ih_sb, 1)
            weight_split(2, 0)
            weight_split(2, 1)
            turned(5)
            experts(2, ACT.Relu)
            weight_split(3, 1)

            act.preload_act_table(ACT.Silu)
            turned(6)
            turned(7)
            for j in range(16):
                act.wait_ge(hid_ps, 48 + j + 1)
                if j >= 2:
                    act.wait_ge(hid_ready, 48 + j - 1)
                act.activation(gate[:, j % 2], bank(gate_bank(j)), ACT.Silu).then_inc(gate_ready, 1)
                if j == 2:
                    act.wait_ge(gap, 4)
                    act.activation(th[:], m2[:], ACT.Tanh, scale=-0.5).then_inc(gap_act, 1)
                if j % 2 == 1 and j >= 5:
                    weight_copy(12, (j - 5) // 2)
            weight_copy(12, 6)
            weight_copy(12, 7)

        @block.tensor
        def _(pe):
            def keep_warm(n, into=5):
                for _ in range(n):
                    pe.matmul(bank(into), idle[:, 0:P], idle[:], start=True, stop=True)

            def turn(n):
                if n:
                    keep_warm(WARM_NORM[n])
                    turned(n - 1)
                m = P if n % 2 else CH
                for t in range(TB):
                    pe.wait_ge(ln_ready, TB * n + t + 1)
                    last = pe.transpose(turn_bank(n, t // 2)[0:m, (t % 2) * P:(t % 2 + 1) * P], xn[:, t, 0:m], ident)
                    if t % 2:
                        last.then_inc(xt_ps, 1)

            def turned(n):
                for side in range(2):
                    pe.wait_ge(xt_sb[side], n + 1)

            def got(*names):
                for n in names:
                    pe.wait_ge(load[n], 16)

            pe.wait_ge(pool_step, 2)
            keep_warm(12)
            got("c32", "alog", "w_xdt", "w_dt")
            pe.transpose(bank(4)[:, 0:64], alog, ident[0:64, 0:64]).then_inc(prep_ps, 1)
            for k in range(DIRS):
                last = pe.matmul(bank(5)[:, k * P:(k + 1) * P], w_xdt[:, k], w_dt[:, k], start=True, stop=True)
            last.then_inc(fdt_ps, 1)
            turn(0)
            got("w_in")
            turned(0)
            pe.wait_ge(xt_padded, 1)
            pe.matmul(bank(1), w_in[:, 0:INNER], xt[:], start=True, stop=True).then_inc(xi_ps, 1)
            pe.matmul(bank(2), w_in[:, INNER:], xt[:], start=True, stop=True).then_inc(z_ps, 1)
            got("w_conv")
            pe.wait_ge(xp_ready, 1)
            for s in range(TAPS):
                dy, dx = divmod(s, 3)
                last = pe.matmul(bank(3), w_conv[:, s], xp[:, :, dy:dy + SIDE, dx:dx + SIDE],
                                 start=(s == 0), stop=(s == TAPS - 1))
            last.then_inc(conv_ps, 1)
            pe.wait_ge(u0_ready, 1)
            pe.wait_ge(fdt_sb, 1)

            def dts(k):
                pe.matmul(bank(k), w_fdt[:, k], u[:, 0 if k < 2 else 2], start=True, stop=True).then_inc(dts_ps, 1)

            def bc_mm(q):
                if q:
                    pe.wait_ge(bc_sb, q)
                pe.matmul(bank(7), w_bc[:, q // 2, q % 2], u[:, 0 if q < 4 else 2], start=True, stop=True).then_inc(bc_ps, 1)

            dts(0)
            dts(1)
            pe.matmul(bank(5), anti, u[:, 0], start=True, stop=True).then_inc(rev_ps, 1)
            got("w_bc")
            bc_mm(0)
            pe.wait_ge(u_ready, 1)
            pe.wait_ge(zs_ready, 1)
            dts(2)
            dts(3)
            pe.wait_ge(diag_ready, 1)
            for a in range(2):
                pe.matmul(bank(6), d_mix[:, a], u[:, 2 * a], start=(a == 0), stop=False, skip_group_check=True)
            bc_mm(1)

            got("w1_0", "cols")
            pe.wait_ge(zeroed, 4)
            pe.wait_ge(aexp_ready, 1)
            for blk in range(16):
                last = pe.matmul(bank(4)[:, blk:blk + 1], w1[:, blk * P:(blk + 1) * P], col("ln_b", blk // 2),
                                 start=True, stop=True)
            last.then_inc(bias_seen, 1)

            def spread_pair(i):
                k = i // PAIRS_PER_DIR
                if i % PAIRS_PER_DIR == 0:
                    pe.wait_ge(stacked[k % 2], 16 * PARTS * (k // 2 + 1))
                if i >= 2:
                    pe.wait_ge(mul_done, i - 1)
                for s, (g, m) in enumerate(pair_tiles[i]):
                    last = pe.matmul(bank(2 + 2 * (i % 2) + s), spread[0:96, m], high(stk[0:96, k % 2, g, 1]),
                                     start=True, stop=True)
                last.then_inc(uspread, 1)
                for s, (g, m) in enumerate(pair_tiles[i]):
                    if i:
                        pe.wait_ge(exp_done, 2 * (i - 1) + s + 1)
                    pe.matmul(bank(s), spread[0:96, m], high(stk[0:96, k % 2, g, 0]),
                              start=True, stop=True).then_inc(dspread, 1)

            def sum_states(q):
                for i in (2 * q, 2 * q + 1):
                    if i < PAIRS - HC_ON_DVE:
                        pe.wait_ge(hc_done, i + 1)
                    else:
                        pe.wait_ge(hc_last, i + 1 - (PAIRS - HC_ON_DVE))
                    for s, (g, m) in enumerate(pair_tiles[i]):
                        last = pe.matmul(ps[32 * g:32 * g + 32, 6, :], state_sum[:, m], hc[:, i % HC_SLOTS, s],
                                         start=False, stop=(q == PAIRS // 2 - 1), skip_group_check=True)
                last.then_inc(sum_done, 1)

            got("c16")
            pe.wait_ge(relu_ready, DIRS)
            pe.wait_ge(u_back_ready, 2)
            keep_warm(8)
            spread_pair(0)
            pe.wait_ge(b1f_ready, 1)
            spread_pair(1)
            for i in range(PAIRS):
                k, ii = divmod(i, PAIRS_PER_DIR)
                if i + 2 < PAIRS:
                    spread_pair(i + 2)
                if i >= 3 and i % 2:
                    sum_states((i - 3) // 2)
                if k < DIRS - 1 and ii in (2, 4):
                    bc_mm(2 * (k + 1) + (ii == 4))
            pe.wait_ge(bc_sb, 2 * DIRS)
            keep_warm(6, 7)
            sum_states(PAIRS // 2 - 1)
            pe.wait_ge(gated_ready, 1)
            got("w_out")
            for t in range(TB):
                last = pe.matmul(bank(1)[:, t * CH:(t + 1) * CH], gated[:, t * P:(t + 1) * P], w_out[:], start=True, stop=True)
            last.then_inc(proj_ps, 1)

            def experts(f):
                n, e_n = LN_OF_FFN[f], E_OF[f]
                pairs = e_n // 2
                base, base_w = 16 * f, 4 * f
                got(f"wr_{f}", f"w2_{f}")
                if f == 0:
                    got("w1_0")
                else:
                    pe.wait_ge(w_split, (0, 2, 4, 8)[f])
                turn(n)
                turned(n)
                for t in range(TB):
                    last = pe.matmul(bank(7)[:, t * e_n:(t + 1) * e_n], xt[:, t * P:(t + 1) * P], wr[f][:], start=True, stop=True)
                last.then_inc(logits, 1)
                if f == 0:
                    pe.wait_ge(w1_scaled, 1)
                per = 16 // pairs

                def products(wanted):
                    for part in range(PARTS):
                        if part == 1:
                            pe.wait_ge(x_rest_ready, f)
                        if part == 2:
                            pe.wait_ge(x_last_ready, f)
                            pe.wait_ge(x_twice, 2 * f)
                        for b, blk in wanted:
                            last = pe.matmul(bank(b), w1_parts[f][part // 2][:, blk * P:(blk + 1) * P],
                                             high((xt[:], x_rest, x_last)[part]), start=(part == 0), stop=(part == PARTS - 1),
                                             skip_group_check=True)
                            if part == PARTS - 1 and (f < 3 or blk >= 16):
                                last.then_inc(hid_ps, 1)

                def hidden(p):
                    if f and p == 0:
                        if f < 3:
                            products([(1 + q, 2 * (q % 2) + q // 2) for q in range(4)])
                        else:
                            products([(1 + 2 * j + h, 16 * h + j) for j in range(2) for h in range(2)])
                        return
                    for q in range(per):
                        j = per * p + q
                        if f < 3:
                            if j >= 4:
                                pe.wait_ge(hid_ready, base + j - 3)
                            blk = 4 * p + 2 * (q % 2) + q // 2
                            if f:
                                products([(1 + j % 4, blk)])
                            else:
                                pe.matmul(bank(1 + j % 4), w1[:, blk * P:(blk + 1) * P], xt[:], start=True, stop=True)\
                                  .then_inc(hid_ps, 1)
                        else:
                            if j > 2:
                                pe.wait_ge(hid_ready, base + j - 1)
                            products([(gate_bank(j), j), (gate_bank(j) + 1, 16 + j)])

                def down(p, between=False):
                    if p == 0:
                        weights_turn()
                    if p >= 2:
                        pe.wait_ge(comb, base_w + p - 1)
                    for q in range(per):
                        if between and q == per // 2:
                            weights(p)
                        j = per * p + q
                        blk = 4 * p + 2 * (q % 2) + q // 2 if f < 3 else j
                        pe.wait_ge(hid_ready, base + j + 1)
                        o = CH * (q % 2)
                        last = pe.matmul(ps[o:o + CH, 5 + p % 2, :], w2[f][:, blk], hid[:, j % RING],
                                         start=(q < 2), stop=(q >= per - 2), skip_group_check=True)
                    last.then_inc(y_ready, 1)

                def weights_turn():
                    pe.wait_ge(w_ready, f + 1)
                    for t in range(TB):
                        last = pe.transpose(bank(7).bitcast(BF16)[0:PARTS * e_n, t * P:(t + 1) * P],
                                            wp[:, t, 0:PARTS * e_n], ident16)
                    last.then_inc(wt_ps, 1)

                def weights(p):
                    if p == 0:
                        pe.wait_ge(wt_sb, f + 1)
                    else:
                        pe.wait_ge(wb_sb, base_w + p)
                    pe.matmul(bank(7), spread_w[e_n][0:PARTS * e_n, p], wt[0:PARTS * e_n, :], start=True, stop=True).then_inc(wb_ps, 1)

                hidden(0)
                if f == 2:
                    pe.wait_ge(oh_ready, 1)
                    for t in range(TB):
                        for t2 in range(t + 1):
                            last = pe.matmul(bank(0)[:, t * 8:t * 8 + 8], tri16 if t2 == t else ones16,
                                             oh16[:, t2 * 8:t2 * 8 + 8], start=(t2 == 0), stop=(t2 == t))
                    last.then_inc(count_ps, 1)
                lag = 0 if f < 3 else 1
                for p in range(1, pairs):
                    hidden(p)
                    if p - 1 - lag >= 0:
                        down(p - 1 - lag)
                        weights(p - 1 - lag)
                for p in range(pairs - 1 - lag, pairs):
                    down(p, between=(p == pairs - 1))
                    if p < pairs - 1:
                        weights(p)
                pe.wait_ge(acc_ready, f + 1)
                for t in range(TB):
                    pe.matmul(bank(0)[:, t * CH:(t + 1) * CH], acc[:, t * P:(t + 1) * P], stack_i,
                              start=(t == 0), stop=False, skip_group_check=True)
                pe.wait_ge(comb, base_w + pairs)
                for t in range(TB):
                    last = pe.matmul(bank(0)[:, t * CH:(t + 1) * CH], tmp[:, (pairs - 1) % 2, t * P:(t + 1) * P], stack_i,
                                     start=False, stop=(t == TB - 1), skip_group_check=True)
                last.then_inc(out_ps, 1)

            experts(0)

            got("w_qk", "w_v", "w_pr")
            turn(2)
            turned(2)
            for a in range(2):
                pe.matmul(bank(1 + a), w_qk[:, a], xt[:], start=True, stop=True).then_inc(qk_ps, 1)
            for t in range(TB):
                for kb in range(2):
                    k0 = (t // 2) * SEQ + KEY_ROW0[t % 2] * SIDE + kb * KEY_HALF
                    last = pe.matmul(bank(5)[0:KEY_HALF, (2 * t + kb) * CH:(2 * t + kb + 1) * CH],
                                     xt[:, k0:k0 + KEY_HALF], w_v[:], start=True, stop=True)
            last.then_inc(v_ps, 1)

            def scores(h):
                pe.wait_ge(qz_ready[h % 2], h // 2 + 1)
                if h >= 2:
                    pe.wait_ge(masked, TB * (h - 2) + TB)
                for t in range(TB):
                    unit = TB * h + t
                    k0 = (t // 2) * SEQ + KEY_ROW0[t % 2] * SIDE
                    o = 256 * (unit % 2)
                    last = pe.matmul(bank(1 + (unit // 2) % 4)[:, o:o + KEYS], qz[:, h, t * P:(t + 1) * P],
                                     kf[:, k0:k0 + KEYS], start=True, stop=True)
                    if t % 2:
                        last.then_inc(score, 1)

            def probs_turn(h):
                pe.wait_ge(normed, h + 1)
                for g in range(2):
                    if h:
                        pe.wait_ge(pt_sb[g], h)
                    for w in range(2):
                        for kb in range(2):
                            o = (2 * w + kb) * P
                            last = pe.transpose(bank(5 + g)[0:KEY_HALF, o:o + P],
                                                pr[:, (TB * h + 2 * g + w) % 16, kb * KEY_HALF:(kb + 1) * KEY_HALF], ident)
                    last.then_inc(pt_ps, 1)

            def values(h):
                o = 32 * (h % 4)
                for g in range(2):
                    pe.wait_ge(pt_sb[g], h + 1)
                    for w in range(2):
                        t = 2 * g + w
                        for kb in range(2):
                            last = pe.matmul(ps[o:o + 32, 7 * (h // 4), t * P:(t + 1) * P],
                                             vz[:, 2 * t + kb, h], pt[:, 2 * (h % 2) + g, (2 * w + kb) * P:(2 * w + kb + 1) * P],
                                             start=(kb == 0), stop=(kb == 1))
                last.then_inc(pv, 1)

            pe.wait_ge(q_sb, 1)
            pe.wait_ge(k_sb, 1)
            for h in range(AHEAD):
                scores(h)
            pe.wait_ge(v_sb, 1)
            for h in range(HEADS):
                if h + AHEAD < HEADS:
                    scores(h + AHEAD)
                probs_turn(h)
                if h:
                    values(h - 1)
            values(HEADS - 1)
            for a in range(2):
                pe.wait_ge(at_sb[a], 1)
                for t in range(TB):
                    last = pe.matmul(bank(1)[:, t * CH:(t + 1) * CH], at[:, a, t * P:(t + 1) * P], w_pr[:, a],
                                     start=(a == 0 and t == 0), stop=(a == 1 and t == TB - 1), skip_group_check=True)
            last.then_inc(apr_ps, 1)

            experts(1)

            got("w_i1", "w_i2")
            turn(4)
            turned(4)
            pe.matmul(bank(1)[0:INV_HID], w_i1[:], xt[:], start=True, stop=True).then_inc(ih_ps, 1)
            keep_warm(4)
            pe.wait_ge(ih_sb, 1)
            for r in range(5):
                m = P if r < 4 else CH
                pe.matmul(bank(2 + r)[0:m], w_i2[:, r, 0:m], ih, start=True, stop=True).then_inc(wq_ps, 1)
            for r in range(5):
                pe.wait_ge(prod_ready, r + 1)
                m = P if r < 4 else CH
                for t in range(TB):
                    last = pe.matmul(bank(7)[:, t * CH:(t + 1) * CH], prod[0:m, r, t * P:(t + 1) * P], tap_sum[0:m, r],
                                     start=(r == 0 and t == 0), stop=(r == 4 and t == TB - 1), skip_group_check=True)
            last.then_inc(inv_ps, 1)

            experts(2)

            got("w_pt")
            turn(6)
            turned(6)
            for t in range(TB):
                last = pe.matmul(bank(1)[:, t * CH:(t + 1) * CH], xt[:, t * P:(t + 1) * P], w_pt[:], start=True, stop=True)
            last.then_inc(proj_ps, 1)
            experts(3)

        @block.vector
        def _(dve):
            steps = [0]

            def mark(ins):
                steps[0] += 1
                ins.then_inc(dve_step, 1)

            def settle():
                dve.wait_ge(dve_step, steps[0])

            def link(ins):
                mark(ins)
                settle()

            def norm(n):
                src = x[:, n]
                if n == 0:
                    dve.wait_ge(load["x"], 16)
                else:
                    dve.wait_ge(resid, n)
                for t in range(TB):
                    mark(dve.bn_stats(stats[:, t], src[:, t]))
                settle()
                for t in range(TB):
                    mark(dve.bn_aggr(mv[:, t], stats[:, t]))
                settle()
                if n == 1:
                    link(dve.tensor_scalar(ve[:, 0], mv[:, :, 1], EPS[n], None, ALU.add))
                    link(dve.reciprocal(sq[:], ve[:, 0]))
                    link(dve.tensor_tensor(sq[:], sq[:], mv[:, :, 1], ALU.mult))
                    dve.tensor_scalar(ve[:, 1], sq[:], EPS[1], None, ALU.add).then_inc(var_ready, 1)
                else:
                    dve.tensor_scalar(ve[:, 0], mv[:, :, 1], EPS[n], None, ALU.add).then_inc(var_ready, 1)
                dve.wait_ge(rstd_ready, n + 1)
                if n == 1:
                    link(dve.tensor_tensor(rstd[:, 1], rstd[:, 0], rstd[:, 1], ALU.mult))
                for t in range(TB):
                    w = 2 if n in (3, 5, 7) else 1
                    last = dve.tensor_scalar(xn[:, t, 0:w * CH].rearrange("p (w c) -> p w c", c=CH),
                                             src[:, t].unsqueeze(1).to_broadcast([P, w, CH]),
                                             mv[:, t, 0:1], rstd[:, 0, t:t + 1], ALU.subtract, ALU.mult)
                    if n == 1:
                        last = dve.tensor_scalar(xn[:, t, CH:P], src[:, t], mv[:, t, 0:1], rstd[:, 1, t:t + 1],
                                                 ALU.subtract, ALU.mult)
                    last.then_inc(ln_ready, 1)
                m = P if n % 2 else CH
                dve.wait_ge(xt_ps, 2 * n + 2)
                dve.tensor_copy(xt[0:m, SEQ:], turn_bank(n, 1)[0:m, 0:SEQ]).then_inc(xt_sb[1], 1)

            norm(0)
            dve.wait_ge(zeroed, 1)
            dve.wait_ge(xi_ps, 1)
            dve.tensor_copy(xp[:, :, 1:SIDE + 1, 1:SIDE + 1],
                            bank(1).rearrange("p (b h w) -> p b h w", b=2, h=SIDE)).then_inc(xp_ready, 1)
            dve.wait_ge(fdt_ps, 1)
            dve.tensor_copy(w_fdt.rearrange("p k c -> p (k c)"), bank(5)).then_inc(fdt_sb, 1)
            dve.wait_ge(load["cols"], 16)
            dve.wait_ge(load["c32"], 16)
            for a in range(2):
                mark(dve.tensor_scalar(d_mix[:, a], to_scan, col("ds", 2 * a), None, ALU.mult))
            settle()
            for a in range(2):
                last = dve.scalar_tensor_tensor(out=d_mix[:, a], in0=anti_to_scan, scalar=col("ds", 2 * a + 1),
                                                in1=d_mix[:, a], op0=ALU.mult, op1=ALU.add)
            last.then_inc(diag_ready, 1)
            dve.wait_ge(u0_ready, 1)

            dve.tensor_copy(grid(u[:, 2]), columns_first(u[:, 0])).then_inc(u_ready, 1)

            def part(k, r):
                if k >= 2 and r == 0:
                    dve.wait_ge(stacked[k % 2], 16 * PARTS)
                if r == 0:
                    dve.wait_ge(*u_made(k))
                else:
                    dve.wait_ge(rest_ready, 2 * k + 1)
                src = (dd[:, k] if r == 0 else res[:, k % 2, 0]).rearrange("p v l -> p (v l)")
                dve.tensor_tensor(res[:, k % 2, r].rearrange("p v l -> p (v l)"), src, high(src), ALU.subtract)\
                   .then_inc(rest_ready, 1)

            def bounded(k):
                dve.wait_ge(z_ready, k + 1)
                dve.tensor_scalar(zmax[:, k], z_[k], LOG_FROM, None, ALU.max).then_inc(zmax_ready, 1)
                dve.tensor_scalar(zmin[k], z_[k], LOG_FROM, None, ALU.min).then_inc(zmin_ready, 1)
                dve.wait_ge(zmax_ready, k + 1)
                dve.tensor_scalar(z1[k], zmax[:, k], 1.0, -1.0, ALU.add, ALU.add).then_inc(z1_ready, 1)

            def small_log(k):
                if k:
                    dve.wait_ge(square_ready, k)
                    link(dve.scalar_tensor_tensor(out=z_[k], in0=z_[k], scalar=LOG_C0 - LOG_C1 ** 2 / 4, in1=zmin[k],
                                                  op0=ALU.add, op1=ALU.mult))
                    return
                dve.wait_ge(zmin_ready, 1)
                link(dve.scalar_tensor_tensor(out=z_[0], in0=zmin[0], scalar=LOG_C1, in1=zmin[0],
                                              op0=ALU.add, op1=ALU.mult))
                link(dve.scalar_tensor_tensor(out=z_[0], in0=z_[0], scalar=LOG_C0, in1=zmin[0],
                                              op0=ALU.add, op1=ALU.mult))

            def delta(k):
                dve.wait_ge(log1p_ready[k > 0], max(k, 1))
                dve.wait_ge(relu_ready, k + 1)
                dve.wait_ge(log_at_ready, 1)
                link(dve.scalar_tensor_tensor(out=z1[k], in0=z1[k], scalar=log_at[:], in1=dd[:, k, 0],
                                              op0=ALU.subtract, op1=ALU.add))
                dve.scalar_tensor_tensor(out=dd[:, k, 0], in0=z_[k], scalar=LOG_C2, in1=z1[k],
                                         op0=ALU.mult, op1=ALU.add).then_inc(delta_ready, 1)

            bounded(0)
            small_log(0)
            log1p(dve, 0)
            delta(0)
            delta_u(dve, 0)
            part(0, 0)
            part(0, 1)
            for k in range(1, DIRS):
                bounded(k)
            dve.wait_ge(bias_seen, 1)
            dve.tensor_tensor(b1f[:], bank(4)[:, 0:16], colv("b1_0"), ALU.add).then_inc(b1f_ready, 1)

            def times_b(i):
                dve.wait_ge(uspread, i + 1)
                if i % PAIRS_PER_DIR == 0:
                    dve.wait_ge(bc_sb, 2 * (i // PAIRS_PER_DIR) + 1)
                b_all = bc[:, i // PAIRS_PER_DIR, 0].unsqueeze(1).to_broadcast([P, 2, 2 * SEQ])
                if i >= 4:
                    dve.wait_ge(hc_done, i - 3)
                dve.tensor_tensor(states[i % 4], ps[:, 2 + 2 * (i % 2):4 + 2 * (i % 2), :], b_all, ALU.mult).then_inc(mul_done, 1)

            times_b(0)
            for i in range(PAIRS):
                k, ii = divmod(i, PAIRS_PER_DIR)
                if i + 1 < PAIRS:
                    times_b(i + 1)
                dve.wait_ge(mul_done, i + 1)
                dve.wait_ge(exp_done, 2 * i + 2)
                h = states[i % 4].rearrange("p s l -> p (s l)")
                dve.tensor_tensor_scan(h,
                                       da[:, i % 2].rearrange("p s l -> p (s l)"),
                                       h,
                                       0.0, ALU.mult, ALU.add).then_inc(scan_done, 1)
                if k < DIRS - 1:
                    if i == 0:
                        small_log(1)
                        delta(1)
                    if ii == 1:
                        if k == 0:
                            delta_u(dve, 1)
                        part(k + 1, 0)
                    if ii == 2:
                        part(k + 1, 1)
                    if k == 0 and ii in (5, 6):
                        small_log(ii // 2)
                        delta(ii // 2)
            c_all = bc[:, DIRS - 1, 1].unsqueeze(1).to_broadcast([P, 2, 2 * SEQ])
            for i in range(PAIRS - HC_ON_DVE, PAIRS):
                dve.wait_ge(scan_done, i + 1)
                dve.wait_ge(sum_done, (i - HC_SLOTS) // 2 + 1)
                dve.tensor_tensor(hc[:, i % HC_SLOTS], states[i % 4], c_all, ALU.mult).then_inc(hc_last, 1)
            dve.wait_ge(sum_done, PAIRS // 2)
            dve.wait_ge(zs_ready, 1)
            dve.tensor_tensor(gated, bank(6), zs, ALU.mult).then_inc(gated_ready, 1)

            def add(n, src, sem_, count):
                dve.wait_ge(sem_, count)
                dve.tensor_tensor(x[:, n + 1], x[:, n], src.rearrange("p (t c) -> p t c", t=TB), ALU.add)\
                   .then_inc(resid, 1)

            add(0, bank(1)[:, 0:TB * CH], proj_ps, 1)

            def split_input(f):
                dve.wait_ge(xt_sb[0], LN_OF_FFN[f] + 1)
                dve.wait_ge(xt_sb[1], LN_OF_FFN[f] + 1)
                dve.tensor_tensor(x_rest, xt[:], high(xt[:]), ALU.subtract).then_inc(x_rest_ready, 1)
                dve.wait_ge(x_rest_ready, f)
                dve.tensor_tensor(x_last[0:CH], x_rest[0:CH], high(x_rest[0:CH]), ALU.subtract).then_inc(x_last_ready, 1)

            def gate_muls(f, *blocks):
                if f == 3:
                    for j in blocks:
                        gate_mul(j)

            def router(f):
                e_n = E_OF[f]
                n = TB * e_n
                dve.wait_ge(load["rows"], 16)
                dve.wait_ge(logits, f + 1)
                link(dve.tensor_tensor(lg[:, 0:n], bank(7)[:, 0:n], row(f"br_{f}"), ALU.add))
                link(dve.tensor_reduce(m1[:], tiles(lg[:, 0:n]), X_AXIS, ALU.max))
                link(dve.tensor_tensor(tiles(dl[:, 0:n]), tiles(lg[:, 0:n]), spread_last(m1[:], e_n), ALU.subtract))
                link(dve.scalar_tensor_tensor(out=c1[:, 0:n], in0=dl[:, 0:n], scalar=0.0, in1=rank_of[e_n],
                                              op0=ALU.is_ge, op1=ALU.mult))
                link(dve.tensor_reduce(i1[:], tiles(c1[:, 0:n]), X_AXIS, ALU.max))
                gate_muls(f, 0, 1)
                if f == 2:
                    dve.tensor_tensor(tiles(oh16[:]), tiles(c1[:, 0:n]), spread_last(i1[:], e_n), ALU.is_equal)\
                       .then_inc(oh_ready, 1)
                link(dve.tensor_tensor(tiles(oh1[:, 0:n]), tiles(c1[:, 0:n]), spread_last(i1[:], e_n), ALU.is_equal))
                if f == 2:
                    dve.sem_inc(gap, 1)
                    dve.wait_ge(gap_act, 3)
                    link(dve.tensor_reduce(m2[:], tiles(ex[:, 0:n]), X_AXIS, ALU.add))
                    link(dve.reciprocal(i2[:], m2[:]))
                    dve.wait_ge(count_ps, 1)
                    link(dve.scalar_tensor_tensor(out=c2[:, 0:n], in0=bank(0)[:, 0:n], scalar=float(CAPACITY), in1=oh1[:, 0:n],
                                                  op0=ALU.is_le, op1=ALU.mult))
                    link(dve.tensor_tensor(tiles(ww[:, 0:n]), tiles(c2[:, 0:n]), spread_last(i2[:], e_n), ALU.mult))
                else:
                    link(dve.scalar_tensor_tensor(out=d2[:, 0:n], in0=oh1[:, 0:n], scalar=-BIG, in1=dl[:, 0:n],
                                                  op0=ALU.mult, op1=ALU.add))
                    dve.tensor_reduce(m2[:], tiles(d2[:, 0:n]), X_AXIS, ALU.max).then_inc(gap, 1)
                    dve.wait_ge(gap, f + 1)
                    link(dve.tensor_tensor(tiles(g2[:, 0:n]), tiles(d2[:, 0:n]), spread_last(m2[:], e_n), ALU.is_ge))
                    link(dve.tensor_tensor(c2[:, 0:n], g2[:, 0:n], rank_of[e_n], ALU.mult))
                    link(dve.tensor_reduce(i2[:], tiles(c2[:, 0:n]), X_AXIS, ALU.max))
                    link(dve.tensor_tensor(tiles(oh2[:, 0:n]), tiles(c2[:, 0:n]), spread_last(i2[:], e_n), ALU.is_equal))
                    gate_muls(f, 2, 3)
                    dve.wait_ge(gap_act, f + 1)
                    mark(dve.tensor_scalar(wa[:], th[:], 0.5, 0.5, ALU.mult, ALU.add))
                    link(dve.tensor_scalar(wc[:], th[:], -0.5, 0.5, ALU.mult, ALU.add))
                    mark(dve.tensor_tensor(tiles(wr1[:, 0:n]), tiles(oh1[:, 0:n]), spread_last(wa[:], e_n), ALU.mult))
                    link(dve.tensor_tensor(tiles(wr2[:, 0:n]), tiles(oh2[:, 0:n]), spread_last(wc[:], e_n), ALU.mult))
                    link(dve.tensor_tensor(ww[:, 0:n], wr1[:, 0:n], wr2[:, 0:n], ALU.add))
                w3 = tiles(ww[:, 0:n])
                r3 = tiles(wr1[:, 0:n])
                link(dve.tensor_copy(wp[:, :, 0:e_n], w3))
                link(dve.tensor_tensor(r3, w3, wp[:, :, 0:e_n], ALU.subtract))
                link(dve.tensor_copy(wp[:, :, e_n:2 * e_n], r3))
                dve.tensor_tensor(wp[:, :, 2 * e_n:3 * e_n], r3, wp[:, :, e_n:2 * e_n], ALU.subtract).then_inc(w_ready, 1)
                dve.wait_ge(wt_ps, f + 1)
                dve.tensor_copy(wt[0:PARTS * e_n, :], bank(7).bitcast(BF16)[0:PARTS * e_n, 0:TOKENS]).then_inc(wt_sb, 1)

            def combine(f, p):
                base_w, pairs = 4 * f, E_OF[f] // 2
                dve.wait_ge(wb_sb, base_w + p + 1)
                dve.wait_ge(y_ready, base_w + p + 1)
                o = acc if p == 0 else tmp[:, p % 2]
                b2 = col(f"b2_{f}", p) if f < 3 else 0.0
                dve.scalar_tensor_tensor(out=o, in0=bank(5 + p % 2), scalar=b2, in1=wb[:, p],
                                         op0=ALU.add, op1=ALU.mult).then_inc(comb, 1)
                if 0 < p < pairs - 1:
                    dve.wait_ge(comb, base_w + p + 1)
                    last = dve.tensor_tensor(acc, acc, tmp[:, p % 2], ALU.add)
                    if p == pairs - 2:
                        last.then_inc(acc_ready, 1)
                    else:
                        link(last)

            def finish(f):
                n = LN_OF_FFN[f]
                if f < 2 or f == 3:
                    add(n, bank(0)[:, 0:TB * CH], out_ps, f + 1)
                    return
                dve.wait_ge(out_ps, f + 1)
                y = bank(0)[:, 0:TB * CH]
                mark(dve.tensor_scalar(nan_a, y, FLT_MAX, 1.0e4, ALU.is_gt, ALU.mult))
                mark(dve.tensor_scalar(nan_b, y, -FLT_MAX, -1.0e4, ALU.is_lt, ALU.mult))
                link(dve.tensor_scalar(finite, y, 0.0, 0.0, ALU.mult, ALU.is_equal))
                link(dve.tensor_tensor(nan_a, nan_a, nan_b, ALU.add))
                link(dve.copy_predicated(nan_a, finite, y))
                dve.tensor_tensor(x[:, n + 1], x[:, n], nan_a.rearrange("p (t c) -> p t c", t=TB), ALU.add).then_inc(resid, 1)

            norm(1)
            router(0)
            for p in range(4):
                combine(0, p)
            finish(0)

            norm(2)
            dve.wait_ge(qk_ps, 2)
            dve.tensor_scalar(kf, bank(2), col("k_b"), None, ALU.add).then_inc(k_sb, 1)
            dve.wait_ge(q_sb, 1)
            for h in range(0, HEADS, 2):
                dve.tensor_scalar(qz[:, h], qf, head_mask[:, h:h + 1], None, ALU.mult).then_inc(qz_ready[0], 1)
            dve.wait_ge(v_ps, 1)
            v_b = row("v_b")[0:KEY_HALF].unsqueeze(1).to_broadcast([KEY_HALF, 8, CH])
            dve.wait_ge(zeroed, 7)
            dve.tensor_tensor(vz[:, :, :, 0:HEAD_CH], bank(5)[0:KEY_HALF].rearrange("p (u h c) -> p u h c", u=8, h=HEADS),
                              v_b.rearrange("p u (h c) -> p u h c", h=HEADS), ALU.add).then_inc(v_sb, 1)
            pr_b = row("pr_b").unsqueeze(1).to_broadcast([P, TB, CH])
            xb = nan_a.rearrange("p (t c) -> p t c", t=TB)
            mark(dve.tensor_tensor(xb, x[:, 2], pr_b, ALU.add))
            dve.wait_ge(bias_ready, 2)

            def inverse_sums(h):
                dve.wait_ge(prob, TB * h + TB)
                dve.reciprocal(rrec[:, TB * h:TB * h + TB], rsum[:, TB * h:TB * h + TB]).then_inc(inverse, 1)

            for h in range(HEADS):
                for t in range(TB):
                    unit = TB * h + t
                    dve.wait_ge(score, unit // 2 + 1)
                    if unit >= 16:
                        dve.wait_ge(prob, unit - 15)
                    o = 256 * (unit % 2)
                    dve.tensor_tensor_reduce(sm[:, unit % 16], bank(1 + (unit // 2) % 4)[:, o:o + KEYS], bias[:, t % 2, h],
                                             1.0, -3.0e38, ALU.add, ALU.max, mx[:, unit:unit + 1]).then_inc(masked, 1)
                dve.wait_ge(masked, TB * h + TB)
                dve.tensor_scalar(nmx[:, TB * h:TB * h + TB], mx[:, TB * h:TB * h + TB], -1.0, None, ALU.mult)\
                   .then_inc(negmax, 1)
                if h >= 1:
                    inverse_sums(h - 1)
                if h >= 2:
                    probs_copy(dve, h - 2, 1)
            inverse_sums(HEADS - 1)
            dve.wait_ge(pv, 4)
            dve.tensor_copy(at[:, 0], bank(0)).then_inc(at_sb[0], 1)
            probs_copy(dve, HEADS - 2, 1)
            probs_copy(dve, HEADS - 1, 1)
            dve.wait_ge(apr_ps, 1)
            settle()
            dve.tensor_tensor(x[:, 3], xb, bank(1)[:, 0:256].rearrange("p (t c) -> p t c", t=TB), ALU.add).then_inc(resid, 1)

            norm(3)
            split_input(1)
            router(1)
            for p in range(4):
                combine(1, p)
            finish(1)

            norm(4)
            dve.wait_ge(xt_sb[0], 5)
            dve.wait_ge(xt_sb[1], 5)
            dve.wait_ge(zeroed, 6)
            dve.tensor_copy(xpp[CH:P, :, 1:SIDE + 1, 0:SIDE],
                            xt[0:CH].rearrange("p (b h w) -> p b h w", b=2, h=SIDE)).then_inc(pad_ready, 1)
            dve.wait_ge(pad_ready, 2)
            for r, taps in enumerate(TAP_BLOCKS):
                dve.wait_ge(wq_ps, r + 1)
                whole = len(taps) == 2 and taps[1] == taps[0] + 1
                for half, tap in enumerate(taps[:1] if whole else taps):
                    dy, dx = divmod(tap, 3)
                    rows_ = slice(0, P) if whole else slice(CH * half, CH * half + CH)
                    dx -= half
                    last = dve.tensor_tensor(grid(prod[rows_, r]), grid(bank(2 + r)[rows_]),
                                             xpp[rows_, :, dy:dy + SIDE, dx:dx + SIDE], ALU.mult)
                last.then_inc(prod_ready, 1)
            add(4, bank(7)[:, 0:256], inv_ps, 1)

            norm(5)
            split_input(2)
            router(2)
            for p in range(4):
                combine(2, p)
            finish(2)

            norm(6)
            add(6, bank(1)[:, 0:256], proj_ps, 2)
            norm(7)
            split_input(3)

            def gate_mul(j):
                dve.wait_ge(gate_ready, j + 1)
                if j >= RING:
                    dve.wait_ge(y_ready, 12 + (j - RING) // 2 + 1)
                dve.tensor_tensor(hid[:, j % RING], gate[:, j % 2], bank(gate_bank(j) + 1), ALU.mult).then_inc(hid_ready, 1)

            router(3)
            for p in range(8):
                if p < 6:
                    gate_mul(2 * p + 4)
                    gate_mul(2 * p + 5)
                combine(3, p)
            finish(3)


def _places(sizes):
    at, o = {}, 0
    for n, s in sizes:
        at[n] = (o, s)
        o += s
    return at, o


C32_AT, C32_COLS = _places([("ident", P), ("anti", P), ("to_scan", P), ("anti_to_scan", P), ("stack_i", CH), ("state_sum", PER_GROUP * 32),
                            ("tap_sum", 5 * CH), ("window", 2 * KEYS), ("head_mask", HEADS), ("rank8", TB * 8), ("rank16", TB * 16)])
C16_AT, C16_COLS = _places([("ident", P), ("tri", P), ("ones", P), ("spread", PER_GROUP * P),
                            ("spread_w8", 4 * P), ("spread_w16", 8 * P)])
COLS_AT, COLS_N = _places([("conv_b", 1), ("dt_b", 4), ("ds", 4), ("b1_0", 16), ("b1_1", 16), ("b1_2", 16),
                           ("b2_0", 4), ("b2_1", 4), ("b2_2", 4), ("q_b", 1), ("k_b", 1), ("b_i1", 1),
                           ("ln_g", 8), ("ln_b", 8)])
ROWS_AT, ROWS_N = _places([("br_0", 32), ("br_1", 32), ("br_2", 32), ("br_3", 64), ("v_b", CH), ("pr_b", CH)])
LOADS = ["x", "c32", "c16", "cols", "rows", "w_in", "alog", "w_xdt", "w_dt", "w_conv", "w_bc", "w_out", "rpb",
         "w_qk", "w_v", "w_pr", "w_i1", "w_i2", "w_pt"] + [f"{a}_{f}" for a in ("w1", "w2", "wr") for f in range(4)]
ARENA = 27136 + (HC_SLOTS + 2) * 1024


def scan_order():
    i = np.arange(INNER)
    return GROUPS * (i % 32) + i // 32


def tap_rows():
    rows = np.full((5, P), -1)
    for r, taps in enumerate(TAP_BLOCKS):
        for half, tap in enumerate(taps):
            rows[r, CH * half:CH * half + CH] = tap * CH + np.arange(CH)
    return rows


def constants():
    c = {n: np.zeros((P, s), np.float32) for n, (_, s) in C32_AT.items()}
    i = np.arange(P)
    c["ident"][:] = np.eye(P)
    c["anti"][:] = np.eye(P)[::-1]
    c["to_scan"][scan_order(), i] = 1
    c["anti_to_scan"][P - 1 - scan_order(), i] = 1
    c["stack_i"][:] = np.tile(np.eye(CH), (2, 1))
    for m in range(PER_GROUP):
        c["state_sum"][i, m * 32 + m * TILE_CH + i // STATE] = 1
    rows = tap_rows()
    for r in range(5):
        ok = rows[r] >= 0
        c["tap_sum"][i[ok], r * CH + rows[r][ok] // TAPS] = 1
    start = np.clip(np.arange(SIDE) - WIN // 2, 0, SIDE - WIN)
    for q in range(2):
        qi, qj = 8 * q + i // SIDE, i % SIDE
        key = np.arange(KEYS)
        ki, kj = KEY_ROW0[q] + key // SIDE, key % SIDE
        inside = ((ki[None] >= start[qi][:, None]) & (ki[None] < start[qi][:, None] + WIN)
                  & (kj[None] >= start[qj][:, None]) & (kj[None] < start[qj][:, None] + WIN))
        c["window"][:, q * KEYS:(q + 1) * KEYS] = np.where(inside, 0.0, -BIG)
    for h in range(HEADS):
        c["head_mask"][HEAD_CH * h:HEAD_CH * (h + 1), h] = float(HEAD_CH) ** -0.5
    c["rank8"][:] = np.tile(8 - np.arange(8), TB)
    c["rank16"][:] = np.tile(16 - np.arange(16), TB)
    h = {n: np.zeros((P, s), np.float32) for n, (_, s) in C16_AT.items()}
    h["ident"][:] = np.eye(P)
    h["tri"][:] = np.triu(np.ones((P, P)))
    h["ones"][:] = 1
    for m in range(PER_GROUP):
        for part in range(PARTS):
            for ch in range(TILE_CH):
                o = m * P + ch * STATE
                h["spread"][32 * part + TILE_CH * m + ch, o:o + STATE] = 1
    for e_n in (8, 16):
        for p in range(e_n // 2):
            for part in range(PARTS):
                for half in range(2):
                    o = p * P + CH * half
                    h[f"spread_w{e_n}"][part * e_n + 2 * p + half, o:o + CH] = 1
    return np.concatenate(list(c.values()), 1), np.concatenate(list(h.values()), 1).astype(mybir.dt.np(BF16))


def lay_out(a):
    def rows_to(w, n=P):
        return np.concatenate([w, np.zeros((n - w.shape[0], *w.shape[1:]), w.dtype)], 0)

    o = {}
    o["c32"], o["c16"] = constants()
    o["x"] = a["x"].reshape(TOKENS, CH)
    w_in = a["L0_conv_in_proj_w"]
    o["w_in"] = rows_to(np.concatenate([w_in[:, :INNER], w_in[:, INNER:][:, scan_order()]], 1))
    o["w_conv"] = a["L0_conv_conv_w"].transpose(1, 2, 3, 0).reshape(INNER, TAPS, INNER)
    xproj = a["L0_conv_xproj_w"]
    half = xproj.shape[0] // 2
    o["w_xdt"] = np.stack([xproj[half * (k // 2) + RANK * (k % 2):][:RANK] for k in range(DIRS)], 1)
    o["w_dt"] = a["L0_conv_dt_w"].transpose(2, 0, 1)
    o["w_bc"] = np.stack([np.stack([np.tile(xproj[half * (k // 2) + 2 * RANK + 2 * STATE * v + STATE * (k % 2):][:STATE].T, (1, TILE_CH))
                                    for v in range(2)], 1) for k in range(DIRS)], 1)
    o["alog"] = a["L0_conv_A_logs"][:, scan_order()].reshape(64, P)
    o["w_out"] = a["L0_conv_out_proj_w"][scan_order()]
    for f, n in enumerate(("L0_ffn_W1", "L1_ffn_W1", "L2_ffn_w1")):
        o[f"w1_{f}"] = a[n].transpose(1, 0, 2).reshape(CH, -1)
        w = a[n[:-2] + ("W2" if f < 2 else "w2")]
        o[f"w2_{f}"] = w.reshape(16, P, CH).transpose(1, 0, 2)
    o["w1_3"] = np.concatenate([a["L3_ffn_" + n].transpose(1, 0, 2).reshape(CH, -1) for n in ("w1", "w2")], 1)
    o["w2_3"] = a["L3_ffn_w3"].transpose(1, 0, 2)
    for f, n in enumerate(("L0_ffn_Wr", "L1_ffn_Wg", "L2_ffn_gate_w", "L3_ffn_gate_w")):
        o[f"wr_{f}"] = rows_to(a[n])
    i, key = np.arange(P)[:, None], np.arange(KEYS)
    o["rpb"] = np.zeros((P, 2, HEADS, KEYS), np.float32)
    for q in range(2):
        di = KEY_ROW0[q] + key // SIDE - (8 * q + i // SIDE) + WIN - 1
        dj = key % SIDE - i % SIDE + WIN - 1
        di, dj = np.broadcast_arrays(di, dj)
        near = (di >= 0) & (di < 2 * WIN - 1) & (dj >= 0) & (dj < 2 * WIN - 1)
        token, at = np.nonzero(near)
        o["rpb"][token, q, :, at] = a["L1_conv_rpb"][:, di[near], dj[near]].T
    qkv, qkv_b = a["L1_conv_qkv_w"], a["L1_conv_qkv_b"]
    o["w_qk"] = rows_to(np.stack([np.tile(qkv[CH * w:CH * (w + 1)].T, (1, 2)) for w in range(2)], 1))
    o["w_v"] = rows_to(qkv[2 * CH:].T)
    o["w_pr"] = np.zeros((P, 2, CH), np.float32)
    for h in range(HEADS):
        o["w_pr"][32 * (h % 4):32 * (h % 4) + HEAD_CH, h // 4] = a["L1_conv_proj_w"].T[HEAD_CH * h:HEAD_CH * (h + 1)]
    o["w_i1"] = rows_to(a["L2_conv_W1"])
    w_i2 = np.concatenate([a["L2_conv_W2"], a["L2_conv_b2"][None]], 0)
    rows = tap_rows()
    of = np.where(rows < 0, 0, rows // (TAPS * CH // INV_GROUPS) * TAPS + rows % TAPS)
    o["w_i2"] = w_i2[:, of]
    o["w_pt"] = rows_to(a["L3_conv_W"])
    c = {n: np.zeros((P, s), np.float32) for n, (_, s) in COLS_AT.items()}
    c["conv_b"][:, 0] = a["L0_conv_conv_b"]
    c["dt_b"][:] = a["L0_conv_dt_b"].T
    c["ds"][:] = a["L0_conv_Ds"].T
    c["ds"][:, 1::2] = c["ds"][::-1, 1::2]
    for f, n in enumerate(("L0_ffn_b1", "L1_ffn_b1", "L2_ffn_b1")):
        c[f"b1_{f}"][:] = a[n].reshape(16, P).T
        c[f"b2_{f}"][:] = a[n[:-1] + "2"].reshape(4, P).T
    c["q_b"][:, 0], c["k_b"][:, 0] = np.tile(qkv_b[0:CH], 2), np.tile(qkv_b[CH:2 * CH], 2)
    c["b_i1"][:INV_HID, 0] = a["L2_conv_b1"]
    c["ln_g"][CH:] = a["L0_ffn_ln_g"].T
    c["ln_b"][CH:] = a["L0_ffn_ln_b"].T
    o["cols"] = np.concatenate(list(c.values()), 1)
    r = [np.tile(a[n], TB) for n in ("L0_ffn_br", "L1_ffn_bg", "L2_ffn_gate_b", "L3_ffn_gate_b")]
    o["rows"] = np.concatenate([*r, qkv_b[2 * CH:], a["L1_conv_proj_b"]])
    return {n: np.ascontiguousarray(v) for n, v in o.items()}


def kernel(**inputs):
    import concourse.bacc as bacc
    from concourse.bass_utils import run_bass_kernel_spmd

    arrays = lay_out({n: np.asarray(v) for n, v in inputs.items()})
    nc = bacc.Bacc("TRN2", target_bir_lowering=False, num_devices=1)
    d = {n: nc.dram_tensor("in_" + n, v.shape, mybir.dt.from_np(v.dtype), kind="ExternalInput").ap()
         for n, v in arrays.items()}
    out = nc.dram_tensor("out", (TOKENS, CH), F32, kind="ExternalOutput").ap()
    build(nc, d, out)
    r = run_bass_kernel_spmd(nc, [{"in_" + n: v for n, v in arrays.items()}], core_ids=[0])
    return r.results[0]["out"].reshape(BATCH, SIDE, SIDE, CH)
```
